# Optimizing a Trainium2 kernel written in Bass

```python
import numpy as np
import jax
import jax.numpy as jnp

def _softmax(x, axis=-1):
    return jax.nn.softmax(x, axis=axis)

def _gelu(x):
    return jax.nn.gelu(x, approximate=True)

def _silu(x):
    return jax.nn.silu(x)

def _sigmoid(x):
    return jax.nn.sigmoid(x)

def _layernorm(x, axis=-1, eps=1e-05):
    m = jnp.mean(x, axis=axis, keepdims=True)
    v = jnp.var(x, axis=axis, keepdims=True)
    return (x - m) / jnp.sqrt(v + eps)

def _scatter_add(tgt, idx, src, axis=0):
    return tgt.at[idx].add(src)

def _segment_sum(src, seg, n):
    return jax.ops.segment_sum(src, seg, n)
kernel_name = 'mk_xattn_ffn_d2_seqx_r4_5739fa'

def setup_inputs(seed: int=0):
    np.random.seed(seed)
    _w = jnp.asarray

    def _rec_inputs():
        import jax
        import jax.numpy as jnp
        _rk = jax.random.key(seed)
        x = -0.0002928 + 1 * jax.random.normal(jax.random.fold_in(_rk, 1), (32, 128, 256), jnp.float32)
        _lenS = 128 - jax.random.randint(jax.random.fold_in(_rk, 7), (32,), 0, max(1, 128 // 4) + 1, jnp.int32)
        _lenS2 = 128 - jax.random.randint(jax.random.fold_in(_rk, 8), (32,), 0, max(1, 128 // 4) + 1, jnp.int32)
        _ctx_1024P = jax.random.normal(jax.random.fold_in(_rk, 11), (32, 16, 256), jnp.float32)
        _ctx_1024c = jax.random.dirichlet(jax.random.fold_in(_rk, 511), 0.3 * jnp.ones((16,), jnp.float32), (32, 128))
        _ctx_1024t = jnp.einsum('bsk,bkd->bsd', _ctx_1024c, _ctx_1024P)
        _ctx_1024t = _ctx_1024t * jax.lax.rsqrt(jnp.mean(jnp.square(_ctx_1024t)) + 1e-12) * 0.953939
        ctx_1024 = -1.39393e-06 + 0.999914 * (_ctx_1024t + 0.3 * jax.random.normal(jax.random.fold_in(_rk, 611), (32, 128, 256), jnp.float32))
        _validS = jnp.arange(128)[None, :] < _lenS[:, None]
        _validS2 = jnp.arange(128)[None, :] < _lenS2[:, None]
        _causal = jnp.tril(jnp.ones((128, 128), dtype=bool))
        mask_BxSxS2_ff1 = jnp.where(jnp.ones((32, 128, 128), dtype=bool), 1.0, 0.0).astype(jnp.float32)
        return (x, ctx_1024, mask_BxSxS2_ff1)
    x, ctx_1024, mask_BxSxS2_ff1 = _rec_inputs()

    def _L0_xattn_setup():
        import jax, jax.numpy as jnp
        import numpy as np
        HIDDEN = 256
        NUM_HEADS = 16
        HEAD_DIM = HIDDEN // NUM_HEADS
        B, LQ, LK = (2, 512, 512)

        def _split_heads(x):
            b, l, _ = x.shape
            return x.reshape(b, l, NUM_HEADS, HEAD_DIM).transpose(0, 2, 1, 3)
        key = jax.random.key(seed)
        ks = jax.random.split(key, 9)
        s = 1.0 / np.sqrt(HIDDEN)
        return {'hidden_states_query': jax.random.normal(ks[0], (B, LQ, HIDDEN), jnp.float32), 'hidden_states_key': jax.random.normal(ks[1], (B, LK, HIDDEN), jnp.float32), 'attention_mask': jnp.ones((B, LQ, LK), jnp.float32), 'Wq': jax.random.normal(ks[2], (HIDDEN, HIDDEN), jnp.float32) * s, 'bq': jax.random.normal(ks[3], (HIDDEN,), jnp.float32) * s, 'Wk': jax.random.normal(ks[4], (HIDDEN, HIDDEN), jnp.float32) * s, 'bk': jax.random.normal(ks[5], (HIDDEN,), jnp.float32) * s, 'Wv': jax.random.normal(ks[6], (HIDDEN, HIDDEN), jnp.float32) * s, 'bv': jax.random.normal(ks[7], (HIDDEN,), jnp.float32) * s}
    _L0_xattn_all = _L0_xattn_setup()
    _L0_xattn_in = {k: v for k, v in _L0_xattn_all.items() if k in ('Wq', 'bq', 'Wk', 'bk', 'Wv', 'bv')}
    del _L0_xattn_all

    def _L0_ffn_setup():
        import jax, jax.numpy as jnp
        import numpy as np

        def _binarize(w):
            alpha = jax.lax.stop_gradient(jnp.mean(jnp.abs(w), axis=1, keepdims=True))
            bw = alpha * jnp.sign(w)
            return w + jax.lax.stop_gradient(bw - w)
        key = jax.random.key(seed)
        k1, k2, k3, k4, k5 = jax.random.split(key, 5)
        D, H = (256, 1024)
        x = jax.random.normal(k1, (64, 196, D), dtype=jnp.float32)
        w1 = jax.random.normal(k2, (H, D), dtype=jnp.float32) * 0.02
        b1 = jax.random.normal(k3, (H,), dtype=jnp.float32) * 0.02
        w2 = jax.random.normal(k4, (D, H), dtype=jnp.float32) * 0.02
        b2 = jax.random.normal(k5, (D,), dtype=jnp.float32) * 0.02
        return {'x': x, 'w1': w1, 'b1': b1, 'w2': w2, 'b2': b2}
    _L0_ffn_all = _L0_ffn_setup()
    _L0_ffn_in = {k: v for k, v in _L0_ffn_all.items() if k in ('w1', 'b1', 'w2', 'b2')}
    del _L0_ffn_all

    def _L1_xattn_setup():
        import jax, jax.numpy as jnp
        import numpy as np
        D_MODEL = 256
        H = 16
        D_K = D_MODEL // H
        key = jax.random.key(seed)
        ks = jax.random.split(key, 11)
        B, S = (4, 512)
        scale = 1.0 / np.sqrt(D_MODEL)
        inp = {'q': jax.random.normal(ks[0], (B, S, D_MODEL), dtype=jnp.float32), 'k': jax.random.normal(ks[1], (B, S, D_MODEL), dtype=jnp.float32), 'v': jax.random.normal(ks[2], (B, S, D_MODEL), dtype=jnp.float32), 'Wq': jax.random.normal(ks[3], (D_MODEL, D_MODEL), dtype=jnp.float32) * scale, 'bq': jnp.zeros((D_MODEL,), dtype=jnp.float32), 'Wk': jax.random.normal(ks[4], (D_MODEL, D_MODEL), dtype=jnp.float32) * scale, 'bk': jnp.zeros((D_MODEL,), dtype=jnp.float32), 'Wv': jax.random.normal(ks[5], (D_MODEL, D_MODEL), dtype=jnp.float32) * scale, 'bv': jnp.zeros((D_MODEL,), dtype=jnp.float32), 'Wo': jax.random.normal(ks[6], (D_MODEL, D_MODEL), dtype=jnp.float32) * scale, 'bo': jnp.zeros((D_MODEL,), dtype=jnp.float32)}
        return inp
    _L1_xattn_all = _L1_xattn_setup()
    _L1_xattn_in = {k: v for k, v in _L1_xattn_all.items() if k in ('Wq', 'bq', 'Wk', 'bk', 'Wv', 'bv', 'Wo', 'bo')}
    del _L1_xattn_all

    def _L1_ffn_setup():
        import math
        import jax, jax.numpy as jnp
        import numpy as np
        B, S, H, I, E = (4, 512, 256, 1024, 8)
        CAPACITY_FACTOR = 1.0
        key = jax.random.key(seed)
        k1, k2, k3, k4, k5 = jax.random.split(key, 5)
        x = jax.random.normal(k1, (B, S, H), dtype=jnp.float32)
        limit = math.sqrt(6.0 / (H + E))
        router_w = jax.random.uniform(k2, (E, H), dtype=jnp.float32, minval=-limit, maxval=limit)
        router_b = jnp.zeros((E,), dtype=jnp.float32)
        experts_inter = jax.random.normal(k3, (E, H, I), dtype=jnp.float32) * 0.02
        experts_out = jax.random.normal(k4, (E, I, H), dtype=jnp.float32) * 0.02
        return {'x': x, 'router_w': router_w, 'router_b': router_b, 'experts_inter': experts_inter, 'experts_out': experts_out}
    _L1_ffn_all = _L1_ffn_setup()
    _L1_ffn_in = {k: v for k, v in _L1_ffn_all.items() if k in ('router_w', 'router_b', 'experts_inter', 'experts_out')}
    del _L1_ffn_all
    return {'x': x, 'ctx_1024': ctx_1024, 'mask_BxSxS2_ff1': mask_BxSxS2_ff1, 'L0_xattn_Wq': _L0_xattn_in['Wq'], 'L0_xattn_bq': _L0_xattn_in['bq'], 'L0_xattn_Wk': _L0_xattn_in['Wk'], 'L0_xattn_bk': _L0_xattn_in['bk'], 'L0_xattn_Wv': _L0_xattn_in['Wv'], 'L0_xattn_bv': _L0_xattn_in['bv'], 'L0_ffn_w1': _L0_ffn_in['w1'], 'L0_ffn_b1': _L0_ffn_in['b1'], 'L0_ffn_w2': _L0_ffn_in['w2'], 'L0_ffn_b2': _L0_ffn_in['b2'], 'L1_xattn_Wq': _L1_xattn_in['Wq'], 'L1_xattn_bq': _L1_xattn_in['bq'], 'L1_xattn_Wk': _L1_xattn_in['Wk'], 'L1_xattn_bk': _L1_xattn_in['bk'], 'L1_xattn_Wv': _L1_xattn_in['Wv'], 'L1_xattn_bv': _L1_xattn_in['bv'], 'L1_xattn_Wo': _L1_xattn_in['Wo'], 'L1_xattn_bo': _L1_xattn_in['bo'], 'L1_ffn_router_w': _L1_ffn_in['router_w'], 'L1_ffn_router_b': _L1_ffn_in['router_b'], 'L1_ffn_experts_inter': _L1_ffn_in['experts_inter'], 'L1_ffn_experts_out': _L1_ffn_in['experts_out']}

def reference(x, ctx_1024, mask_BxSxS2_ff1, L0_xattn_Wq, L0_xattn_bq, L0_xattn_Wk, L0_xattn_bk, L0_xattn_Wv, L0_xattn_bv, L0_ffn_w1, L0_ffn_b1, L0_ffn_w2, L0_ffn_b2, L1_xattn_Wq, L1_xattn_bq, L1_xattn_Wk, L1_xattn_bk, L1_xattn_Wv, L1_xattn_bv, L1_xattn_Wo, L1_xattn_bo, L1_ffn_router_w, L1_ffn_router_b, L1_ffn_experts_inter, L1_ffn_experts_out):
    import jax
    import jax.numpy as jnp

    def _L0_xattn_ref(hidden_states_query, hidden_states_key, attention_mask, Wq, bq, Wk, bk, Wv, bv):
        import jax, jax.numpy as jnp
        import numpy as np
        HIDDEN = 256
        NUM_HEADS = 16
        HEAD_DIM = HIDDEN // NUM_HEADS
        B, LQ, LK = (2, 512, 512)

        def _split_heads(x):
            b, l, _ = x.shape
            return x.reshape(b, l, NUM_HEADS, HEAD_DIM).transpose(0, 2, 1, 3)
        q = _split_heads(hidden_states_query @ Wq.T + bq)
        k = _split_heads(hidden_states_key @ Wk.T + bk)
        v = _split_heads(hidden_states_key @ Wv.T + bv)
        scale = 1.0 / np.sqrt(HEAD_DIM)
        scores = jnp.einsum('bhqd,bhkd->bhqk', q * scale, k)
        scores = scores + ((1.0 - attention_mask) * -10000.0)[:, None, :, :]
        probs = jax.nn.softmax(scores, axis=-1)
        ctx = jnp.einsum('bhqk,bhkd->bhqd', probs, v)
        b, h, lq, d = ctx.shape
        return ctx.transpose(0, 2, 1, 3).reshape(b, lq, h * d)

    def _L0_ffn_ref(x, w1, b1, w2, b2):
        import jax, jax.numpy as jnp
        import numpy as np

        def _binarize(w):
            alpha = jax.lax.stop_gradient(jnp.mean(jnp.abs(w), axis=1, keepdims=True))
            bw = alpha * jnp.sign(w)
            return w + jax.lax.stop_gradient(bw - w)
        bw1 = _binarize(w1)
        h = jnp.einsum('bsd,hd->bsh', x, bw1) + b1
        h = jax.nn.gelu(h, approximate=False)
        bw2 = _binarize(w2)
        out = jnp.einsum('bsh,dh->bsd', h, bw2) + b2
        return out

    def _L1_xattn_ref(q, k, v, Wq, bq, Wk, bk, Wv, bv, Wo, bo):
        import jax, jax.numpy as jnp
        import numpy as np
        D_MODEL = 256
        H = 16
        D_K = D_MODEL // H
        B, S, _ = q.shape
        query = q @ Wq.T + bq
        key_p = k @ Wk.T + bk
        value = v @ Wv.T + bv
        query = query.reshape(B, S, H, D_K).transpose(0, 2, 1, 3)
        key_p = key_p.reshape(B, S, H, D_K).transpose(0, 2, 1, 3)
        value = value.reshape(B, S, H, D_K).transpose(0, 2, 1, 3)
        scores = jnp.einsum('bhqd,bhkd->bhqk', query, key_p) / jnp.sqrt(jnp.asarray(D_K, dtype=query.dtype))
        attn = jax.nn.softmax(scores, axis=-1)
        x = jnp.einsum('bhqk,bhkd->bhqd', attn, value)
        x = x.transpose(0, 2, 1, 3).reshape(B, S, D_MODEL)
        return x @ Wo.T + bo

    def _L1_ffn_ref(x, router_w, router_b, experts_inter, experts_out):
        import math
        import jax, jax.numpy as jnp
        import numpy as np
        B, S, H, I, E = (4, 512, 256, 1024, 8)
        CAPACITY_FACTOR = 1.0
        b, s, h = x.shape
        e = experts_inter.shape[0]
        capacity = math.ceil(b * s / e * CAPACITY_FACTOR)
        routing_weights = jax.nn.softmax(x @ router_w.T + router_b, axis=-1)
        x_flat = x.reshape(-1, h)
        w_flat = routing_weights.reshape(-1, e)
        routing_mask = (w_flat > 0).astype(jnp.int32)
        sorted_indices = jnp.argsort(-routing_mask, axis=0, stable=True)
        sorted_mask = jnp.take_along_axis(routing_mask, sorted_indices, axis=0)[:capacity]
        sorted_indices = sorted_indices[:capacity]
        used_tokens_indices = (sorted_indices * sorted_mask).reshape(-1)
        mask_f = sorted_mask.reshape(-1).astype(x.dtype)[:, None]
        inputs_tokens = x_flat[used_tokens_indices] * mask_f
        inputs_tokens = inputs_tokens.reshape(capacity, e, h)
        inputs_weights = jnp.take_along_axis(w_flat, sorted_indices, axis=0)
        inter = jnp.einsum('ceh,ehi->cei', inputs_tokens, experts_inter)
        inter = jax.nn.relu(inter)
        out = jnp.einsum('cei,eih->ceh', inter, experts_out)
        out = out * inputs_weights[..., None]
        out = out.reshape(-1, h)
        combined = jnp.zeros_like(x_flat).at[used_tokens_indices].add(out)
        return combined.reshape(b, s, h)
    x = x + _L0_xattn_ref(_layernorm(x, axis=-1), ctx_1024, mask_BxSxS2_ff1, L0_xattn_Wq, L0_xattn_bq, L0_xattn_Wk, L0_xattn_bk, L0_xattn_Wv, L0_xattn_bv)
    x = x + _L0_ffn_ref(_layernorm(x, axis=-1), L0_ffn_w1, L0_ffn_b1, L0_ffn_w2, L0_ffn_b2)
    x = x + _L1_xattn_ref(_layernorm(x, axis=-1), ctx_1024, ctx_1024, L1_xattn_Wq, L1_xattn_bq, L1_xattn_Wk, L1_xattn_bk, L1_xattn_Wv, L1_xattn_bv, L1_xattn_Wo, L1_xattn_bo)
    x = x + _L1_ffn_ref(_layernorm(x, axis=-1), L1_ffn_router_w, L1_ffn_router_b, L1_ffn_experts_inter, L1_ffn_experts_out)
    return x

_drawn_inputs = setup_inputs


def setup_inputs(seed=0):
    import zlib

    import numpy as np

    out = dict(_drawn_inputs(seed))
    spreads = {'L1_xattn_bq': (0.0, 0.453),
     'L1_xattn_bk': (0.0, 2.0),
     'L1_xattn_bv': (0.0, 0.1),
     'L1_xattn_bo': (0.0, 0.1),
     'L1_ffn_router_b': (0.0, 2.0)}
    factors = {'L0_xattn_bq': 5.164,
     'L0_xattn_bk': 64.0,
     'L0_ffn_b1': 8.0,
     'L0_ffn_b2': 3.643,
     'L1_ffn_router_w': 3.321,
     'L1_ffn_experts_inter': 3.056}
    for name, (base, spread) in spreads.items():
        noise = np.random.default_rng([zlib.crc32(name.encode()), seed]).standard_normal(out[name].shape)
        drawn = base * np.exp(spread * noise) if base else spread * noise
        out[name] = jnp.asarray(drawn.astype(out[name].dtype))
    for name, factor in factors.items():
        out[name] = (out[name] * factor).astype(out[name].dtype)
    return out
```

```python
from contextlib import ExitStack

import concourse.bass as bass
from concourse import mybir

F32 = mybir.dt.float32
F32R = mybir.dt.float32r
BF16 = mybir.dt.bfloat16
I32 = mybir.dt.int32
ALU = mybir.AluOpType
ACT = mybir.ActivationFunctionType
AX = mybir.AxisListType

P = 128
D = 256
KC = D // P
NH = 16
HD = D // NH
NI = 1024
IC = NI // P
NE = 8
B = 32
GB = 4
NG = B // GB
GT = GB * P
UH = 8
NU = GB * NH // UH
NT = 6
SR = NT * HD
EPS = 1e-5
MASKED = 10000.0
CAPACITY = B * P // NE
RING = 4
AHEAD = 4
QK_SCALE = float(HD) ** -0.5
Q_PART = (0, 0, 1, 1, 0, 2)
K_PART = (0, 1, 0, 1, 2, 0)
WQ, WK, WV, WO = (0, 3), (1, 4), (2, 5), 6


def build(nc, x, ctxT, mask, wT, bq, bk, bv, bo, w1, w1T, b1, w2T, b2, rwT, rb, e1, e2, out):
    assert GT == CAPACITY == 512
    x_g = x.rearrange("(g b) t d -> g t b d", b=GB)
    out_g = out.rearrange("(g b) t d -> g t b d", b=GB)
    mask_g = mask.rearrange("(g b) q k -> g q b k", b=GB)
    ctx_g = ctxT.rearrange("(c p) (g t) -> g p c t", p=P, t=GT)
    e1_c = e1.rearrange("e (c p) (i n) -> e i p c n", p=P, n=P)
    e2_c = e2.rearrange("e (i p) d -> e i p d", p=P)

    ctx = ExitStack()
    with ctx:
        def sb(name, shape, dt=F32):
            return ctx.enter_context(nc.sbuf_tensor(name, shape, dt))

        def sem(name):
            return ctx.enter_context(nc.semaphore(name))

        w_hi = sb("w_hi", [P, 7, KC, D], F32R)
        w_lo = sb("w_lo", [P, 7, KC, D], F32R)
        sign1 = sb("sign1", [P, KC, NI], F32R)
        sign2 = sb("sign2", [P, IC, D], F32R)
        alpha1 = sb("alpha1", [P, IC])
        alpha2 = sb("alpha2", [P, D])
        bq_sb = sb("bq_sb", [P, 2, KC])
        bk_sb = sb("bk_sb", [P, 2, KC])
        bv_sb = sb("bv_sb", [P, 2, D])
        bo_sb = sb("bo_sb", [P, D])
        b1_sb = sb("b1_sb", [P, IC])
        b2_sb = sb("b2_sb", [P, D])
        rw_raw = sb("rw_raw", [P, KC, NE])
        rw_hi = sb("rw_hi", [P, KC, NE], F32R)
        rw_lo = sb("rw_lo", [P, KC, NE], F32R)
        rb_sb = sb("rb_sb", [P, NE])
        ident = sb("ident", [P, P])
        identb = sb("identb", [P, P], BF16)
        ones = sb("ones", [P, P])
        half = sb("half", [P, GB])
        eps = sb("eps", [P, GB])
        far = sb("far", [P, GB])
        carrier = sb("carrier", [P, 1])
        xa = sb("xa", [P, GB, D])
        xr = sb("xr", [P, GB, D])
        xn = sb("xn", [P, GB, D])
        stats = sb("stats", [P, GB, 6])
        mv = sb("mv", [P, GB, 2])
        vpe = sb("vpe", [P, GB])
        rstd = sb("rstd", [P, GB])
        xT_hi = sb("xT_hi", [P, KC, GT], F32R)
        xT_lo = sb("xT_lo", [P, KC, GT], F32R)
        xm_hi = sb("xm_hi", [P, KC, GT], F32R)
        xm_lo = sb("xm_lo", [P, KC, GT], F32R)
        c_raw = sb("c_raw", [P, KC, GT])
        c_hi = sb("c_hi", [P, KC, GT], F32R)
        c_lo = sb("c_lo", [P, KC, GT], F32R)
        pf = sb("pf", [P, KC, GT])
        parts = sb("parts", [P, 3, KC, GT], BF16)
        v_sb = sb("v_sb", [P, 2, GB, NH, HD + 1])
        qs = sb("qs", [SR + 2, NH, GT], BF16)
        ks = sb("ks", [SR + 2, NH, GT], BF16)
        mask_raw = sb("mask_raw", [P, GB, P])
        mbias = sb("mbias", [P, GB, P])
        mparts = sb("mparts", [P, 3, GB, P], BF16)
        mdiff = sb("mdiff", [P, GB, P], BF16)
        mcnt = sb("mcnt", [P, 1])
        mflag = sb("mflag", [1, 1], I32)
        mneg = sb("mneg", [P, 2, NH])
        mpack = sb("mpack", [P, 2, 2 * NH], BF16)
        mrow = sb("mrow", [2 * NH, 2, P], BF16)
        prob = sb("prob", [P, 2, UH * P])
        pvs = sb("pvs", [P, 2, GB * P])
        rsum = sb("rsum", [P, 2, NH])
        att = sb("att", [P, GB, D])
        hf = pf
        h_hi = sb("h_hi", [P, 3, GT], F32R)
        h_lo = sb("h_lo", [P, 3, GT], F32R)
        ew_raw = sb("ew_raw", [P, RING, 2 * D])
        ew_hi = sb("ew_hi", [P, RING, 2 * D], F32R)
        ew_lo = sb("ew_lo", [P, RING, 2 * D], F32R)
        acc = sb("acc", [P, GB, D])
        lg = sb("lg", [P, GB, NE])
        lmax = sb("lmax", [P, GB])
        lsum = sb("lsum", [P, GB])
        lrec = sb("lrec", [P, GB])
        route = sb("route", [P, GB, NE])
        taken = sb("taken", [P, GB, NE])
        carry = sb("carry", [P, NE])
        filled = sb("filled", [1, 1], I32)

        ps = ctx.enter_context(nc.psum_tensor("ps", [P, 8, 512], F32))
        ps_bf = ps[:, 7, :].bitcast(BF16)

        k_scr = [nc.dram_tensor(f"k_scr{l}", [3, D, GT], BF16).ap() for l in range(2)]
        q_scr = [nc.dram_tensor(f"q_scr{l}", [3, D, GT], BF16).ap() for l in range(2)]

        s_wload = [sem("s_wload_a"), sem("s_wload_b")]
        s_small = sem("s_small_loaded")
        s_const = sem("s_constants")
        s_zero = sem("s_pv_bank_zeroed")
        s_whi = sem("s_weights_hi")
        s_wlo = sem("s_weights_lo")
        s_abs = sem("s_abs_w2")
        s_a2mm = sem("s_alpha2_product")
        s_alpha = sem("s_alphas")
        s_bq = sem("s_scaled_bq")
        s_x = sem("s_x_loaded")
        s_ctx = sem("s_ctx_loaded")
        s_mask = sem("s_mask_loaded")
        s_chi = sem("s_ctx_hi")
        s_clo = sem("s_ctx_lo")
        s_kvmm = sem("s_kv_products")
        s_vev = sem("s_v_evacuated")
        s_qmm = sem("s_q_products")
        s_pev = sem("s_projection_evacuated")
        s_ph = sem("s_part0")
        s_pr = sem("s_rest0")
        s_pm = sem("s_part1")
        s_pl = sem("s_part2")
        s_scr = sem("s_parts_in_dram")
        s_ks = [sem("s_keys_stacked_a"), sem("s_keys_stacked_b")]
        s_qs = [sem("s_queries_stacked_a"), sem("s_queries_stacked_b")]
        s_mcnt = sem("s_mask_counted")
        s_mflmm = sem("s_mask_count_summed")
        s_mfl = sem("s_mask_flag")
        s_mb = sem("s_mask_bias_steps")
        s_mparts = sem("s_mask_parts")
        s_smm = sem("s_scores_for_max")
        s_max = sem("s_row_max")
        s_mhi = sem("s_max_hi")
        s_mpk = sem("s_max_packed")
        s_mtmm = sem("s_max_transposed")
        s_mtc = sem("s_max_rows_copied")
        s_mrow = [sem("s_max_row_placed_a"), sem("s_max_row_placed_b")]
        s_stmm = sem("s_scores_shifted")
        s_exp = sem("s_exp")
        s_pv = sem("s_pv")
        s_pvc = sem("s_pv_copied")
        s_otmm = sem("s_att_transposed")
        s_rs = sem("s_row_sum_inverted")
        s_att = sem("s_att_normalised")
        s_x1 = sem("s_x1")
        s_st = sem("s_ln_stats")
        s_mv = sem("s_ln_moments")
        s_vpe = sem("s_ln_var_eps")
        s_rstd = sem("s_ln_rstd")
        s_xn = sem("s_ln_out")
        s_xtmm = sem("s_xT_products")
        s_xhi = sem("s_xT_hi")
        s_xlo = sem("s_xT_lo")
        s_f1 = sem("s_ffn_up")
        s_gelu = sem("s_gelu")
        s_fhi = sem("s_ffn_h_hi")
        s_flo = sem("s_ffn_h_lo")
        s_f2 = sem("s_ffn_down")
        s_fb2 = sem("s_x1_plus_b2")
        s_fy = sem("s_ffn_scaled")
        s_x2 = sem("s_x2")
        s_x2b = sem("s_x2_plus_bo")
        s_wohi = sem("s_attT_hi")
        s_wolo = sem("s_attT_lo")
        s_wotr = sem("s_attT_products")
        s_womm = sem("s_wo_products")
        s_x3 = sem("s_x3")
        s_out = sem("s_out_stored")
        s_first = sem("s_first_group_stored")
        s_rmm = sem("s_router_products")
        s_rl = sem("s_router_steps")
        s_rex = sem("s_router_exp")
        s_route = sem("s_routing_weights")
        s_ew = [sem(f"s_expert_chunk{r}_loaded") for r in range(RING)]
        s_ewhi = sem("s_expert_chunk_hi")
        s_ewlo = sem("s_expert_chunk_lo")
        s_m1 = sem("s_moe_up")
        s_mhhi = sem("s_moe_h_hi")
        s_mhlo = sem("s_moe_h_lo")
        s_m2 = sem("s_moe_down")
        s_macc = sem("s_moe_added")
        s_taken = sem("s_taken")
        s_count = sem("s_taken_counted")
        s_carry = sem("s_carry_started")
        s_filled = sem("s_filled")
        g_tri = sem("g_triangle")
        g_x = sem("g_x_loaded")
        g_st = sem("g_ln_stats")
        g_mv = sem("g_ln_moments")
        g_vpe = sem("g_ln_var_eps")
        g_rstd = sem("g_ln_rstd")
        g_xn = sem("g_ln_out")
        g_xt = sem("g_xT_products")
        g_xtc = sem("g_xT_copied")
        g_log = sem("g_router_products")
        g_r = sem("g_router_steps")
        g_exp = sem("g_router_exp")
        g_taken = sem("g_taken")
        g_cnt = sem("g_taken_counted")
        g_sel = sem("g_selection_steps")
        g_w = sem("g_expert_loaded")
        g_up = sem("g_up")
        g_relu = sem("g_relu")
        g_down = sem("g_down")
        g_acc = sem("g_added")
        g_st_out = sem("g_stored")

        def count(value):
            return max(value, 0) if isinstance(value, int) else value

        def ln_index(stage, g):
            if stage == 3:
                return 4
            late = 1 if not isinstance(g, int) or g > 1 or (g == 1 and stage > 0) else 0
            return 3 * g + stage + late


        def ln_stats(dve, src, t):
            for b in range(GB):
                dve.bn_stats(stats[:, b], src[:, b]).then_inc(s_st, 1)
            dve.wait_ge(s_st, GB * (t + 1))
            dve.tensor_copy(carrier[:], stats[:, GB - 1, 0:1])
            for b in range(GB):
                dve.bn_aggr(mv[:, b], stats[:, b]).then_inc(s_mv, 1)

        def ln_norm(dve, src, t, hi, lo):
            dve.wait_ge(s_rstd, t + 1)
            dve.wait_ge(s_xtmm, t)
            for b in range(GB):
                dve.tensor_scalar(xn[:, b], src[:, b], mv[:, b, 0:1], rstd[:, b:b + 1],
                                  ALU.subtract, ALU.mult).then_inc(s_xn, 1)
            dve.wait_ge(s_xhi, t + 1)
            dve.tensor_tensor(lo[:], ps[:, 6:8, :], hi[:].bitcast(F32), ALU.subtract).then_inc(s_xlo, 1)

        def ln_pool(pool, t):
            pool.wait_ge(s_mv, GB * (t + 1))
            pool.tensor_tensor(vpe[:], mv[:, :, 1], eps[:], ALU.add).then_inc(s_vpe, 1)
            pool.wait_ge(s_vpe, t + 1)
            pool.tensor_tensor(rstd[:], vpe[:], half[:], ALU.pow).then_inc(s_rstd, 1)

        def ln_tensor(pe, t):
            for b in range(GB):
                pe.wait_ge(s_xn, GB * t + b + 1)
                for c in range(KC):
                    mm = pe.transpose(ps[:, 6 + c, b * P:(b + 1) * P], xn[:, b, c * P:(c + 1) * P], ident[:])
            mm.then_inc(s_xtmm, 1)

        def ln_scalar(act, t, hi):
            act.wait_ge(s_xtmm, t + 1)
            act.activation(hi[:], ps[:, 6:8, :], ACT.Copy).then_inc(s_xhi, 1)

        def split_products(pe, dst, l_hi, l_lo, r_hi, r_lo, n):
            terms = [(l, r) for c in range(n) for l, r in ((l_hi, r_hi), (l_hi, r_lo), (l_lo, r_hi))
                     for l, r in ((l(c), r(c)),)]
            for k, (l, r) in enumerate(terms):
                mm = pe.matmul(dst, l, r, start=(k == 0), stop=(k == len(terms) - 1))
            return mm

        def kv_tensor(pe, l, g):
            v = 2 * g + l
            p = 4 * g + 2 * l
            pe.wait_ge(s_chi, g + 1)
            pe.wait_ge(s_clo, g + 1)
            for n in range(KC):
                cols = slice(n * P, (n + 1) * P)
                split_products(pe, ps[:, n, :],
                               lambda c: w_hi[:, WK[l], c, cols], lambda c: w_lo[:, WK[l], c, cols],
                               lambda c: c_hi[:, c, :], lambda c: c_lo[:, c, :], KC).then_inc(s_kvmm, 1)
            for b in range(GB):
                rows = slice(b * P, (b + 1) * P)
                if b < 2:
                    pe.wait_ge(s_pev, KC * p + b + 1)
                else:
                    pe.wait_ge(s_vev, GB * v + b - 1)
                split_products(pe, ps[:, b % 2, 0:D],
                               lambda c: c_hi[:, c, rows], lambda c: c_lo[:, c, rows],
                               lambda c: w_hi[:, WV[l], c, :], lambda c: w_lo[:, WV[l], c, :],
                               KC).then_inc(s_kvmm, 1)

        def ctx_scalar(act, g):
            act.wait_ge(s_ctx, 16 * (g + 1))
            act.wait_ge(s_kvmm, 6 * 2 * g)
            act.activation(c_hi[:], c_raw[:], ACT.Copy).then_inc(s_chi, 1)

        def ctx_pool(pool, g):
            pool.wait_ge(s_chi, g + 1)
            pool.tensor_tensor(c_lo[:], c_raw[:], c_hi[:].bitcast(F32), ALU.subtract).then_inc(s_clo, 1)

        def k_scalar(act, l, g):
            p = 4 * g + 2 * l
            for n in range(KC):
                act.wait_ge(s_kvmm, 6 * (2 * g + l) + n + 1)
                act.wait_ge(s_pl, p)
                act.activation(pf[:, n, :], ps[:, n, :], ACT.Identity,
                               bias=bk_sb[:, l, n:n + 1]).then_inc(s_pev, 1)

        def q_scalar(act, l, g):
            p = 4 * g + 2 * l + 1
            for n in range(KC):
                act.wait_ge(s_qmm, KC * (2 * g + l) + n + 1)
                act.wait_ge(s_pl, p)
                if l == 1:
                    act.wait_ge(s_flo, IC * (g + 1))
                act.activation(pf[:, n, :], ps[:, n, :], ACT.Identity,
                               bias=bq_sb[:, l, n:n + 1], scale=QK_SCALE).then_inc(s_pev, 1)

        def q_tensor(pe, l, g, t):
            pe.wait_ge(s_xhi, t + 1)
            pe.wait_ge(s_xlo, t + 1)
            for n in range(KC):
                cols = slice(n * P, (n + 1) * P)
                split_products(pe, ps[:, n, :],
                               lambda c: w_hi[:, WQ[l], c, cols], lambda c: w_lo[:, WQ[l], c, cols],
                               lambda c: xT_hi[:, c, :], lambda c: xT_lo[:, c, :], KC).then_inc(s_qmm, 1)

        def part0_vector(dve, p):
            dve.wait_ge(s_pev, KC * (p + 1))
            dve.wait_ge(s_scr, 16 * p)
            dve.tensor_copy(parts[:, 0], pf[:]).then_inc(s_ph, 1)

        def part1_vector(dve, p):
            dve.wait_ge(s_pr, p + 1)
            dve.tensor_copy(parts[:, 1], pf[:]).then_inc(s_pm, 1)

        def rest_pool(pool, p):
            pool.wait_ge(s_ph, p + 1)
            pool.tensor_tensor(pf[:], pf[:], parts[:, 0], ALU.subtract).then_inc(s_pr, 1)

        def part2_pool(pool, p):
            pool.wait_ge(s_pm, p + 1)
            pool.tensor_tensor(parts[:, 2], pf[:], parts[:, 1], ALU.subtract).then_inc(s_pl, 1)

        def v_vector(dve, l, g):
            v = 2 * g + l
            for b in range(GB):
                dve.wait_ge(s_kvmm, 6 * v + KC + b + 1)
                if b == 0:
                    dve.wait_ge(s_pv, count(NU * (v - 1)))
                dve.tensor_tensor(v_sb[:, l, b, :, 0:HD],
                                  ps[:, b % 2, 0:D].rearrange("p (h d) -> p h d", d=HD),
                                  bv_sb[:, l, :].rearrange("p (h d) -> p h d", d=HD),
                                  ALU.add).then_inc(s_vev, 1)

        def scratch_store(sp, scr, p):
            sp.wait_ge(s_pl, p + 1)
            sp.dma_start(scr.rearrange("t (c p) n -> p t c n", p=P), parts[:, :, :, :]).then_inc(s_scr, 16)

        def stack_load(sp, dst, scr, part_of, s, p, v, halves=(0, 1)):
            for hf_ in halves:
                if hf_ == 0:
                    sp.wait_ge(s_scr, 16 * (p + 1))
                cols = slice(hf_ * GT // 2, (hf_ + 1) * GT // 2)
                sp.wait_ge(s_stmm, count(NU * (v - 1) + NU // 2 * (hf_ + 1)))
                for j, part in enumerate(part_of):
                    sp.dma_start(dst[j * HD:(j + 1) * HD, :, cols],
                                 scr[part].rearrange("(h d) n -> d h n", d=HD)[:, :, cols]).then_inc(s[hf_], 16)

        def max_scores(pe, v, b, u):
            j = NU * v + 2 * b + u
            if u == 0:
                pe.wait_ge(s_qs[b // 2], 16 * NT * (v + 1))
                pe.wait_ge(s_ks[b // 2], 16 * NT * (v + 1))
            pe.wait_ge(s_max, j)
            rows = slice(b * P, (b + 1) * P)
            for n in range(UH):
                h = UH * u + n
                mm = pe.matmul(ps[:, n // 4, (n % 4) * P:(n % 4 + 1) * P], qs[0:SR, h, rows], ks[0:SR, h, rows],
                               start=(n % 4 == 0), stop=True, skip_group_check=True)
            return mm

        def mask_max(pe, b, n):
            for part in range(3):
                mm = pe.matmul(ps[:, n, :].rearrange("p (h k) -> p h k", k=P), identb[:],
                               mparts[:, part, b, :].unsqueeze(1).broadcast_to([P, 4, P]),
                               start=False, stop=True, skip_group_check=True)
            return mm

        def mask_shifted(pe, b, n):
            for part in range(3):
                mm = pe.matmul(ps[:, n, :].rearrange("p (h k) -> p h k", k=P), mparts[:, part, b, :],
                               identb[:].unsqueeze(1).broadcast_to([P, 4, P]),
                               start=False, stop=True, skip_group_check=True)
            return mm

        def attention_tensor(pe, l, g):
            v = 2 * g + l
            if l == 1:
                attention_products(pe, l, g, False)
                return
            pe.wait_ge(s_mcnt, g + 1)
            pe.matmul(ps[0:1, 7, 0:1], mcnt[:], ones[:, 0:1], start=True, stop=True).then_inc(s_mflmm, 1)
            pe.wait_ge(s_const, CONSTS)
            pe.wait_ge(s_mfl, g + 1)
            pe.wait_ge(s_mparts, g + 1)
            flag = pe.value_load(mflag[0:1, 0:1], min_val=0, max_val=P * GT)
            with pe.If(flag > 0):
                attention_products(pe, l, g, True)
                pe.nop()
            with pe.Else():
                attention_products(pe, l, g, False)
                pe.nop()

        def attention_products(pe, l, g, masked):
            v = 2 * g + l

            def scores_for_max(n):
                b, u = divmod(n, 2)
                mm = max_scores(pe, v, b, u)
                if masked:
                    for bank in (0, 1):
                        mm = mask_max(pe, b, bank)
                mm.then_inc(s_smm, 1)

            def transposed_max(b):
                pe.wait_ge(s_mpk, GB * v + b + 1)
                pe.wait_ge(s_mtc, GB * v + b)
                if b >= 2:
                    pe.wait_ge(s_att, GB * v + b - 1)
                elif b == 0 and l == 0:
                    pe.wait_ge(s_mfl, g + 1)
                pe.transpose(ps_bf[0:2 * NH, 0:P], mpack[:, b % 2, :], identb[:]).then_inc(s_mtmm, 1)

            def shifted_scores(n):
                b, u = divmod(n, 2)
                j = NU * v + n
                pe.wait_ge(s_mrow[b % 2], 32 * (2 * v + b // 2 + 1))
                pe.wait_ge(s_exp, count(j - 1))
                rows = slice(b * P, (b + 1) * P)
                for k in range(UH):
                    h = UH * u + k
                    mm = pe.matmul(ps[:, 2 + 2 * u + k // 4, (k % 4) * P:(k % 4 + 1) * P],
                                   ks[:, h, rows], qs[:, h, rows],
                                   start=(k % 4 == 0), stop=True, skip_group_check=True)
                if masked:
                    for bank in (2 + 2 * u, 3 + 2 * u):
                        mm = mask_shifted(pe, b, bank)
                mm.then_inc(s_stmm, 1)

            def product_with_values(n):
                b, u = divmod(n, 2)
                pe.wait_ge(s_exp, NU * v + n + 1)
                if u == 0:
                    pe.wait_ge(s_pvc, GB * v + b)
                for k in range(UH):
                    h = UH * u + k
                    q = 32 * (h % 4)
                    mm = pe.matmul(ps[q:q + HD + 1, 6, (h // 4) * P:(h // 4 + 1) * P],
                                   v_sb[:, l, b, h, :], prob[:, u, k * P:(k + 1) * P], start=True, stop=True)
                mm.then_inc(s_pv, 1)

            def transposed_out(b):
                pe.wait_ge(s_pvc, GB * v + b + 1)
                pe.wait_ge(s_mtc, GB * v + min(b + 2, GB))
                pe.wait_ge(s_att, GB * v + b)
                for n in range(4):
                    mm = pe.transpose(ps[:, 7, n * P:(n + 1) * P], pvs[:, b % 2, n * P:(n + 1) * P], ident[:])
                mm.then_inc(s_otmm, 1)

            for b in range(AHEAD // 2):
                scores_for_max(2 * b)
                scores_for_max(2 * b + 1)
                transposed_max(b)
            shifted_scores(0)
            for n in range(NU):
                if n + AHEAD < NU:
                    scores_for_max(n + AHEAD)
                if n + 1 < NU:
                    shifted_scores(n + 1)
                product_with_values(n)
                if n % 2:
                    transposed_out(n // 2)
                    if n + AHEAD < NU:
                        transposed_max((n + AHEAD) // 2)

        def attention_vector(dve, l, g):
            v = 2 * g + l

            def row_max(n):
                b, u = divmod(n, 2)
                dve.wait_ge(s_smm, NU * v + n + 1)
                dve.tensor_reduce(mneg[:, b % 2, u * UH:(u + 1) * UH],
                                  ps[:, 0:2, :].rearrange("p a (h k) -> p (a h) k", k=P),
                                  AX.X, ALU.max, negate=True).then_inc(s_max, 1)
                if u == 1:
                    dve.wait_ge(s_max, NU * v + n + 1)
                    dve.wait_ge(s_mtmm, count(GB * v + b - 1))
                    dve.tensor_copy(mpack[:, b % 2, 0:NH], mneg[:, b % 2]).then_inc(s_mhi, 1)
                    dve.wait_ge(s_mhi, GB * v + b + 1)
                    dve.tensor_tensor(mpack[:, b % 2, NH:2 * NH], mneg[:, b % 2],
                                      mpack[:, b % 2, 0:NH], ALU.subtract).then_inc(s_mpk, 1)

            def normalise(b):
                dve.wait_ge(s_otmm, GB * v + b + 1)
                o = ps[:, 7, :].rearrange("p (h d) -> p h d", d=32)
                dve.reciprocal(rsum[:, b % 2, :], o[:, :, HD]).then_inc(s_rs, 1)
                dve.wait_ge(s_rs, GB * v + b + 1)
                if b == 0:
                    if l == 0:
                        dve.wait_ge(s_wotr, g)
                    else:
                        dve.wait_ge(s_x1, GB * (g + 1))
                dve.tensor_tensor(att[:, b].rearrange("p (h d) -> p h d", d=HD), o[:, :, 0:HD],
                                  rsum[:, b % 2, :].unsqueeze(2).broadcast_to([P, NH, HD]),
                                  ALU.mult).then_inc(s_att, 1)

            for n in range(AHEAD):
                row_max(n)
            for n in range(NU):
                if n + AHEAD < NU:
                    row_max(n + AHEAD)
                if n % 2:
                    normalise(n // 2)

        def attention_scalar(act, l, g):
            v = 2 * g + l

            def max_copy(b):
                act.wait_ge(s_mtmm, GB * v + b + 1)
                act.wait_ge(s_mrow[b % 2], 32 * (2 * v + b // 2))
                act.activation(mrow[:, b % 2, :], ps_bf[0:2 * NH, 0:P], ACT.Copy).then_inc(s_mtc, 1)

            def exponential(n):
                j = NU * v + n
                act.wait_ge(s_stmm, j + 1)
                act.wait_ge(s_pv, count(j - 1))
                u = n % 2
                act.activation(prob[:, u, :], ps[:, 2 + 2 * u:4 + 2 * u, :], ACT.Exp).then_inc(s_exp, 1)

            def out_copy(b):
                act.wait_ge(s_pv, NU * v + 2 * b + 2)
                act.wait_ge(s_otmm, count(GB * v + b - 1))
                act.activation(pvs[:, b % 2, :], ps[:, 6, :], ACT.Copy).then_inc(s_pvc, 1)

            for b in range(AHEAD // 2):
                max_copy(b)
            exponential(0)
            for n in range(NU):
                if n + 1 < NU:
                    exponential(n + 1)
                if n % 2:
                    out_copy(n // 2)
                    if n + AHEAD < NU:
                        max_copy((n + AHEAD) // 2)

        def attention_sync(sp, l, g):
            v = 2 * g + l
            for b in range(GB):
                sp.wait_ge(s_mtc, GB * v + b + 1)
                for k in range(2):
                    sp.dma_start(qs[SR + k:SR + k + 1, :, b * P:(b + 1) * P],
                                 mrow[k * NH:(k + 1) * NH, b % 2, :]).then_inc(s_mrow[b % 2], 16)

        def x1_pool(pool, g):
            pool.wait_ge(s_out, 16 * g)
            for b in range(GB):
                pool.wait_ge(s_att, GB * 2 * g + b + 1)
                pool.tensor_tensor(xr[:, b], xa[:, b], att[:, b], ALU.add).then_inc(s_x1, 1)

        def mask_vector(dve, g):
            dve.wait_ge(s_mask, 16 * (g + 1))
            dve.wait_ge(s_mflmm, g)
            dve.wait_ge(s_mparts, g)
            dve.tensor_scalar(mdiff[:], mask_raw[:], 1.0, 0.0, ALU.not_equal, ALU.add,
                              accum_out=mcnt[:]).then_inc(s_mcnt, 1)

        def mask_flag_vector(dve, g):
            dve.wait_ge(s_mflmm, g + 1)
            dve.tensor_copy(mflag[:], ps[0:1, 7, 0:1]).then_inc(s_mfl, 1)

        def mask_pool(pool, g):
            n = 5 * g
            one = ones[:].unsqueeze(1).broadcast_to([P, GB, P])
            pool.wait_ge(s_mask, 16 * (g + 1))
            pool.wait_ge(s_stmm, count(NU * 2 * g - NU))
            pool.tensor_tensor(mbias[:], mask_raw[:], one, ALU.subtract).then_inc(s_mb, 1)
            pool.wait_ge(s_mb, n + 1)
            pool.tensor_tensor(mbias[:], mbias[:], far[:].unsqueeze(2).broadcast_to([P, GB, P]),
                               ALU.mult).then_inc(s_mb, 1)
            pool.wait_ge(s_mb, n + 2)
            pool.tensor_tensor(mparts[:, 0], mbias[:], one, ALU.mult).then_inc(s_mb, 1)
            pool.wait_ge(s_mb, n + 3)
            pool.tensor_tensor(mbias[:], mbias[:], mparts[:, 0], ALU.subtract).then_inc(s_mb, 1)
            pool.wait_ge(s_mb, n + 4)
            pool.tensor_tensor(mparts[:, 1], mbias[:], one, ALU.mult).then_inc(s_mb, 1)
            pool.wait_ge(s_mb, n + 5)
            pool.tensor_tensor(mparts[:, 2], mbias[:], mparts[:, 1], ALU.subtract).then_inc(s_mparts, 1)

        def ffn_tensor(pe, g, t):
            pe.wait_ge(s_xhi, t + 1)
            pe.wait_ge(s_xlo, t + 1)

            def up(i):
                pe.wait_ge(s_gelu, count(IC * g + i - 1))
                k = 0
                for c in range(KC):
                    for m in (xT_hi, xT_lo):
                        mm = pe.matmul(ps[:, i % 2, :], sign1[:, c, i * P:(i + 1) * P], m[:, c, :],
                                       start=(k == 0), stop=(k == 2 * KC - 1))
                        k += 1
                mm.then_inc(s_f1, 1)

            def down(i):
                for m, s in ((h_hi, s_fhi), (h_lo, s_flo)):
                    pe.wait_ge(s, IC * g + i + 1)
                    for b in range(GB):
                        mm = pe.matmul(ps[:, 2 + b // 2, (b % 2) * D:(b % 2 + 1) * D],
                                       m[:, i % 3, b * P:(b + 1) * P], sign2[:, i, :],
                                       start=(i == 0 and m is h_hi and b % 2 == 0),
                                       stop=(i == IC - 1 and m is h_lo), skip_group_check=True)
                mm.then_inc(s_f2, 1)

            up(0)
            up(1)
            for i in range(IC):
                if i + 2 < IC:
                    up(i + 2)
                down(i)

        def ffn_scalar(act, g):
            for i in range(IC):
                act.wait_ge(s_f1, IC * g + i + 1)
                act.wait_ge(s_flo, count(IC * g + i - 1))
                if i == 0:
                    act.wait_ge(s_pl, 4 * g + 3)
                act.activation(hf[:, i % 2, :], ps[:, i % 2, :], ACT.Gelu,
                               bias=b1_sb[:, i:i + 1], scale=alpha1[:, i:i + 1]).then_inc(s_gelu, 1)

        def ffn_vector(dve, g):
            for i in range(IC):
                n = IC * g + i
                dve.wait_ge(s_gelu, n + 1)
                if i >= 3:
                    dve.wait_ge(s_f2, n - 2)
                dve.tensor_copy(h_hi[:, i % 3, :], hf[:, i % 2, :]).then_inc(s_fhi, 1)
                dve.wait_ge(s_fhi, n + 1)
                dve.tensor_tensor(h_lo[:, i % 3, :], hf[:, i % 2, :], h_hi[:, i % 3, :].bitcast(F32),
                                  ALU.subtract).then_inc(s_flo, 1)
            dve.wait_ge(s_f2, IC * (g + 1))
            dve.wait_ge(s_fb2, g + 1)
            y = att
            for n in range(2):
                dve.tensor_tensor(y[:, 2 * n:2 * n + 2, :], ps[:, 2 + n, :].rearrange("p (b d) -> p b d", d=D),
                                  alpha2[:].unsqueeze(1).broadcast_to([P, 2, D]), ALU.mult).then_inc(s_fy, 1)
            for n in range(2):
                dve.wait_ge(s_fy, 2 * g + n + 1)
                dve.tensor_tensor(xr[:, 2 * n:2 * n + 2, :], xr[:, 2 * n:2 * n + 2, :], y[:, 2 * n:2 * n + 2, :],
                                  ALU.add).then_inc(s_x2, 1)

        def b2_pool(pool, g, t):
            pool.wait_ge(s_xn, GB * (t + 1))
            pool.tensor_tensor(xr[:], xr[:], b2_sb[:].unsqueeze(1).broadcast_to([P, GB, D]),
                               ALU.add).then_inc(s_fb2, 1)

        def bo_pool(pool, g, t):
            pool.wait_ge(s_xn, GB * (t + 1))
            pool.tensor_tensor(xr[:], xr[:], bo_sb[:].unsqueeze(1).broadcast_to([P, GB, D]),
                               ALU.add).then_inc(s_x2b, 1)

        def wo_tensor(pe, g):
            v = 2 * g + 1
            for b in range(GB):
                pe.wait_ge(s_att, GB * v + b + 1)
                for c in range(KC):
                    mm = pe.transpose(ps[:, 6 + c, b * P:(b + 1) * P], att[:, b, c * P:(c + 1) * P], ident[:])
            mm.then_inc(s_wotr, 1)
            pe.wait_ge(s_wohi, g + 1)
            pe.wait_ge(s_wolo, g + 1)
            for b in range(GB):
                rows = slice(b * P, (b + 1) * P)
                terms = [(l, r) for c in range(KC) for l, r in ((xT_hi, w_hi), (xT_hi, w_lo), (xT_lo, w_hi))
                         for l, r in ((l[:, c, rows], r[:, WO, c, :]),)]
                for k, (lh, rh) in enumerate(terms):
                    mm = pe.matmul(ps[:, 2 + b // 2, (b % 2) * D:(b % 2 + 1) * D], lh, rh,
                                   start=(k == 0 and b % 2 == 0), stop=(k == len(terms) - 1),
                                   skip_group_check=True)
                mm.then_inc(s_womm, 1)

        def wo_scalar(act, g):
            act.wait_ge(s_wotr, g + 1)
            act.activation(xT_hi[:], ps[:, 6:8, :], ACT.Copy).then_inc(s_wohi, 1)

        def wo_vector(dve, g):
            dve.wait_ge(s_wohi, g + 1)
            dve.tensor_tensor(xT_lo[:], ps[:, 6:8, :], xT_hi[:].bitcast(F32), ALU.subtract).then_inc(s_wolo, 1)
            dve.wait_ge(s_x2b, g + 1)
            for n in range(2):
                dve.wait_ge(s_womm, GB * g + 2 * n + 2)
                dve.tensor_tensor(xr[:, 2 * n:2 * n + 2, :], ps[:, 2 + n, :].rearrange("p (b d) -> p b d", d=D),
                                  xr[:, 2 * n:2 * n + 2, :], ALU.add).then_inc(s_x3, 1)

        def router_tensor(pe, t):
            pe.wait_ge(s_xhi, t + 1)
            pe.wait_ge(s_xlo, t + 1)
            for b in range(GB):
                rows = slice(b * P, (b + 1) * P)
                mm = split_products(pe, ps[:, 1, b * NE:(b + 1) * NE],
                                    lambda c: xm_hi[:, c, rows], lambda c: xm_lo[:, c, rows],
                                    lambda c: rw_hi[:, c, :], lambda c: rw_lo[:, c, :], KC)
            mm.then_inc(s_rmm, 1)

        def router_vector(dve):
            dve.wait_ge(s_rmm, 1)
            dve.tensor_tensor(lg[:], ps[:, 1, 0:GB * NE].rearrange("p (b e) -> p b e", e=NE),
                              rb_sb[:].unsqueeze(1).broadcast_to([P, GB, NE]), ALU.add).then_inc(s_rl, 1)
            dve.wait_ge(s_rl, 1)
            dve.tensor_reduce(lmax[:], lg[:], AX.X, ALU.max).then_inc(s_rl, 1)
            dve.wait_ge(s_rl, 2)
            dve.tensor_tensor(lg[:], lg[:], lmax[:].unsqueeze(2).broadcast_to([P, GB, NE]),
                              ALU.subtract).then_inc(s_rl, 1)
            dve.wait_ge(s_rex, 1)
            dve.tensor_reduce(lsum[:], route[:], AX.X, ALU.add).then_inc(s_rl, 1)
            dve.wait_ge(s_rl, 4)
            dve.reciprocal(lrec[:], lsum[:]).then_inc(s_rl, 1)
            dve.wait_ge(s_rl, 5)
            dve.tensor_tensor(route[:], route[:], lrec[:].unsqueeze(2).broadcast_to([P, GB, NE]),
                              ALU.mult).then_inc(s_route, 1)

            dve.wait_ge(s_route, 1)
            dve.tensor_scalar(taken[:], route[:], 0.0, None, ALU.is_gt).then_inc(s_taken, 1)
            dve.wait_ge(s_count, 1)
            dve.tensor_copy(carry[:], ps[:, 1, 0:NE]).then_inc(s_carry, 1)
            dve.wait_ge(s_carry, 1)
            dve.tensor_reduce(lsum[0:1, 0:1], carry[0:1, :], AX.X, ALU.add).then_inc(s_rl, 1)
            dve.wait_ge(s_rl, 6)
            dve.tensor_copy(filled[:], lsum[0:1, 0:1]).then_inc(s_filled, 1)

        def router_count_tensor(pe):
            pe.wait_ge(s_taken, 1)
            for b in range(GB):
                mm = pe.matmul(ps[:, 1, 0:NE], ones[:], taken[:, b, :], start=(b == 0), stop=(b == GB - 1))
            mm.then_inc(s_count, 1)

        def router_scalar(act):
            act.wait_ge(s_rl, 3)
            act.activation(route[:], lg[:], ACT.Exp).then_inc(s_rex, 1)

        def expert_sync(sp, e):
            for i in range(IC):
                n = IC * e + i
                r = i % RING
                if i >= RING:
                    sp.wait_ge(s_ewlo, n - RING + 1)
                sp.dma_start(ew_raw[:, r, 0:D].rearrange("p (c n) -> p c n", n=P), e1_c[e, i]).then_inc(s_ew[r], 16)
                sp.dma_start(ew_raw[:, r, D:2 * D], e2_c[e, i]).then_inc(s_ew[r], 16)

        def expert_split_scalar(act, e, i):
            n = IC * e + i
            r = i % RING
            act.wait_ge(s_ew[r], 32 * (2 * e + i // RING + 1))
            if i >= RING:
                act.wait_ge(s_m2, n - RING + 1)
            act.activation(ew_hi[:, r, :], ew_raw[:, r, :], ACT.Copy).then_inc(s_ewhi, 1)

        def expert_pool(pool, e):
            for i in range(IC):
                pool.wait_ge(s_ewhi, IC * e + i + 1)
                pool.tensor_tensor(ew_lo[:, i % RING, :], ew_raw[:, i % RING, :],
                                   ew_hi[:, i % RING, :].bitcast(F32), ALU.subtract).then_inc(s_ewlo, 1)

        def expert_tensor(pe, e):

            def up(i):
                n = IC * e + i
                r = i % RING
                if i >= 2:
                    pe.wait_ge(s_mhlo, n - 1)
                pe.wait_ge(s_ewhi, n + 1)
                pe.wait_ge(s_ewlo, n + 1)
                split_products(pe, ps[:, i % 2, :],
                               lambda c: ew_hi[:, r, c * P:(c + 1) * P], lambda c: ew_lo[:, r, c * P:(c + 1) * P],
                               lambda c: xm_hi[:, c, :], lambda c: xm_lo[:, c, :], KC).then_inc(s_m1, 1)

            def down(i):
                n = IC * e + i
                r = i % RING
                pe.wait_ge(s_mhhi, n + 1)
                for k, (m, w) in enumerate(((h_hi, ew_hi), (h_hi, ew_lo), (h_lo, ew_hi))):
                    if k == 2:
                        pe.wait_ge(s_mhlo, n + 1)
                    for b in range(GB):
                        mm = pe.matmul(ps[:, 4 + b // 2, (b % 2) * D:(b % 2 + 1) * D],
                                       m[:, i % 3, b * P:(b + 1) * P], w[:, r, D:2 * D],
                                       start=(i == 0 and k == 0 and b % 2 == 0),
                                       stop=(i == IC - 1 and k == 2), skip_group_check=True)
                mm.then_inc(s_m2, 1)

            up(0)
            up(1)
            for i in range(IC):
                if i + 2 < IC:
                    up(i + 2)
                down(i)

        def expert_scalar(act, e):
            for i in range(RING):
                expert_split_scalar(act, e, i)
            for i in range(IC):
                n = IC * e + i
                act.wait_ge(s_m1, n + 1)
                if i >= 3:
                    act.wait_ge(s_m2, n - 2)
                act.activation(h_hi[:, i % 3, :], ps[:, i % 2, :], ACT.Relu).then_inc(s_mhhi, 1)
                if i >= 1 and i - 1 + RING < IC:
                    expert_split_scalar(act, e, i - 1 + RING)

        def expert_vector(dve, e, column):
            for i in range(IC):
                n = IC * e + i
                dve.wait_ge(s_mhhi, n + 1)
                dve.scalar_tensor_tensor(out=h_lo[:, i % 3, :], in0=ps[:, i % 2, :], scalar=0.0,
                                         in1=h_hi[:, i % 3, :].bitcast(F32), op0=ALU.max,
                                         op1=ALU.subtract).then_inc(s_mhlo, 1)
            dve.wait_ge(s_m2, IC * (e + 1))
            for b in range(GB):
                dve.scalar_tensor_tensor(out=acc[:, b], in0=ps[:, 4 + b // 2, (b % 2) * D:(b % 2 + 1) * D],
                                         scalar=column(b), in1=acc[:, b], op0=ALU.mult,
                                         op1=ALU.add).then_inc(s_macc, 1)


        GN = B - GB
        RSTEPS, SSTEPS = 6, 4
        tri = xa[:, 0, 0:P]
        gx = xa[:, 1]
        gxT = c_raw[:, :, 0:P]
        gw1 = prob[:].rearrange("p u n -> p (u n)").rearrange("p (c n) -> p c n", c=KC)
        gw2 = ew_raw[:].rearrange("p r n -> p (r n)").rearrange("p (i d) -> p i d", d=D)
        gh = pf[:].rearrange("p c n -> p (c n)")
        grank = lg[:, 1, :]
        gsel = lg[:, 2, :]

        def general(eng, program):
            eng.wait_ge(s_filled, 1)
            n = eng.value_load(filled[0:1, 0:1], min_val=0, max_val=NE * CAPACITY)
            with eng.If(n < NE * CAPACITY):
                program(eng)
                eng.nop()
            with eng.Else():
                eng.nop()

        def tiles(eng, tile):
            tile(0)
            with eng.Fori(1, GN) as k:
                tile(k)

        def experts(eng, k, expert):
            expert(k, 0)
            with eng.Fori(1, NE) as e:
                expert(k, e)

        def general_sync(sp):
            def expert(k, e):
                sp.wait_ge(g_down, NE * k + e)
                sp.dma_start(gw1, e1[e].rearrange("(c p) n -> p c n", p=P)).then_inc(g_w, 16)
                sp.dma_start(gw2, e2[e].rearrange("(i p) d -> p i d", p=P)).then_inc(g_w, 16)

            def tile(k):
                sp.wait_ge(g_st_out, 16 * k)
                sp.dma_start(gx, out[k + GB]).then_inc(g_x, 16)
                experts(sp, k, expert)
                sp.wait_ge(g_acc, NE * k + NE)
                sp.dma_start(out[k + GB], gx).then_inc(g_st_out, 16)

            sp.wait_ge(s_out, 16 * NG)
            sp.wait_ge(s_macc, GB * NE)
            tiles(sp, tile)
            sp.wait_ge(g_st_out, 16 * GN)

        def general_pool(pool):
            def tile(k):
                pool.wait_ge(g_mv, k + 1)
                pool.tensor_tensor(vpe[:, 0:1], mv[:, 0, 1:2], eps[:, 0:1], ALU.add).then_inc(g_vpe, 1)
                pool.wait_ge(g_vpe, k + 1)
                pool.tensor_tensor(rstd[:, 0:1], vpe[:, 0:1], half[:, 0:1], ALU.pow).then_inc(g_rstd, 1)

            pool.memset(tri, 1.0).then_inc(g_tri, 1)
            pool.wait_ge(g_tri, 1)
            pool.affine_select(out=tri, in_=tri, compare_op=ALU.is_gt, fill=0.0, base=0,
                               pattern=[[1, P]], channel_multiplier=-1).then_inc(g_tri, 1)
            tiles(pool, tile)

        def general_vector(dve):
            def expert(k, e):
                dve.wait_ge(g_down, NE * k + e + 1)
                dve.wait_ge(g_sel, SSTEPS * k + 4)
                dve.wait_ge(g_acc, NE * k + e)
                dve.scalar_tensor_tensor(out=gx, in0=ps[:, 2, 0:D], scalar=route[:, 0, bass.ds(e, 1)],
                                         in1=gx, op0=ALU.mult, op1=ALU.add).then_inc(g_acc, 1)

            def tile(k):
                dve.wait_ge(g_x, 16 * k + 16)
                dve.bn_stats(stats[:, 0], gx).then_inc(g_st, 1)
                dve.wait_ge(g_st, k + 1)
                dve.tensor_copy(carrier[:], stats[:, 0, 0:1])
                dve.bn_aggr(mv[:, 0], stats[:, 0]).then_inc(g_mv, 1)
                dve.wait_ge(g_rstd, k + 1)
                dve.tensor_scalar(xn[:, 0], gx, mv[:, 0, 0:1], rstd[:, 0:1],
                                  ALU.subtract, ALU.mult).then_inc(g_xn, 1)
                r, n = lg[:, 0, :], RSTEPS * k
                dve.wait_ge(g_log, k + 1)
                dve.tensor_tensor(r, ps[:, 3, 0:NE], rb_sb[:], ALU.add).then_inc(g_r, 1)
                dve.wait_ge(g_r, n + 1)
                dve.tensor_reduce(lmax[:, 0:1], r, AX.X, ALU.max).then_inc(g_r, 1)
                dve.wait_ge(g_r, n + 2)
                dve.tensor_scalar(r, r, lmax[:, 0:1], None, ALU.subtract).then_inc(g_r, 1)
                dve.wait_ge(g_exp, k + 1)
                dve.tensor_reduce(lsum[:, 0:1], route[:, 0, :], AX.X, ALU.add).then_inc(g_r, 1)
                dve.wait_ge(g_r, n + 4)
                dve.reciprocal(lrec[:, 0:1], lsum[:, 0:1]).then_inc(g_r, 1)
                dve.wait_ge(g_r, n + 5)
                dve.tensor_scalar(route[:, 0, :], route[:, 0, :], lrec[:, 0:1], None, ALU.mult).then_inc(g_r, 1)
                dve.wait_ge(g_r, n + 6)
                dve.tensor_scalar(taken[:, 0, :], route[:, 0, :], 0.0, None, ALU.is_gt).then_inc(g_taken, 1)
                m = SSTEPS * k
                dve.wait_ge(g_cnt, k + 1)
                dve.tensor_tensor(grank, ps[:, 3, NE:2 * NE], carry[:], ALU.add).then_inc(g_sel, 1)
                dve.wait_ge(g_sel, m + 1)
                dve.tensor_scalar(gsel, grank, float(CAPACITY), None, ALU.is_lt).then_inc(g_sel, 1)
                dve.wait_ge(g_sel, m + 2)
                dve.tensor_tensor(route[:, 0, :], route[:, 0, :], gsel, ALU.mult).then_inc(g_sel, 1)
                dve.tensor_tensor(carry[:], ps[:, 3, 2 * NE:3 * NE], carry[:], ALU.add).then_inc(g_sel, 1)
                experts(dve, k, expert)

            tiles(dve, tile)

        def general_scalar(act):
            def expert(k, e):
                act.wait_ge(g_up, NE * k + e + 1)
                act.activation(gh, ps[:, 0:2, :], ACT.Relu).then_inc(g_relu, 1)

            def tile(k):
                act.wait_ge(g_xt, k + 1)
                act.activation(gxT, ps[:, 6, 0:D].rearrange("p (c n) -> p c n", c=KC), ACT.Copy).then_inc(g_xtc, 1)
                act.wait_ge(g_r, RSTEPS * k + 3)
                act.activation(route[:, 0, :], lg[:, 0, :], ACT.Exp).then_inc(g_exp, 1)
                experts(act, k, expert)

            tiles(act, tile)

        def general_tensor(pe):
            def expert(k, e):
                n = NE * k + e
                pe.wait_ge(g_w, 32 * n + 32)
                pe.wait_ge(g_relu, n)
                for i in range(IC):
                    for c in range(KC):
                        mm = pe.matmul(ps[:, i // 4, (i % 4) * P:(i % 4 + 1) * P], gw1[:, c, i * P:(i + 1) * P],
                                       gxT[:, c, :], start=(c == 0), stop=(c == KC - 1))
                mm.then_inc(g_up, 1)
                pe.wait_ge(g_relu, n + 1)
                pe.wait_ge(g_acc, n)
                for i in range(IC):
                    mm = pe.matmul(ps[:, 2, 0:D], gh[:, i * P:(i + 1) * P], gw2[:, i, :],
                                   start=(i == 0), stop=(i == IC - 1))
                mm.then_inc(g_down, 1)

            def tile(k):
                pe.wait_ge(g_xn, k + 1)
                for c in range(KC):
                    mm = pe.transpose(ps[:, 6, c * P:(c + 1) * P], xn[:, 0, c * P:(c + 1) * P], ident[:])
                mm.then_inc(g_xt, 1)
                pe.wait_ge(g_xtc, k + 1)
                pe.wait_ge(g_sel, SSTEPS * k)
                for c in range(KC):
                    mm = pe.matmul(ps[:, 3, 0:NE], gxT[:, c, :], rw_raw[:, c, :], start=(c == 0), stop=(c == KC - 1))
                mm.then_inc(g_log, 1)
                pe.wait_ge(g_taken, k + 1)
                pe.matmul(ps[:, 3, NE:2 * NE], tri, taken[:, 0, :], start=True, stop=True)
                pe.matmul(ps[:, 3, 2 * NE:3 * NE], ones[:], taken[:, 0, :], start=True, stop=True).then_inc(g_cnt, 1)
                experts(pe, k, expert)

            pe.wait_ge(g_tri, 2)
            tiles(pe, tile)

        def after_kv(pe, l, g):
            pe.wait_ge(s_vev, GB * (2 * g + l + 1))

        def after_q(pe, l, g):
            pe.wait_ge(s_pev, KC * (4 * g + 2 * l + 2))

        def after_attention(pe, l, g):
            v = 2 * g + l
            pe.wait_ge(s_max, NU * (v + 1))
            pe.wait_ge(s_exp, NU * (v + 1))
            pe.wait_ge(s_pvc, GB * (v + 1))
            pe.wait_ge(s_att, GB * (v + 1))

        def after_ffn(pe, g):
            pe.wait_ge(s_gelu, IC * (g + 1))
            pe.wait_ge(s_fy, 2 * (g + 1))

        def after_expert(pe, e):
            pe.wait_ge(s_mhlo, IC * (e + 1))
            pe.wait_ge(s_macc, GB * (e + 1))

        def after_wo(pe, g):
            pe.wait_ge(s_x3, 2 * (g + 1))
            pe.wait_ge(s_wolo, g + 1)

        block = ctx.enter_context(nc.Block())

        @block.sync
        def _(sp):
            for n in range(4):
                sp.dma_start(ew_raw[:, n, :].rearrange("p (c d) -> p c d", d=D),
                             wT[n].rearrange("(c p) d -> p c d", p=P)).then_inc(s_wload[0], 16)
            sp.dma_start(c_raw[:], ctx_g[0]).then_inc(s_ctx, 16)
            sp.dma_start(xa[:], x_g[0]).then_inc(s_x, 16)
            for n in range(3):
                sp.dma_start(prob[:].rearrange("p u n -> p (u n)")[:, n * 2 * D:(n + 1) * 2 * D]
                             .rearrange("p (c d) -> p c d", d=D),
                             wT[4 + n].rearrange("(c p) d -> p c d", p=P)).then_inc(s_wload[1], 16)
            sp.dma_start(mask_raw[:], mask_g[0]).then_inc(s_mask, 16)
            sp.wait_ge(s_wlo, 1)
            sp.dma_start(ew_raw[:].rearrange("p r (a n) -> p (r a n)", a=1).rearrange("p (c n) -> p c n", c=KC),
                         w1T.rearrange("(c p) n -> p c n", p=P)).then_inc(s_wload[0], 16)
            sp.wait_ge(s_wlo, 2)
            sp.dma_start(prob[:].rearrange("p u n -> p (u n)").rearrange("p (i d) -> p i d", d=D),
                         w1.rearrange("(i p) d -> p i d", p=P)).then_inc(s_wload[1], 16)
            sp.wait_ge(s_whi, 3)
            sp.dma_start(ew_raw[:].rearrange("p r n -> p (r n)").rearrange("p (i d) -> p i d", d=D),
                         w2T.rearrange("(i p) d -> p i d", p=P)).then_inc(s_wload[0], 16)

            def store_kv(l, g):
                scratch_store(sp, k_scr[l], 4 * g + 2 * l)

            def store_q(l, g):
                scratch_store(sp, q_scr[l], 4 * g + 2 * l + 1)

            def load_k(l, g, halves=(0, 1)):
                stack_load(sp, ks, k_scr[l], K_PART, s_ks, 4 * g + 2 * l, 2 * g + l, halves)

            def load_q(l, g, halves=(0, 1)):
                stack_load(sp, qs, q_scr[l], Q_PART, s_qs, 4 * g + 2 * l + 1, 2 * g + l, halves)

            def body(g, last):
                attention_sync(sp, 0, g)
                if not last:
                    sp.wait_ge(s_clo, g + 1)
                    sp.dma_start(c_raw[:], ctx_g[g + 1]).then_inc(s_ctx, 16)
                    sp.wait_ge(s_x1, GB * (g + 1))
                    sp.dma_start(xa[:], x_g[g + 1]).then_inc(s_x, 16)
                    sp.wait_ge(s_mcnt, g + 1)
                    sp.wait_ge(s_mparts, g + 1)
                    sp.dma_start(mask_raw[:], mask_g[g + 1]).then_inc(s_mask, 16)
                store_kv(1, g)
                load_k(1, g)
                store_q(1, g)
                load_q(1, g)
                if not last:
                    store_kv(0, g + 1)
                    store_q(0, g + 1)

            def body_tail(g, last):
                attention_sync(sp, 1, g)
                if not last:
                    for hf_ in range(2):
                        load_k(0, g + 1, (hf_,))
                        load_q(0, g + 1, (hf_,))

            store_kv(0, 0)
            load_k(0, 0)
            store_q(0, 0)
            load_q(0, 0)
            body(0, False)
            body_tail(0, False)
            with sp.Fori(1, NG - 1) as g:
                body(g, False)
                expert_sync(sp, g - 1)
                body_tail(g, False)
            body(NG - 1, True)
            expert_sync(sp, NG - 2)
            body_tail(NG - 1, True)
            expert_sync(sp, NG - 1)
            general(sp, general_sync)
            sp.wait_ge(s_macc, GB * NE)
            sp.dma_start(out_g[0], acc[:]).then_inc(s_first, 16)
            sp.wait_ge(s_first, 16)
            sp.wait_ge(s_out, 16 * NG)

        @block.gpsimd
        def _(pool):
            pool.memset(ident[:], 0.0).then_inc(s_const, 1)
            pool.memset(identb[:], 0.0).then_inc(s_const, 1)
            pool.wait_ge(s_const, 2)
            for m in (ident, identb):
                pool.affine_select(out=m[:], in_=m[:], compare_op=ALU.not_equal, fill=1.0, base=0,
                                   pattern=[[-1, P]], channel_multiplier=1).then_inc(s_const, 1)
            pool.memset(ones[:], 1.0).then_inc(s_const, 1)
            pool.memset(half[:], -0.5).then_inc(s_const, 1)
            pool.memset(eps[:], EPS).then_inc(s_const, 1)
            pool.memset(far[:], MASKED).then_inc(s_const, 1)
            pool.memset(v_sb[:, :, :, :, HD:HD + 1], 1.0).then_inc(s_const, 1)
            pool.dma_start(bk_sb[:], bk).then_inc(s_small, 16)
            pool.dma_start(bq_sb[:], bq).then_inc(s_small, 16)
            for k in range(2):
                pool.dma_start(bv_sb[:, k, :], bv[k].partition_broadcast(P)).then_inc(s_small, 16)
            pool.dma_start(b1_sb[:], b1).then_inc(s_small, 16)
            pool.dma_start(b2_sb[:], b2.partition_broadcast(P)).then_inc(s_small, 16)
            pool.dma_start(bo_sb[:], bo.partition_broadcast(P)).then_inc(s_small, 16)
            pool.dma_start(rb_sb[:], rb.partition_broadcast(P)).then_inc(s_small, 16)
            pool.dma_start(rw_raw[:], rwT.rearrange("(c p) e -> p c e", p=P)).then_inc(s_small, 16)
            pool.wait_ge(s_small, SMALL)
            pool.wait_ge(s_const, CONSTS)

            ctx_pool(pool, 0)
            ln_pool(pool, ln_index(0, 0))
            rest_pool(pool, 0)
            part2_pool(pool, 0)
            rest_pool(pool, 1)
            part2_pool(pool, 1)
            mask_pool(pool, 0)

            def body(g, last):
                x1_pool(pool, g)
                rest_pool(pool, 4 * g + 2)
                ln_pool(pool, ln_index(1, g))
                part2_pool(pool, 4 * g + 2)
                b2_pool(pool, g, ln_index(1, g))
                ln_pool(pool, ln_index(2, g))
                bo_pool(pool, g, ln_index(2, g))
                rest_pool(pool, 4 * g + 3)
                part2_pool(pool, 4 * g + 3)
                if not last:
                    ctx_pool(pool, g + 1)
                    ln_pool(pool, ln_index(0, g + 1))
                    rest_pool(pool, 4 * g + 4)
                    part2_pool(pool, 4 * g + 4)
                    rest_pool(pool, 4 * g + 5)
                    part2_pool(pool, 4 * g + 5)
                    mask_pool(pool, g + 1)

            def store(g):
                pool.wait_ge(s_x3, 2 * (g + 1))
                pool.dma_start(out_g[g], xr[:]).then_inc(s_out, 16)

            body(0, False)
            pool.wait_ge(s_x3, 2)
            pool.dma_start(acc[:], xr[:]).then_inc(s_out, 16)
            ln_pool(pool, ln_index(3, 0))
            with pool.Fori(1, NG - 1) as g:
                body(g, False)
                expert_pool(pool, g - 1)
                store(g)
            body(NG - 1, True)
            expert_pool(pool, NG - 2)
            store(NG - 1)
            expert_pool(pool, NG - 1)
            general(pool, general_pool)

        @block.scalar
        def _(act):
            act.wait_ge(s_small, SMALL)
            act.wait_ge(s_wload[0], 64)
            raw_a = ew_raw[:].rearrange("p r (c d) -> p r c d", d=D)
            raw_b = prob[:].rearrange("p u n -> p (u n)")
            act.activation(w_hi[:, 0:4], raw_a, ACT.Copy).then_inc(s_whi, 1)
            ctx_scalar(act, 0)
            act.wait_ge(s_wload[1], 48)
            act.activation(w_hi[:, 4:7].rearrange("p a c d -> p (a c d)"), raw_b[:, 0:6 * D], ACT.Copy).then_inc(s_whi, 1)
            k_scalar(act, 0, 0)
            ln_scalar(act, 0, xT_hi)
            q_scalar(act, 0, 0)
            act.wait_ge(s_wload[0], 80)
            act.activation(sign1[:].rearrange("p c n -> p (c n)"), ew_raw[:].rearrange("p r n -> p (r n)"),
                           ACT.Sign).then_inc(s_whi, 1)
            act.wait_ge(s_wload[0], 96)
            act.activation(sign2[:].rearrange("p i d -> p (i d)"), ew_raw[:].rearrange("p r n -> p (r n)"),
                           ACT.Sign).then_inc(s_whi, 1)
            act.activation(rw_hi[:], rw_raw[:], ACT.Copy).then_inc(s_whi, 1)
            act.wait_ge(s_alpha, 1)
            act.activation(raw_b, ew_raw[:].rearrange("p r n -> p (r n)"), ACT.Abs).then_inc(s_abs, 1)

            def body(g, last):
                attention_scalar(act, 0, g)
                k_scalar(act, 1, g)
                ln_scalar(act, ln_index(1, g), xT_hi)
                ffn_scalar(act, g)
                ln_scalar(act, ln_index(2, g), xT_hi)
                q_scalar(act, 1, g)
                if not last:
                    ctx_scalar(act, g + 1)
                    k_scalar(act, 0, g + 1)
                    ln_scalar(act, ln_index(0, g + 1), xT_hi)
                    q_scalar(act, 0, g + 1)

            body(0, False)
            attention_scalar(act, 1, 0)
            wo_scalar(act, 0)
            ln_scalar(act, ln_index(3, 0), xm_hi)
            router_scalar(act)
            with act.Fori(1, NG - 1) as g:
                body(g, False)
                act.wait_ge(s_f2, IC * (g + 1))
                expert_scalar(act, g - 1)
                attention_scalar(act, 1, g)
                wo_scalar(act, g)
            body(NG - 1, True)
            act.wait_ge(s_f2, IC * NG)
            expert_scalar(act, NG - 2)
            attention_scalar(act, 1, NG - 1)
            wo_scalar(act, NG - 1)
            expert_scalar(act, NG - 1)
            general(act, general_scalar)

        @block.vector
        def _(dve):
            dve.memset(ps[:, 6, :], 0.0).then_inc(s_zero, 1)
            dve.memset(ks[SR:SR + 2, :, :], 1.0).then_inc(s_zero, 1)
            dve.wait_ge(s_small, SMALL)
            dve.tensor_scalar(bq_sb[:], bq_sb[:], QK_SCALE, None, ALU.mult).then_inc(s_bq, 1)
            raw_a = ew_raw[:].rearrange("p r (c d) -> p r c d", d=D)
            raw_b = prob[:].rearrange("p u n -> p (u n)")
            dve.wait_ge(s_whi, 1)
            dve.tensor_tensor(w_lo[:, 0:4], raw_a, w_hi[:, 0:4].bitcast(F32), ALU.subtract).then_inc(s_wlo, 1)
            dve.wait_ge(s_whi, 2)
            dve.tensor_tensor(w_lo[:, 4:7].rearrange("p a c d -> p (a c d)"), raw_b[:, 0:6 * D],
                              w_hi[:, 4:7].rearrange("p a c d -> p (a c d)").bitcast(F32),
                              ALU.subtract).then_inc(s_wlo, 1)
            dve.wait_ge(s_x, 16)
            ln_stats(dve, xa, 0)
            part0_vector(dve, 0)
            part1_vector(dve, 0)
            v_vector(dve, 0, 0)
            ln_norm(dve, xa, 0, xT_hi, xT_lo)
            part0_vector(dve, 1)
            part1_vector(dve, 1)
            mask_vector(dve, 0)
            dve.wait_ge(s_wload[1], 64)
            dve.tensor_reduce(alpha1[:], raw_b.rearrange("p (i d) -> p i d", d=D), AX.X, ALU.add,
                              apply_absolute_value=True).then_inc(s_alpha, 1)
            dve.wait_ge(s_alpha, 1)
            dve.tensor_scalar(alpha1[:], alpha1[:], 1.0 / D, None, ALU.mult).then_inc(s_alpha, 1)
            dve.wait_ge(s_whi, 5)
            dve.tensor_tensor(rw_lo[:], rw_raw[:], rw_hi[:].bitcast(F32), ALU.subtract).then_inc(s_wlo, 1)
            dve.wait_ge(s_a2mm, 1)
            dve.tensor_scalar(alpha2[:], ps[:, 5, 0:D], 1.0 / NI, None, ALU.mult).then_inc(s_alpha, 1)

            def body(g, last):
                mask_flag_vector(dve, g)
                attention_vector(dve, 0, g)
                ln = ln_index(1, g)
                part0_vector(dve, 4 * g + 2)
                v_vector(dve, 1, g)
                dve.wait_ge(s_x1, GB * (g + 1))
                ln_stats(dve, xr, ln)
                part1_vector(dve, 4 * g + 2)
                ln_norm(dve, xr, ln, xT_hi, xT_lo)
                ffn_vector(dve, g)
                dve.wait_ge(s_x2, 2 * (g + 1))
                ln_stats(dve, xr, ln_index(2, g))
                ln_norm(dve, xr, ln_index(2, g), xT_hi, xT_lo)
                part0_vector(dve, 4 * g + 3)
                part1_vector(dve, 4 * g + 3)
                if not last:
                    ln = ln_index(0, g + 1)
                    dve.wait_ge(s_x, 16 * (g + 2))
                    ln_stats(dve, xa, ln)
                    part0_vector(dve, 4 * g + 4)
                    v_vector(dve, 0, g + 1)
                    part1_vector(dve, 4 * g + 4)
                    ln_norm(dve, xa, ln, xT_hi, xT_lo)
                    part0_vector(dve, 4 * g + 5)
                    part1_vector(dve, 4 * g + 5)
                    mask_vector(dve, g + 1)

            body(0, False)
            attention_vector(dve, 1, 0)
            wo_vector(dve, 0)
            dve.wait_ge(s_x3, 2)
            ln_stats(dve, xr, ln_index(3, 0))
            ln_norm(dve, xr, ln_index(3, 0), xm_hi, xm_lo)
            router_vector(dve)
            dve.wait_ge(s_route, 1)
            dve.wait_ge(s_out, 16)
            with dve.Fori(1, NG - 1) as g:
                body(g, False)
                expert_vector(dve, g - 1, lambda b: route[:, b, bass.ds(g - 1, 1)])
                attention_vector(dve, 1, g)
                wo_vector(dve, g)
            body(NG - 1, True)
            expert_vector(dve, NG - 2, lambda b: route[:, b, NG - 2:NG - 1])
            attention_vector(dve, 1, NG - 1)
            wo_vector(dve, NG - 1)
            expert_vector(dve, NG - 1, lambda b: route[:, b, NG - 1:NG])
            general(dve, general_vector)

        @block.tensor
        def _(pe):
            pe.wait_ge(s_const, CONSTS)
            pe.wait_ge(s_zero, 2)
            pe.wait_ge(s_wlo, 2)
            pe.wait_ge(s_bq, 1)
            kv_tensor(pe, 0, 0)
            ln_tensor(pe, 0)
            after_kv(pe, 0, 0)
            q_tensor(pe, 0, 0, 0)
            pe.wait_ge(s_abs, 1)
            raw_b = prob[:].rearrange("p u n -> p (u n)")
            for i in range(IC):
                mm = pe.matmul(ps[:, 5, 0:D], ones[:], raw_b[:, i * D:(i + 1) * D], start=(i == 0), stop=(i == IC - 1))
            mm.then_inc(s_a2mm, 1)
            pe.wait_ge(s_alpha, 3)

            def body(g, last):
                pe.wait_ge(s_xlo, ln_index(0, g) + 1)
                attention_tensor(pe, 0, g)
                after_attention(pe, 0, g)
                kv_tensor(pe, 1, g)
                ln_tensor(pe, ln_index(1, g))
                after_kv(pe, 1, g)
                ffn_tensor(pe, g, ln_index(1, g))
                ln_tensor(pe, ln_index(2, g))
                after_ffn(pe, g)
                q_tensor(pe, 1, g, ln_index(2, g))
                if not last:
                    after_q(pe, 1, g)
                    kv_tensor(pe, 0, g + 1)
                    ln_tensor(pe, ln_index(0, g + 1))
                    after_kv(pe, 0, g + 1)
                    q_tensor(pe, 0, g + 1, ln_index(0, g + 1))

            def tail(g):
                attention_tensor(pe, 1, g)
                after_attention(pe, 1, g)
                wo_tensor(pe, g)

            after_q(pe, 0, 0)
            body(0, False)
            after_q(pe, 0, 1)
            pe.wait_ge(s_xlo, ln_index(0, 1) + 1)
            tail(0)
            after_wo(pe, 0)
            ln_tensor(pe, ln_index(3, 0))
            router_tensor(pe, ln_index(3, 0))
            router_count_tensor(pe)
            pe.wait_ge(s_carry, 1)
            with pe.Fori(1, NG - 1) as g:
                after_wo(pe, g - 1)
                body(g, False)
                after_q(pe, 0, g + 1)
                expert_tensor(pe, g - 1)
                after_expert(pe, g - 1)
                tail(g)
            after_wo(pe, NG - 2)
            body(NG - 1, True)
            after_q(pe, 1, NG - 1)
            expert_tensor(pe, NG - 2)
            after_expert(pe, NG - 2)
            tail(NG - 1)
            after_wo(pe, NG - 1)
            expert_tensor(pe, NG - 1)
            pe.wait_ge(s_macc, GB * NE)
            general(pe, general_tensor)


SMALL = 16 * 9
CONSTS = 9


def kernel(**inputs):
    import numpy as np
    import concourse.bacc as bacc
    from concourse.bass_utils import run_bass_kernel_spmd

    a = {k: np.asarray(v) for k, v in inputs.items()}
    layers = ("L0_xattn_", "L1_xattn_")

    def by_feature(vectors):
        return np.ascontiguousarray(np.stack(vectors).reshape(len(vectors), -1, P).transpose(2, 0, 1))

    arrays = {
        "x": a["x"],
        "ctxT": np.ascontiguousarray(a["ctx_1024"].reshape(B * P, D).T),
        "mask": a["mask_BxSxS2_ff1"],
        "wT": np.stack([a[l + w].T for l in layers for w in ("Wq", "Wk", "Wv")] + [a["L1_xattn_Wo"].T]),
        "bq": by_feature([a[l + "bq"] for l in layers]),
        "bk": by_feature([a[l + "bk"] for l in layers]),
        "bv": np.stack([a[l + "bv"] for l in layers]),
        "bo": a["L1_xattn_bo"],
        "w1": a["L0_ffn_w1"],
        "w1T": np.ascontiguousarray(a["L0_ffn_w1"].T),
        "b1": by_feature([a["L0_ffn_b1"]])[:, 0],
        "w2T": np.ascontiguousarray(a["L0_ffn_w2"].T),
        "b2": a["L0_ffn_b2"],
        "rwT": np.ascontiguousarray(a["L1_ffn_router_w"].T),
        "rb": a["L1_ffn_router_b"],
        "e1": a["L1_ffn_experts_inter"],
        "e2": a["L1_ffn_experts_out"],
    }
    nc = bacc.Bacc("TRN2", target_bir_lowering=False, num_devices=1)
    args = [nc.dram_tensor(n, v.shape, mybir.dt.from_np(v.dtype), kind="ExternalInput").ap()
            for n, v in arrays.items()]
    out = nc.dram_tensor("out", (B, P, D), F32, kind="ExternalOutput").ap()
    build(nc, *args, out)
    r = run_bass_kernel_spmd(nc, [arrays], core_ids=[0])
    return r.results[0]["out"]
```

```python
from contextlib import ExitStack

import concourse.bass as bass
from concourse import mybir

F32 = mybir.dt.float32
F32R = mybir.dt.float32r
BF16 = mybir.dt.bfloat16
I32 = mybir.dt.int32
ALU = mybir.AluOpType
ACT = mybir.ActivationFunctionType
AX = mybir.AxisListType

P = 128
D = 256
KC = D // P
NH = 16
HD = D // NH
NI = 1024
IC = NI // P
NE = 8
B = 32
GB = 4
NG = B // GB
GT = GB * P
UH = 8
NU = GB * NH // UH
NT = 6
SR = NT * HD
EPS = 1e-5
MASKED = 10000.0
CAPACITY = B * P // NE
RING = 4
AHEAD = 6
EARLY = 3
QK_SCALE = float(HD) ** -0.5
Q_PART = (0, 0, 1, 1, 0, 2)
K_PART = (0, 1, 0, 1, 2, 0)
WQ, WK, WV, WO = (0, 3), (1, 4), (2, 5), 6


def build(nc, x, ctxT, mask, wT, bq, bk, bv, bo, w1, w1T, b1, w2T, b2, rwT, rb, e1, e2, out):
    assert GT == CAPACITY == 512
    x_g = x.rearrange("(g b) t d -> g t b d", b=GB)
    out_g = out.rearrange("(g b) t d -> g t b d", b=GB)
    mask_g = mask.rearrange("(g b) q k -> g q b k", b=GB)
    ctx_g = ctxT.rearrange("(c p) (g t) -> g p c t", p=P, t=GT)
    e1_c = e1.rearrange("e (c p) (i n) -> e i p c n", p=P, n=P)
    e2_c = e2.rearrange("e (i p) d -> e i p d", p=P)

    ctx = ExitStack()
    with ctx:
        def sb(name, shape, dt=F32):
            return ctx.enter_context(nc.sbuf_tensor(name, shape, dt))

        def sem(name):
            return ctx.enter_context(nc.semaphore(name))

        w_hi = sb("w_hi", [P, 7, KC, D], F32R)
        w_lo = sb("w_lo", [P, 7, KC, D], F32R)
        sign1 = sb("sign1", [P, KC, NI], F32R)
        sign2 = sb("sign2", [P, IC, D], F32R)
        alpha1 = sb("alpha1", [P, IC])
        alpha2 = sb("alpha2", [P, D])
        bq_sb = sb("bq_sb", [P, 2, KC])
        bk_sb = sb("bk_sb", [P, 2, KC])
        bv_sb = sb("bv_sb", [P, 2, D])
        bo_sb = sb("bo_sb", [P, D])
        b1_sb = sb("b1_sb", [P, IC])
        b2_sb = sb("b2_sb", [P, D])
        rw_raw = sb("rw_raw", [P, KC, NE])
        rw_hi = sb("rw_hi", [P, KC, NE], F32R)
        rw_lo = sb("rw_lo", [P, KC, NE], F32R)
        rb_sb = sb("rb_sb", [P, NE])
        ident = sb("ident", [P, P])
        identb = sb("identb", [P, P], BF16)
        ones = sb("ones", [P, P])
        half = sb("half", [P, GB])
        eps = sb("eps", [P, GB])
        far = sb("far", [P, GB])
        carrier = sb("carrier", [P, 1])
        warm = sb("warm", [P, 1])
        xa = sb("xa", [P, GB, D])
        xr = sb("xr", [P, GB, D])
        xn = sb("xn", [P, GB, D])
        stats = sb("stats", [P, GB, 6])
        mv = sb("mv", [P, GB, 2])
        vpe = sb("vpe", [P, GB])
        rstd = sb("rstd", [P, GB])
        xT_hi = sb("xT_hi", [P, KC, GT], F32R)
        xT_lo = sb("xT_lo", [P, KC, GT], F32R)
        xm_hi = sb("xm_hi", [P, KC, GT], F32R)
        xm_lo = sb("xm_lo", [P, KC, GT], F32R)
        c_raw = sb("c_raw", [P, KC, GT])
        c_hi = sb("c_hi", [P, KC, GT], F32R)
        c_lo = sb("c_lo", [P, KC, GT], F32R)
        pf = sb("pf", [P, KC, GT])
        parts = sb("parts", [P, 3, KC, GT], BF16)
        v_sb = sb("v_sb", [P, 2, GB, NH, HD + 1])
        qs = sb("qs", [SR + 2, NH, GT], BF16)
        ks = sb("ks", [SR + 2, NH, GT], BF16)
        mask_raw = sb("mask_raw", [P, GB, P])
        mbias = sb("mbias", [P, GB, P])
        mparts = sb("mparts", [P, 3, GB, P], BF16)
        mdiff = sb("mdiff", [P, GB, P], BF16)
        mcnt = sb("mcnt", [P, 1])
        mflag = sb("mflag", [1, 1], I32)
        mneg = sb("mneg", [P, 2, NH])
        mpack = sb("mpack", [P, 2, 2 * NH], BF16)
        mrow = sb("mrow", [2 * NH, 2, P], BF16)
        prob = sb("prob", [P, 2, UH * P])
        pvs = sb("pvs", [P, 2, GB * P])
        rsum = sb("rsum", [P, 2, NH])
        att = sb("att", [P, GB, D])
        hf = pf
        h_hi = sb("h_hi", [P, 3, GT], F32R)
        h_lo = sb("h_lo", [P, 3, GT], F32R)
        ew_raw = sb("ew_raw", [P, RING, 2 * D])
        ew_hi = sb("ew_hi", [P, RING, 2 * D], F32R)
        ew_lo = sb("ew_lo", [P, RING, 2 * D], F32R)
        acc = sb("acc", [P, GB, D])
        lg = sb("lg", [P, GB, NE])
        lmax = sb("lmax", [P, GB])
        lsum = sb("lsum", [P, GB])
        lrec = sb("lrec", [P, GB])
        route = sb("route", [P, GB, NE])
        taken = sb("taken", [P, GB, NE])
        carry = sb("carry", [P, NE])
        filled = sb("filled", [1, 1], I32)

        ps = ctx.enter_context(nc.psum_tensor("ps", [P, 8, 512], F32))
        ps_bf = ps[:, 7, :].bitcast(BF16)

        k_scr = [nc.dram_tensor(f"k_scr{l}", [3, D, GT], BF16).ap() for l in range(2)]
        q_scr = [nc.dram_tensor(f"q_scr{l}", [3, D, GT], BF16).ap() for l in range(2)]

        s_wload = [sem("s_wload_a"), sem("s_wload_b")]
        s_small = sem("s_small_loaded")
        s_const = sem("s_constants")
        s_zero = sem("s_pv_bank_zeroed")
        s_whi = sem("s_weights_hi")
        s_wlo = sem("s_weights_lo")
        s_abs = sem("s_abs_w2")
        s_a2mm = sem("s_alpha2_product")
        s_alpha = sem("s_alphas")
        s_bq = sem("s_scaled_bq")
        s_x = sem("s_x_loaded")
        s_ctx = sem("s_ctx_loaded")
        s_mask = sem("s_mask_loaded")
        s_chi = sem("s_ctx_hi")
        s_clo = sem("s_ctx_lo")
        s_kvmm = sem("s_kv_products")
        s_vev = sem("s_v_evacuated")
        s_qmm = sem("s_q_products")
        s_pev = sem("s_projection_evacuated")
        s_ph = sem("s_part0")
        s_pr = sem("s_rest0")
        s_pm = sem("s_part1")
        s_pl = sem("s_part2")
        s_scr = sem("s_parts_in_dram")
        s_ks = [sem("s_keys_stacked_a"), sem("s_keys_stacked_b")]
        s_qs = [sem("s_queries_stacked_a"), sem("s_queries_stacked_b")]
        s_mcnt = sem("s_mask_counted")
        s_mflmm = sem("s_mask_count_summed")
        s_mfl0 = sem("s_first_mask_flag")
        s_mfl = sem("s_mask_flag")
        s_mb = sem("s_mask_bias_steps")
        s_mparts = sem("s_mask_parts")
        s_smm = sem("s_scores_for_max")
        s_max = sem("s_row_max")
        s_mhi = sem("s_max_hi")
        s_mpk = sem("s_max_packed")
        s_mtmm = sem("s_max_transposed")
        s_mtc = sem("s_max_rows_copied")
        s_mrow = [sem("s_max_row_placed_a"), sem("s_max_row_placed_b")]
        s_stmm = sem("s_scores_shifted")
        s_exp = sem("s_exp")
        s_pv = sem("s_pv")
        s_pvc = sem("s_pv_copied")
        s_otmm = sem("s_att_transposed")
        s_rs = sem("s_row_sum_inverted")
        s_att = sem("s_att_normalised")
        s_x1 = sem("s_x1")
        s_st = sem("s_ln_stats")
        s_mv = sem("s_ln_moments")
        s_vpe = sem("s_ln_var_eps")
        s_rstd = sem("s_ln_rstd")
        s_xn = sem("s_ln_out")
        s_xtmm = sem("s_xT_products")
        s_xhi = sem("s_xT_hi")
        s_xlo = sem("s_xT_lo")
        s_f1 = sem("s_ffn_up")
        s_gelu = sem("s_gelu")
        s_fhi = sem("s_ffn_h_hi")
        s_flo = sem("s_ffn_h_lo")
        s_f2 = sem("s_ffn_down")
        s_fb2 = sem("s_x1_plus_b2")
        s_fy = sem("s_ffn_scaled")
        s_x2 = sem("s_x2")
        s_x2b = sem("s_x2_plus_bo")
        s_wohi = sem("s_attT_hi")
        s_wolo = sem("s_attT_lo")
        s_wotr = sem("s_attT_products")
        s_womm = sem("s_wo_products")
        s_x3 = sem("s_x3")
        s_out = sem("s_out_stored")
        s_first = sem("s_first_group_stored")
        s_rmm = sem("s_router_products")
        s_rl = sem("s_router_steps")
        s_rex = sem("s_router_exp")
        s_route = sem("s_routing_weights")
        s_ew = [sem(f"s_expert_chunk{r}_loaded") for r in range(RING)]
        s_ewhi = sem("s_expert_chunk_hi")
        s_ewlo = sem("s_expert_chunk_lo")
        s_m1 = sem("s_moe_up")
        s_mhhi = sem("s_moe_h_hi")
        s_mhlo = sem("s_moe_h_lo")
        s_m2 = sem("s_moe_down")
        s_macc = sem("s_moe_added")
        s_taken = sem("s_taken")
        s_count = sem("s_taken_counted")
        s_carry = sem("s_carry_started")
        s_filled = sem("s_filled")
        g_tri = sem("g_triangle")
        g_x = sem("g_x_loaded")
        g_st = sem("g_ln_stats")
        g_mv = sem("g_ln_moments")
        g_vpe = sem("g_ln_var_eps")
        g_rstd = sem("g_ln_rstd")
        g_xn = sem("g_ln_out")
        g_xt = sem("g_xT_products")
        g_xtc = sem("g_xT_copied")
        g_log = sem("g_router_products")
        g_r = sem("g_router_steps")
        g_exp = sem("g_router_exp")
        g_taken = sem("g_taken")
        g_cnt = sem("g_taken_counted")
        g_sel = sem("g_selection_steps")
        g_w = sem("g_expert_loaded")
        g_up = sem("g_up")
        g_relu = sem("g_relu")
        g_down = sem("g_down")
        g_acc = sem("g_added")
        g_st_out = sem("g_stored")

        def count(value):
            return max(value, 0) if isinstance(value, int) else value

        def ln_index(stage, g):
            if stage == 3:
                return 4
            late = 1 if not isinstance(g, int) or g > 1 or (g == 1 and stage > 0) else 0
            return 3 * g + stage + late

        def g_is_later(g):
            return not isinstance(g, int) or g > 0

        def key_split(l, g):
            if l == 1:
                return 4 * g + 2
            return 0 if isinstance(g, int) and g == 0 else 4 * g - 1

        def last_query_split(g):
            last = isinstance(g, int) and g == NG - 1
            return query_split(1, g) if last else query_split(0, g + 1)

        def query_split(l, g):
            if l == 0:
                return 4 * g + 1
            return 4 * g + 3 if isinstance(g, int) and g == NG - 1 else 4 * g + 4

        def ln_stats(dve, src, t):
            for b in range(GB):
                dve.bn_stats(stats[:, b], src[:, b]).then_inc(s_st, 1)
            dve.wait_ge(s_st, GB * (t + 1))
            dve.tensor_copy(carrier[:], stats[:, GB - 1, 0:1])
            for b in range(GB):
                dve.bn_aggr(mv[:, b], stats[:, b]).then_inc(s_mv, 1)

        def ln_norm(dve, src, t):
            dve.wait_ge(s_rstd, t + 1)
            dve.wait_ge(s_xtmm, KC * t)
            for b in range(GB):
                dve.tensor_scalar(xn[:, b], src[:, b], mv[:, b, 0:1], rstd[:, b:b + 1],
                                  ALU.subtract, ALU.mult).then_inc(s_xn, 1)

        def ln_low(dve, t, hi, lo):
            for c in range(KC):
                dve.wait_ge(s_xhi, KC * t + c + 1)
                dve.tensor_tensor(lo[:, c, :], ps[:, 6 + c, :], hi[:, c, :].bitcast(F32),
                                  ALU.subtract).then_inc(s_xlo, 1)

        def ln_pool(pool, t):
            pool.wait_ge(s_mv, GB * (t + 1))
            pool.tensor_tensor(vpe[:], mv[:, :, 1], eps[:], ALU.add).then_inc(s_vpe, 1)
            pool.wait_ge(s_vpe, t + 1)
            pool.tensor_tensor(rstd[:], vpe[:], half[:], ALU.pow).then_inc(s_rstd, 1)

        def ln_tensor(pe, t):
            for c in range(KC):
                for b in range(GB):
                    if c == 0:
                        pe.wait_ge(s_xn, GB * t + b + 1)
                    mm = pe.transpose(ps[:, 6 + c, b * P:(b + 1) * P], xn[:, b, c * P:(c + 1) * P], ident[:])
                mm.then_inc(s_xtmm, 1)

        def ln_scalar(act, t, hi):
            for c in range(KC):
                act.wait_ge(s_xtmm, KC * t + c + 1)
                act.activation(hi[:, c, :], ps[:, 6 + c, :], ACT.Copy).then_inc(s_xhi, 1)

        def split_products(pe, dst, l_hi, l_lo, r_hi, r_lo, n):
            terms = [(l, r) for c in range(n) for l, r in ((l_hi, r_hi), (l_hi, r_lo), (l_lo, r_hi))
                     for l, r in ((l(c), r(c)),)]
            for k, (l, r) in enumerate(terms):
                mm = pe.matmul(dst, l, r, start=(k == 0), stop=(k == len(terms) - 1))
            return mm

        def kv_tensor(pe, l, g):
            v = 2 * g + l
            p = key_split(l, g)
            for n in range(KC):
                key_products(pe, l, g, n, n)
            for b in range(GB):
                if b < 2:
                    pe.wait_ge(s_pev, KC * p + b + 1)
                else:
                    pe.wait_ge(s_vev, GB * v + b - 1)
                value_products(pe, l, g, b, ps[:, b % 2, 0:D])

        def key_products(pe, l, g, n, bank):
            pe.wait_ge(s_clo, g + 1)
            cols = slice(n * P, (n + 1) * P)
            split_products(pe, ps[:, bank, :],
                           lambda c: w_hi[:, WK[l], c, cols], lambda c: w_lo[:, WK[l], c, cols],
                           lambda c: c_hi[:, c, :], lambda c: c_lo[:, c, :], KC).then_inc(s_kvmm, 1)

        def value_products(pe, l, g, b, dst):
            rows = slice(b * P, (b + 1) * P)
            split_products(pe, dst,
                           lambda c: c_hi[:, c, rows], lambda c: c_lo[:, c, rows],
                           lambda c: w_hi[:, WV[l], c, :], lambda c: w_lo[:, WV[l], c, :],
                           KC).then_inc(s_kvmm, 1)

        def value_place(l, b):
            return ps[:, b % 2, 0:D] if l == 0 else ps[:, 4 + b // 2, (b % 2) * D:(b % 2 + 1) * D]

        def ctx_scalar(act, g):
            act.wait_ge(s_ctx, 16 * (g + 1))
            act.wait_ge(s_kvmm, 6 * 2 * g)
            act.activation(c_hi[:], c_raw[:], ACT.Copy).then_inc(s_chi, 1)

        def ctx_pool(pool, g):
            pool.wait_ge(s_chi, g + 1)
            pool.tensor_tensor(c_lo[:], c_raw[:], c_hi[:].bitcast(F32), ALU.subtract).then_inc(s_clo, 1)

        def k_scalar(act, l, g, chunks=range(KC)):
            p = key_split(l, g)
            first_bank = 0 if l == 0 else 2
            if l == 0:
                act.wait_ge(s_flo, count(IC * g))
            for n in chunks:
                act.wait_ge(s_kvmm, 6 * (2 * g + l) + n + 1)
                act.wait_ge(s_pl, p)
                act.activation(pf[:, n, :], ps[:, first_bank + n, :], ACT.Identity,
                               bias=bk_sb[:, l, n:n + 1]).then_inc(s_pev, 1)

        def q_scalar(act, l, g):
            p = query_split(l, g)
            for n in range(KC):
                act.wait_ge(s_qmm, KC * (2 * g + l) + n + 1)
                act.wait_ge(s_pl, p)
                if l == 1:
                    act.wait_ge(s_flo, IC * (g + 1))
                act.activation(pf[:, n, :], ps[:, n, :], ACT.Identity,
                               bias=bq_sb[:, l, n:n + 1], scale=QK_SCALE).then_inc(s_pev, 1)

        def q_tensor(pe, l, g, t):
            for c in range(KC):
                pe.wait_ge(s_xhi, KC * t + c + 1)
                for n in range(KC):
                    for w in (w_hi, w_lo):
                        pe.matmul(ps[:, n, :], w[:, WQ[l], c, n * P:(n + 1) * P], xT_hi[:, c, :],
                                  start=(c == 0 and w is w_hi), stop=False)
            pe.wait_ge(s_xlo, KC * t + KC)
            for n in range(KC):
                for c in range(KC):
                    mm = pe.matmul(ps[:, n, :], w_hi[:, WQ[l], c, n * P:(n + 1) * P], xT_lo[:, c, :],
                                   start=False, stop=(c == KC - 1))
                mm.then_inc(s_qmm, 1)

        def part0_scalar(act, p):
            act.wait_ge(s_pev, KC * (p + 1))
            act.wait_ge(s_scr, 16 * p)
            act.activation(parts[:, 0], pf[:], ACT.Copy).then_inc(s_ph, 1)

        def part1_vector(dve, p):
            dve.wait_ge(s_pr, p + 1)
            dve.tensor_copy(parts[:, 1], pf[:]).then_inc(s_pm, 1)

        def rest_pool(pool, p):
            pool.wait_ge(s_ph, p + 1)
            pool.tensor_tensor(pf[:], pf[:], parts[:, 0], ALU.subtract).then_inc(s_pr, 1)

        def part2_pool(pool, p):
            pool.wait_ge(s_pm, p + 1)
            pool.tensor_tensor(parts[:, 2], pf[:], parts[:, 1], ALU.subtract).then_inc(s_pl, 1)

        def v_vector(dve, l, g, batches):
            v = 2 * g + l
            for b in batches:
                dve.wait_ge(s_kvmm, 6 * v + KC + b + 1)
                if b == 0:
                    dve.wait_ge(s_pv, count(NU * (v - 1)))
                dve.tensor_tensor(v_sb[:, l, b, :, 0:HD],
                                  value_place(l, b).rearrange("p (h d) -> p h d", d=HD),
                                  bv_sb[:, l, :].rearrange("p (h d) -> p h d", d=HD),
                                  ALU.add).then_inc(s_vev, 1)

        def v_pair_vector(dve, g, b):
            v = 2 * g + 1
            dve.wait_ge(s_kvmm, 6 * v + KC + b + 2)
            dve.wait_ge(s_pv, count(NU * (v - 1)))
            dve.tensor_tensor(v_sb[:, 1, b:b + 2, :, 0:HD],
                              ps[:, 4 + b // 2, :].rearrange("p (b h d) -> p b h d", h=NH, d=HD),
                              bv_sb[:, 1, :].rearrange("p (h d) -> p h d", d=HD).unsqueeze(1)
                              .broadcast_to([P, 2, NH, HD]),
                              ALU.add).then_inc(s_vev, 2)

        def scratch_store(sp, scr, p):
            sp.wait_ge(s_pl, p + 1)
            sp.dma_start(scr.rearrange("t (c p) n -> p t c n", p=P), parts[:, :, :, :]).then_inc(s_scr, 16)

        def stack_load(sp, dst, scr, part_of, s, p, v, halves=(0, 1)):
            for hf_ in halves:
                if hf_ == 0:
                    sp.wait_ge(s_scr, 16 * (p + 1))
                cols = slice(hf_ * GT // 2, (hf_ + 1) * GT // 2)
                sp.wait_ge(s_stmm, count(NU * (v - 1) + NU // 2 * (hf_ + 1)))
                for j, part in enumerate(part_of):
                    sp.dma_start(dst[j * HD:(j + 1) * HD, :, cols],
                                 scr[part].rearrange("(h d) n -> d h n", d=HD)[:, :, cols]).then_inc(s[hf_], 16)

        def max_scores(pe, v, b, u, masked):
            j = NU * v + 2 * b + u
            if u == 0:
                pe.wait_ge(s_qs[b // 2], 16 * NT * (v + 1))
                pe.wait_ge(s_ks[b // 2], 16 * NT * (v + 1))
            rows = slice(b * P, (b + 1) * P)
            for n in range(UH):
                h = UH * u + n
                if n % 4 == 0:
                    pe.wait_ge(s_max, count(2 * j + n // 4 - 1))
                mm = pe.matmul(ps[:, n // 4, (n % 4) * P:(n % 4 + 1) * P], qs[0:SR, h, rows], ks[0:SR, h, rows],
                               start=(n % 4 == 0), stop=True, skip_group_check=True)
                if n % 4 == 3:
                    if masked:
                        mm = mask_max(pe, b, n // 4)
                    mm.then_inc(s_smm, 1)

        def mask_max(pe, b, n):
            for part in range(3):
                mm = pe.matmul(ps[:, n, :].rearrange("p (h k) -> p h k", k=P), identb[:],
                               mparts[:, part, b, :].unsqueeze(1).broadcast_to([P, 4, P]),
                               start=False, stop=True, skip_group_check=True)
            return mm

        def mask_shifted(pe, b, n):
            for part in range(3):
                mm = pe.matmul(ps[:, n, :].rearrange("p (h k) -> p h k", k=P), mparts[:, part, b, :],
                               identb[:].unsqueeze(1).broadcast_to([P, 4, P]),
                               start=False, stop=True, skip_group_check=True)
            return mm

        def attention_tensor(pe, l, g):
            v = 2 * g + l
            if l == 1:
                attention_products(pe, l, g, False)
                return
            pe.wait_ge(s_const, CONSTS)
            if isinstance(g, int) and g == 0:
                pe.wait_ge(s_mfl0, 1)
            else:
                pe.wait_ge(s_mfl, g)
            flag = pe.value_load(mflag[0:1, 0:1], min_val=0, max_val=P * GT)
            with pe.If(flag > 0):
                attention_products(pe, l, g, True)
                pe.nop()
            with pe.Else():
                attention_products(pe, l, g, False)
                pe.nop()

        def mask_count_tensor(pe, g):
            pe.wait_ge(s_mcnt, g + 1)
            pe.matmul(ps[0:1, 5, 0:1], mcnt[:], ones[:, 0:1], start=True, stop=True).then_inc(s_mflmm, 1)

        def transposed_out(pe, v, b):
            pe.wait_ge(s_pvc, GB * v + b + 1)
            pe.wait_ge(s_mtc, GB * v + min(b + 1 + AHEAD // 2, GB))
            pe.wait_ge(s_att, GB * v + b)
            for n in range(4):
                mm = pe.transpose(ps[:, 7, n * P:(n + 1) * P], pvs[:, b % 2, n * P:(n + 1) * P], ident[:])
            mm.then_inc(s_otmm, 1)

        def attention_products(pe, l, g, masked):
            v = 2 * g + l
            if masked:
                pe.wait_ge(s_mparts, g + 1)

            def scores_for_max(n):
                max_scores(pe, v, n // 2, n % 2, masked)

            def transposed_max(b):
                pe.wait_ge(s_mpk, GB * v + b + 1)
                pe.wait_ge(s_mtc, GB * v + b)
                if b == 0 and l == 0:
                    pe.wait_ge(s_wolo, KC * g)
                if b > AHEAD // 2:
                    pe.wait_ge(s_att, GB * v + b - AHEAD // 2)
                pe.transpose(ps_bf[0:2 * NH, 0:P], mpack[:, b % 2, :], identb[:]).then_inc(s_mtmm, 1)

            def shifted_scores(n):
                b, u = divmod(n, 2)
                j = NU * v + n
                pe.wait_ge(s_mrow[b % 2], 32 * (2 * v + b // 2 + 1))
                pe.wait_ge(s_exp, count(j - 1))
                if n == 0 and l == 0:
                    pe.wait_ge(s_pev, KC * (key_split(1, g) + 1))
                elif n == 1 and l == 0:
                    pe.wait_ge(s_vev, GB * (v + 2))
                elif n == 0 and g_is_later(g):
                    pe.wait_ge(s_mhlo, IC * g)
                elif n == 0:
                    pe.wait_ge(s_fy, 2)
                elif n == 1 and l == 1:
                    pe.wait_ge(s_macc, GB * g)
                rows = slice(b * P, (b + 1) * P)
                for k in range(UH):
                    h = UH * u + k
                    mm = pe.matmul(ps[:, 2 + 2 * u + k // 4, (k % 4) * P:(k % 4 + 1) * P],
                                   ks[:, h, rows], qs[:, h, rows],
                                   start=(k % 4 == 0), stop=True, skip_group_check=True)
                if masked:
                    for bank in (2 + 2 * u, 3 + 2 * u):
                        mm = mask_shifted(pe, b, bank)
                mm.then_inc(s_stmm, 1)

            def product_with_values(n):
                b, u = divmod(n, 2)
                pe.wait_ge(s_exp, NU * v + n + 1)
                if u == 0:
                    pe.wait_ge(s_pvc, GB * v + b)
                for k in range(UH):
                    h = UH * u + k
                    q = 32 * (h % 4)
                    mm = pe.matmul(ps[q:q + HD + 1, 6, (h // 4) * P:(h // 4 + 1) * P],
                                   v_sb[:, l, b, h, :], prob[:, u, k * P:(k + 1) * P], start=True, stop=True)
                mm.then_inc(s_pv, 1)

            if l == 0:
                scores_for_max(0)
                scores_for_max(1)
                pe.wait_ge(s_x3, 2 * g)
                key_products(pe, 1, g, 0, 2)
                scores_for_max(2)
                transposed_max(0)
                key_products(pe, 1, g, 1, 3)
                scores_for_max(3)
                scores_for_max(4)
                transposed_max(1)
                value_products(pe, 1, g, 0, value_place(1, 0))
                value_products(pe, 1, g, 1, value_place(1, 1))
                scores_for_max(5)
                value_products(pe, 1, g, 2, value_place(1, 2))
                value_products(pe, 1, g, 3, value_place(1, 3))
                transposed_max(2)
            else:
                if g_is_later(g):
                    pe.wait_ge(s_fy, 2 * (g + 1))
                    expert_up(pe, g - 1, 3)
                    expert_up(pe, g - 1, 4)
                    expert_up(pe, g - 1, 5)
                    expert_down(pe, g - 1, 3)
                pe.wait_ge(s_pev, KC * (last_query_split(g) + 1))
                scores_for_max(0)
                if g_is_later(g):
                    expert_up(pe, g - 1, 6)
                    expert_down(pe, g - 1, 4)
                scores_for_max(1)
                if g_is_later(g):
                    expert_up(pe, g - 1, 7)
                    expert_down(pe, g - 1, 5)
                scores_for_max(2)
                transposed_max(0)
                if g_is_later(g):
                    expert_down(pe, g - 1, 6)
                scores_for_max(3)
                if g_is_later(g):
                    expert_down(pe, g - 1, 7)
                scores_for_max(4)
                transposed_max(1)
                scores_for_max(5)
                transposed_max(2)
            shifted_scores(0)
            for n in range(NU):
                if n + AHEAD < NU:
                    scores_for_max(n + AHEAD)
                if n + 1 < NU:
                    shifted_scores(n + 1)
                product_with_values(n)
                if n % 2 and n + AHEAD < NU:
                    transposed_max((n + AHEAD) // 2)
                if n % 2 == 0 and n > 0:
                    transposed_out(pe, v, n // 2 - 1)

        def attention_vector(dve, l, g, column=None):
            v = 2 * g + l

            def row_max(n):
                b, u = divmod(n, 2)
                for a in range(2):
                    dve.wait_ge(s_smm, 2 * (NU * v + n) + a + 1)
                    dve.tensor_reduce(mneg[:, b % 2, u * UH + 4 * a:u * UH + 4 * (a + 1)],
                                      ps[:, a, :].rearrange("p (h k) -> p h k", k=P),
                                      AX.X, ALU.max, negate=True).then_inc(s_max, 1)
                if u == 1:
                    dve.wait_ge(s_max, 2 * (NU * v + n + 1))
                    dve.wait_ge(s_mtmm, count(GB * v + b - 1))
                    dve.tensor_copy(mpack[:, b % 2, 0:NH], mneg[:, b % 2]).then_inc(s_mhi, 1)
                    dve.wait_ge(s_mhi, GB * v + b + 1)
                    dve.tensor_tensor(mpack[:, b % 2, NH:2 * NH], mneg[:, b % 2],
                                      mpack[:, b % 2, 0:NH], ALU.subtract).then_inc(s_mpk, 1)

            def normalise(b):
                dve.wait_ge(s_otmm, GB * v + b + 1)
                o = ps[:, 7, :].rearrange("p (h d) -> p h d", d=32)
                dve.reciprocal(rsum[:, b % 2, :], o[:, :, HD]).then_inc(s_rs, 1)
                dve.wait_ge(s_rs, GB * v + b + 1)
                if b == 0:
                    if l == 0:
                        dve.wait_ge(s_wotr, KC * g)
                    else:
                        dve.wait_ge(s_x1, GB * (g + 1))
                dve.tensor_tensor(att[:, b].rearrange("p (h d) -> p h d", d=HD), o[:, :, 0:HD],
                                  rsum[:, b % 2, :].unsqueeze(2).broadcast_to([P, NH, HD]),
                                  ALU.mult).then_inc(s_att, 1)

            if l == 0:
                for n in range(AHEAD):
                    row_max(n)
                for b in (0, 2):
                    v_pair_vector(dve, g, b)
                part1_vector(dve, key_split(1, g))
            else:
                later = g_is_later(g)
                if later:
                    expert_low(dve, g - 1, 5)
                row_max(0)
                if later:
                    expert_low(dve, g - 1, 6)
                row_max(1)
                if later:
                    expert_low(dve, g - 1, 7)
                for n in range(2, AHEAD):
                    row_max(n)
                    if n == 3 and later:
                        expert_add(dve, g - 1, column)
            for n in range(NU):
                if n + AHEAD < NU:
                    row_max(n + AHEAD)
                if n % 2 == 0 and n > 0:
                    normalise(n // 2 - 1)
            normalise(GB - 1)

        def attention_scalar(act, l, g):
            v = 2 * g + l

            def max_copy(b):
                act.wait_ge(s_mtmm, GB * v + b + 1)
                act.wait_ge(s_mrow[b % 2], 32 * (2 * v + b // 2))
                act.activation(mrow[:, b % 2, :], ps_bf[0:2 * NH, 0:P], ACT.Copy).then_inc(s_mtc, 1)

            def exponential(n):
                j = NU * v + n
                act.wait_ge(s_stmm, j + 1)
                act.wait_ge(s_pv, count(j - 1))
                u = n % 2
                act.activation(prob[:, u, :], ps[:, 2 + 2 * u:4 + 2 * u, :], ACT.Exp).then_inc(s_exp, 1)

            def out_copy(b):
                act.wait_ge(s_pv, NU * v + 2 * b + 2)
                act.wait_ge(s_otmm, count(GB * v + b - 1))
                act.activation(pvs[:, b % 2, :], ps[:, 6, :], ACT.Copy).then_inc(s_pvc, 1)

            if l == 0:
                k_scalar(act, 1, g, range(0, 1))
                max_copy(0)
                k_scalar(act, 1, g, range(1, 2))
                part0_scalar(act, key_split(1, g))
                max_copy(1)
                max_copy(2)
            else:
                for b in range(AHEAD // 2):
                    max_copy(b)
            exponential(0)
            for n in range(NU):
                if n + 1 < NU:
                    exponential(n + 1)
                if l == 0 and g_is_later(g) and 0 <= n - 3 < EARLY:
                    expert_split_scalar(act, g - 1, n - 3)
                if n % 2:
                    out_copy(n // 2)
                    if n + AHEAD < NU:
                        max_copy((n + AHEAD) // 2)

        def attention_sync(sp, l, g):
            v = 2 * g + l
            for b in range(GB):
                sp.wait_ge(s_mtc, GB * v + b + 1)
                for k in range(2):
                    sp.dma_start(qs[SR + k:SR + k + 1, :, b * P:(b + 1) * P],
                                 mrow[k * NH:(k + 1) * NH, b % 2, :]).then_inc(s_mrow[b % 2], 16)
                if l == 0 and b == AHEAD // 2 - 1 and g_is_later(g):
                    expert_sync(sp, g - 1, range(RING))

        def x1_pool(pool, g):
            pool.wait_ge(s_out, 16 * g)
            for b in range(GB):
                if g_is_later(g) and b < EARLY:
                    expert_pool(pool, g - 1, range(b, b + 1))
                pool.wait_ge(s_att, GB * 2 * g + b + 1)
                pool.tensor_tensor(xr[:, b], xa[:, b], att[:, b], ALU.add).then_inc(s_x1, 1)

        def mask_vector(dve, g):
            dve.wait_ge(s_mask, 16 * (g + 1))
            dve.wait_ge(s_mflmm, g)
            dve.tensor_scalar(mdiff[:], mask_raw[:], 1.0, 0.0, ALU.not_equal, ALU.add,
                              accum_out=mcnt[:]).then_inc(s_mcnt, 1)

        def mask_flag_vector(dve, g):
            dve.wait_ge(s_mflmm, g + 1)
            first = isinstance(g, int) and g == 0
            dve.tensor_copy(mflag[:], ps[0:1, 5, 0:1]).then_inc(s_mfl0 if first else s_mfl, 1)

        def mask_pool(pool, g):
            n = 5 * g
            one = ones[:].unsqueeze(1).broadcast_to([P, GB, P])
            pool.wait_ge(s_mask, 16 * (g + 1))
            pool.wait_ge(s_stmm, count(NU * 2 * g - NU))
            pool.tensor_tensor(mbias[:], mask_raw[:], one, ALU.subtract).then_inc(s_mb, 1)
            pool.wait_ge(s_mb, n + 1)
            pool.tensor_tensor(mbias[:], mbias[:], far[:].unsqueeze(2).broadcast_to([P, GB, P]),
                               ALU.mult).then_inc(s_mb, 1)
            pool.wait_ge(s_mb, n + 2)
            pool.tensor_tensor(mparts[:, 0], mbias[:], one, ALU.mult).then_inc(s_mb, 1)
            pool.wait_ge(s_mb, n + 3)
            pool.tensor_tensor(mbias[:], mbias[:], mparts[:, 0], ALU.subtract).then_inc(s_mb, 1)
            pool.wait_ge(s_mb, n + 4)
            pool.tensor_tensor(mparts[:, 1], mbias[:], one, ALU.mult).then_inc(s_mb, 1)
            pool.wait_ge(s_mb, n + 5)
            pool.tensor_tensor(mparts[:, 2], mbias[:], mparts[:, 1], ALU.subtract).then_inc(s_mparts, 1)

        def ffn_tensor(pe, g, t):
            def up_part(i, m):
                for c in range(KC):
                    mm = pe.matmul(ps[:, i % 2, :], sign1[:, c, i * P:(i + 1) * P], m[:, c, :],
                                   start=(m is xT_hi and c == 0), stop=(m is xT_lo and c == KC - 1))
                return mm

            def up(i):
                pe.wait_ge(s_gelu, IC * g + i - 1)
                up_part(i, xT_hi)
                up_part(i, xT_lo).then_inc(s_f1, 1)

            def down(i):
                for m, s in ((h_hi, s_fhi), (h_lo, s_flo)):
                    pe.wait_ge(s, IC * g + i + 1)
                    for b in range(GB):
                        mm = pe.matmul(ps[:, 2 + b // 2, (b % 2) * D:(b % 2 + 1) * D],
                                       m[:, i % 3, b * P:(b + 1) * P], sign2[:, i, :],
                                       start=(i == 0 and m is h_hi and b % 2 == 0),
                                       stop=(i == IC - 1 and m is h_lo), skip_group_check=True)
                mm.then_inc(s_f2, 1)

            pe.wait_ge(s_xhi, KC * t + KC)
            up_part(0, xT_hi)
            up_part(1, xT_hi)
            pe.wait_ge(s_xlo, KC * t + KC)
            up_part(0, xT_lo).then_inc(s_f1, 1)
            up_part(1, xT_lo).then_inc(s_f1, 1)
            for i in range(IC):
                if i + 2 < IC:
                    up(i + 2)
                down(i)

        def ffn_scalar(act, g):
            for i in range(IC):
                act.wait_ge(s_f1, IC * g + i + 1)
                act.wait_ge(s_flo, count(IC * g + i - 1))
                if i == 0:
                    act.wait_ge(s_pl, 4 * g + 3)
                act.activation(hf[:, i % 2, :], ps[:, i % 2, :], ACT.Gelu,
                               bias=b1_sb[:, i:i + 1], scale=alpha1[:, i:i + 1]).then_inc(s_gelu, 1)
                if g_is_later(g) and 1 <= i <= 4:
                    expert_split_scalar(act, g - 1, EARLY + i - 1)

        def ffn_vector(dve, g):
            for i in range(IC):
                n = IC * g + i
                dve.wait_ge(s_gelu, n + 1)
                if g_is_later(g) and i < EARLY:
                    dve.wait_ge(s_m2, n - IC + 1)
                if i >= 3:
                    dve.wait_ge(s_f2, n - 2)
                dve.tensor_copy(h_hi[:, i % 3, :], hf[:, i % 2, :]).then_inc(s_fhi, 1)
                dve.wait_ge(s_fhi, n + 1)
                dve.tensor_tensor(h_lo[:, i % 3, :], hf[:, i % 2, :], h_hi[:, i % 3, :].bitcast(F32),
                                  ALU.subtract).then_inc(s_flo, 1)
            dve.wait_ge(s_f2, IC * (g + 1))
            dve.wait_ge(s_fb2, g + 1)
            y = att
            for n in range(2):
                dve.tensor_tensor(y[:, 2 * n:2 * n + 2, :], ps[:, 2 + n, :].rearrange("p (b d) -> p b d", d=D),
                                  alpha2[:].unsqueeze(1).broadcast_to([P, 2, D]), ALU.mult).then_inc(s_fy, 1)
            for n in range(2):
                dve.wait_ge(s_fy, 2 * g + n + 1)
                dve.tensor_tensor(xr[:, 2 * n:2 * n + 2, :], xr[:, 2 * n:2 * n + 2, :], y[:, 2 * n:2 * n + 2, :],
                                  ALU.add).then_inc(s_x2, 1)

        def b2_pool(pool, g, t):
            pool.wait_ge(s_xn, GB * (t + 1))
            pool.tensor_tensor(xr[:], xr[:], b2_sb[:].unsqueeze(1).broadcast_to([P, GB, D]),
                               ALU.add).then_inc(s_fb2, 1)

        def bo_pool(pool, g, t):
            pool.wait_ge(s_xn, GB * (t + 1))
            pool.tensor_tensor(xr[:], xr[:], bo_sb[:].unsqueeze(1).broadcast_to([P, GB, D]),
                               ALU.add).then_inc(s_x2b, 1)

        def wo_tensor(pe, g):
            v = 2 * g + 1
            for c in range(KC):
                for b in range(GB):
                    if c == 0:
                        pe.wait_ge(s_att, GB * v + b + 1)
                    mm = pe.transpose(ps[:, 6 + c, b * P:(b + 1) * P], att[:, b, c * P:(c + 1) * P], ident[:])
                mm.then_inc(s_wotr, 1)

            def products(b, m, w, c):
                return pe.matmul(ps[:, 2 + b // 2, (b % 2) * D:(b % 2 + 1) * D], m[:, c, b * P:(b + 1) * P],
                                 w[:, WO, c, :], start=(c == 0 and m is xT_hi and w is w_hi and b % 2 == 0),
                                 stop=(c == KC - 1 and m is xT_lo), skip_group_check=True)

            for c in range(KC):
                pe.wait_ge(s_wohi, KC * g + c + 1)
                for b in range(GB):
                    products(b, xT_hi, w_hi, c)
                    products(b, xT_hi, w_lo, c)
            pe.wait_ge(s_wolo, KC * g + KC)
            for b in range(GB):
                for c in range(KC):
                    mm = products(b, xT_lo, w_hi, c)
                mm.then_inc(s_womm, 1)

        def wo_scalar(act, g):
            for c in range(KC):
                act.wait_ge(s_wotr, KC * g + c + 1)
                act.activation(xT_hi[:, c, :], ps[:, 6 + c, :], ACT.Copy).then_inc(s_wohi, 1)

        def wo_vector(dve, g):
            for c in range(KC):
                dve.wait_ge(s_wohi, KC * g + c + 1)
                dve.tensor_tensor(xT_lo[:, c, :], ps[:, 6 + c, :], xT_hi[:, c, :].bitcast(F32),
                                  ALU.subtract).then_inc(s_wolo, 1)
            dve.wait_ge(s_x2b, g + 1)
            for n in range(2):
                dve.wait_ge(s_womm, GB * g + 2 * n + 2)
                dve.tensor_tensor(xr[:, 2 * n:2 * n + 2, :], ps[:, 2 + n, :].rearrange("p (b d) -> p b d", d=D),
                                  xr[:, 2 * n:2 * n + 2, :], ALU.add).then_inc(s_x3, 1)

        def router_tensor(pe, t):
            pe.wait_ge(s_xhi, KC * t + KC)
            pe.wait_ge(s_xlo, KC * t + KC)
            for b in range(GB):
                rows = slice(b * P, (b + 1) * P)
                mm = split_products(pe, ps[:, 1, b * NE:(b + 1) * NE],
                                    lambda c: xm_hi[:, c, rows], lambda c: xm_lo[:, c, rows],
                                    lambda c: rw_hi[:, c, :], lambda c: rw_lo[:, c, :], KC)
            mm.then_inc(s_rmm, 1)

        def router_vector(dve):
            dve.wait_ge(s_rmm, 1)
            dve.tensor_tensor(lg[:], ps[:, 1, 0:GB * NE].rearrange("p (b e) -> p b e", e=NE),
                              rb_sb[:].unsqueeze(1).broadcast_to([P, GB, NE]), ALU.add).then_inc(s_rl, 1)
            dve.wait_ge(s_rl, 1)
            dve.tensor_reduce(lmax[:], lg[:], AX.X, ALU.max).then_inc(s_rl, 1)
            dve.wait_ge(s_rl, 2)
            dve.tensor_tensor(lg[:], lg[:], lmax[:].unsqueeze(2).broadcast_to([P, GB, NE]),
                              ALU.subtract).then_inc(s_rl, 1)
            dve.wait_ge(s_rex, 1)
            dve.tensor_reduce(lsum[:], route[:], AX.X, ALU.add).then_inc(s_rl, 1)
            dve.wait_ge(s_rl, 4)
            dve.reciprocal(lrec[:], lsum[:]).then_inc(s_rl, 1)
            dve.wait_ge(s_rl, 5)
            dve.tensor_tensor(route[:], route[:], lrec[:].unsqueeze(2).broadcast_to([P, GB, NE]),
                              ALU.mult).then_inc(s_route, 1)

            dve.wait_ge(s_route, 1)
            dve.tensor_scalar(taken[:], route[:], 0.0, None, ALU.is_gt).then_inc(s_taken, 1)
            dve.wait_ge(s_count, 1)
            dve.tensor_copy(carry[:], ps[:, 1, 0:NE]).then_inc(s_carry, 1)
            dve.wait_ge(s_carry, 1)
            dve.tensor_reduce(lsum[0:1, 0:1], carry[0:1, :], AX.X, ALU.add).then_inc(s_rl, 1)
            dve.wait_ge(s_rl, 6)
            dve.tensor_copy(filled[:], lsum[0:1, 0:1]).then_inc(s_filled, 1)

        def router_count_tensor(pe):
            pe.wait_ge(s_taken, 1)
            for b in range(GB):
                mm = pe.matmul(ps[:, 1, 0:NE], ones[:], taken[:, b, :], start=(b == 0), stop=(b == GB - 1))
            mm.then_inc(s_count, 1)

        def router_scalar(act):
            act.wait_ge(s_rl, 3)
            act.activation(route[:], lg[:], ACT.Exp).then_inc(s_rex, 1)

        def expert_sync(sp, e, chunks):
            for i in chunks:
                n = IC * e + i
                r = i % RING
                if i >= RING:
                    sp.wait_ge(s_ewlo, n - RING + 1)
                sp.dma_start(ew_raw[:, r, 0:D].rearrange("p (c n) -> p c n", n=P), e1_c[e, i]).then_inc(s_ew[r], 16)
                sp.dma_start(ew_raw[:, r, D:2 * D], e2_c[e, i]).then_inc(s_ew[r], 16)

        def expert_split_scalar(act, e, i):
            n = IC * e + i
            r = i % RING
            act.wait_ge(s_ew[r], 32 * (2 * e + i // RING + 1))
            if i >= RING:
                act.wait_ge(s_m2, n - RING + 1)
            act.activation(ew_hi[:, r, :], ew_raw[:, r, :], ACT.Copy).then_inc(s_ewhi, 1)

        def expert_pool(pool, e, chunks):
            for i in chunks:
                pool.wait_ge(s_ewhi, IC * e + i + 1)
                pool.tensor_tensor(ew_lo[:, i % RING, :], ew_raw[:, i % RING, :],
                                   ew_hi[:, i % RING, :].bitcast(F32), ALU.subtract).then_inc(s_ewlo, 1)

        def hidden_bank(i):
            return i % 2 + (0 if i < EARLY else 2)

        def expert_up(pe, e, i):
            n = IC * e + i
            r = i % RING
            if i >= 2:
                pe.wait_ge(s_mhlo, n - 1)
            pe.wait_ge(s_ewhi, n + 1)
            pe.wait_ge(s_ewlo, n + 1)
            split_products(pe, ps[:, hidden_bank(i), :],
                           lambda c: ew_hi[:, r, c * P:(c + 1) * P], lambda c: ew_lo[:, r, c * P:(c + 1) * P],
                           lambda c: xm_hi[:, c, :], lambda c: xm_lo[:, c, :], KC).then_inc(s_m1, 1)

        def expert_down(pe, e, i):
            n = IC * e + i
            r = i % RING
            pe.wait_ge(s_mhhi, n + 1)
            for k, (m, w) in enumerate(((h_hi, ew_hi), (h_hi, ew_lo), (h_lo, ew_hi))):
                if k == 2:
                    pe.wait_ge(s_mhlo, n + 1)
                for b in range(GB):
                    mm = pe.matmul(ps[:, 4 + b // 2, (b % 2) * D:(b % 2 + 1) * D],
                                   m[:, i % 3, b * P:(b + 1) * P], w[:, r, D:2 * D],
                                   start=(i == 0 and k == 0 and b % 2 == 0),
                                   stop=(i == IC - 1 and k == 2), skip_group_check=True)
            mm.then_inc(s_m2, 1)

        def expert_relu(act, e, i):
            n = IC * e + i
            act.wait_ge(s_m1, n + 1)
            if i >= 3:
                act.wait_ge(s_m2, n - 2)
            act.activation(h_hi[:, i % 3, :], ps[:, hidden_bank(i), :], ACT.Relu).then_inc(s_mhhi, 1)

        def expert_low(dve, e, i):
            dve.wait_ge(s_mhhi, IC * e + i + 1)
            dve.scalar_tensor_tensor(out=h_lo[:, i % 3, :], in0=ps[:, hidden_bank(i), :], scalar=0.0,
                                     in1=h_hi[:, i % 3, :].bitcast(F32), op0=ALU.max,
                                     op1=ALU.subtract).then_inc(s_mhlo, 1)

        def expert_add(dve, e, column):
            dve.wait_ge(s_m2, IC * (e + 1))
            for b in range(GB):
                dve.scalar_tensor_tensor(out=acc[:, b], in0=ps[:, 4 + b // 2, (b % 2) * D:(b % 2 + 1) * D],
                                         scalar=column(b), in1=acc[:, b], op0=ALU.mult,
                                         op1=ALU.add).then_inc(s_macc, 1)


        GN = B - GB
        RSTEPS, SSTEPS = 6, 4
        tri = xa[:, 0, 0:P]
        gx = xa[:, 1]
        gxT = c_raw[:, :, 0:P]
        gw1 = prob[:].rearrange("p u n -> p (u n)").rearrange("p (c n) -> p c n", c=KC)
        gw2 = ew_raw[:].rearrange("p r n -> p (r n)").rearrange("p (i d) -> p i d", d=D)
        gh = pf[:].rearrange("p c n -> p (c n)")
        grank = lg[:, 1, :]
        gsel = lg[:, 2, :]

        def general(eng, program):
            eng.wait_ge(s_filled, 1)
            n = eng.value_load(filled[0:1, 0:1], min_val=0, max_val=NE * CAPACITY)
            with eng.If(n < NE * CAPACITY):
                program(eng)
                eng.nop()
            with eng.Else():
                eng.nop()

        def tiles(eng, tile):
            tile(0)
            with eng.Fori(1, GN) as k:
                tile(k)

        def experts(eng, k, expert):
            expert(k, 0)
            with eng.Fori(1, NE) as e:
                expert(k, e)

        def general_sync(sp):
            def expert(k, e):
                sp.wait_ge(g_down, NE * k + e)
                sp.dma_start(gw1, e1[e].rearrange("(c p) n -> p c n", p=P)).then_inc(g_w, 16)
                sp.dma_start(gw2, e2[e].rearrange("(i p) d -> p i d", p=P)).then_inc(g_w, 16)

            def tile(k):
                sp.wait_ge(g_st_out, 16 * k)
                sp.dma_start(gx, out[k + GB]).then_inc(g_x, 16)
                experts(sp, k, expert)
                sp.wait_ge(g_acc, NE * k + NE)
                sp.dma_start(out[k + GB], gx).then_inc(g_st_out, 16)

            sp.wait_ge(s_out, 16 * NG)
            sp.wait_ge(s_macc, GB * NE)
            tiles(sp, tile)
            sp.wait_ge(g_st_out, 16 * GN)

        def general_pool(pool):
            def tile(k):
                pool.wait_ge(g_mv, k + 1)
                pool.tensor_tensor(vpe[:, 0:1], mv[:, 0, 1:2], eps[:, 0:1], ALU.add).then_inc(g_vpe, 1)
                pool.wait_ge(g_vpe, k + 1)
                pool.tensor_tensor(rstd[:, 0:1], vpe[:, 0:1], half[:, 0:1], ALU.pow).then_inc(g_rstd, 1)

            pool.memset(tri, 1.0).then_inc(g_tri, 1)
            pool.wait_ge(g_tri, 1)
            pool.affine_select(out=tri, in_=tri, compare_op=ALU.is_gt, fill=0.0, base=0,
                               pattern=[[1, P]], channel_multiplier=-1).then_inc(g_tri, 1)
            tiles(pool, tile)

        def general_vector(dve):
            def expert(k, e):
                dve.wait_ge(g_down, NE * k + e + 1)
                dve.wait_ge(g_sel, SSTEPS * k + 4)
                dve.wait_ge(g_acc, NE * k + e)
                dve.scalar_tensor_tensor(out=gx, in0=ps[:, 2, 0:D], scalar=route[:, 0, bass.ds(e, 1)],
                                         in1=gx, op0=ALU.mult, op1=ALU.add).then_inc(g_acc, 1)

            def tile(k):
                dve.wait_ge(g_x, 16 * k + 16)
                dve.bn_stats(stats[:, 0], gx).then_inc(g_st, 1)
                dve.wait_ge(g_st, k + 1)
                dve.tensor_copy(carrier[:], stats[:, 0, 0:1])
                dve.bn_aggr(mv[:, 0], stats[:, 0]).then_inc(g_mv, 1)
                dve.wait_ge(g_rstd, k + 1)
                dve.tensor_scalar(xn[:, 0], gx, mv[:, 0, 0:1], rstd[:, 0:1],
                                  ALU.subtract, ALU.mult).then_inc(g_xn, 1)
                r, n = lg[:, 0, :], RSTEPS * k
                dve.wait_ge(g_log, k + 1)
                dve.tensor_tensor(r, ps[:, 3, 0:NE], rb_sb[:], ALU.add).then_inc(g_r, 1)
                dve.wait_ge(g_r, n + 1)
                dve.tensor_reduce(lmax[:, 0:1], r, AX.X, ALU.max).then_inc(g_r, 1)
                dve.wait_ge(g_r, n + 2)
                dve.tensor_scalar(r, r, lmax[:, 0:1], None, ALU.subtract).then_inc(g_r, 1)
                dve.wait_ge(g_exp, k + 1)
                dve.tensor_reduce(lsum[:, 0:1], route[:, 0, :], AX.X, ALU.add).then_inc(g_r, 1)
                dve.wait_ge(g_r, n + 4)
                dve.reciprocal(lrec[:, 0:1], lsum[:, 0:1]).then_inc(g_r, 1)
                dve.wait_ge(g_r, n + 5)
                dve.tensor_scalar(route[:, 0, :], route[:, 0, :], lrec[:, 0:1], None, ALU.mult).then_inc(g_r, 1)
                dve.wait_ge(g_r, n + 6)
                dve.tensor_scalar(taken[:, 0, :], route[:, 0, :], 0.0, None, ALU.is_gt).then_inc(g_taken, 1)
                m = SSTEPS * k
                dve.wait_ge(g_cnt, k + 1)
                dve.tensor_tensor(grank, ps[:, 3, NE:2 * NE], carry[:], ALU.add).then_inc(g_sel, 1)
                dve.wait_ge(g_sel, m + 1)
                dve.tensor_scalar(gsel, grank, float(CAPACITY), None, ALU.is_lt).then_inc(g_sel, 1)
                dve.wait_ge(g_sel, m + 2)
                dve.tensor_tensor(route[:, 0, :], route[:, 0, :], gsel, ALU.mult).then_inc(g_sel, 1)
                dve.tensor_tensor(carry[:], ps[:, 3, 2 * NE:3 * NE], carry[:], ALU.add).then_inc(g_sel, 1)
                experts(dve, k, expert)

            tiles(dve, tile)

        def general_scalar(act):
            def expert(k, e):
                act.wait_ge(g_up, NE * k + e + 1)
                act.activation(gh, ps[:, 0:2, :], ACT.Relu).then_inc(g_relu, 1)

            def tile(k):
                act.wait_ge(g_xt, k + 1)
                act.activation(gxT, ps[:, 6, 0:D].rearrange("p (c n) -> p c n", c=KC), ACT.Copy).then_inc(g_xtc, 1)
                act.wait_ge(g_r, RSTEPS * k + 3)
                act.activation(route[:, 0, :], lg[:, 0, :], ACT.Exp).then_inc(g_exp, 1)
                experts(act, k, expert)

            tiles(act, tile)

        def general_tensor(pe):
            def expert(k, e):
                n = NE * k + e
                pe.wait_ge(g_w, 32 * n + 32)
                pe.wait_ge(g_relu, n)
                for i in range(IC):
                    for c in range(KC):
                        mm = pe.matmul(ps[:, i // 4, (i % 4) * P:(i % 4 + 1) * P], gw1[:, c, i * P:(i + 1) * P],
                                       gxT[:, c, :], start=(c == 0), stop=(c == KC - 1))
                mm.then_inc(g_up, 1)
                pe.wait_ge(g_relu, n + 1)
                pe.wait_ge(g_acc, n)
                for i in range(IC):
                    mm = pe.matmul(ps[:, 2, 0:D], gh[:, i * P:(i + 1) * P], gw2[:, i, :],
                                   start=(i == 0), stop=(i == IC - 1))
                mm.then_inc(g_down, 1)

            def tile(k):
                pe.wait_ge(g_xn, k + 1)
                for c in range(KC):
                    mm = pe.transpose(ps[:, 6, c * P:(c + 1) * P], xn[:, 0, c * P:(c + 1) * P], ident[:])
                mm.then_inc(g_xt, 1)
                pe.wait_ge(g_xtc, k + 1)
                pe.wait_ge(g_sel, SSTEPS * k)
                for c in range(KC):
                    mm = pe.matmul(ps[:, 3, 0:NE], gxT[:, c, :], rw_raw[:, c, :], start=(c == 0), stop=(c == KC - 1))
                mm.then_inc(g_log, 1)
                pe.wait_ge(g_taken, k + 1)
                pe.matmul(ps[:, 3, NE:2 * NE], tri, taken[:, 0, :], start=True, stop=True)
                pe.matmul(ps[:, 3, 2 * NE:3 * NE], ones[:], taken[:, 0, :], start=True, stop=True).then_inc(g_cnt, 1)
                experts(pe, k, expert)

            pe.wait_ge(g_tri, 2)
            tiles(pe, tile)

        block = ctx.enter_context(nc.Block())

        @block.sync
        def _(sp):
            for n in range(4):
                sp.dma_start(ew_raw[:, n, :].rearrange("p (c d) -> p c d", d=D),
                             wT[n].rearrange("(c p) d -> p c d", p=P)).then_inc(s_wload[0], 16)
            sp.dma_start(c_raw[:], ctx_g[0]).then_inc(s_ctx, 16)
            sp.dma_start(xa[:], x_g[0]).then_inc(s_x, 16)
            for n in range(3):
                sp.dma_start(prob[:].rearrange("p u n -> p (u n)")[:, n * 2 * D:(n + 1) * 2 * D]
                             .rearrange("p (c d) -> p c d", d=D),
                             wT[4 + n].rearrange("(c p) d -> p c d", p=P)).then_inc(s_wload[1], 16)
            sp.dma_start(mask_raw[:], mask_g[0]).then_inc(s_mask, 16)
            sp.wait_ge(s_wlo, 1)
            sp.dma_start(ew_raw[:].rearrange("p r (a n) -> p (r a n)", a=1).rearrange("p (c n) -> p c n", c=KC),
                         w1T.rearrange("(c p) n -> p c n", p=P)).then_inc(s_wload[0], 16)
            sp.wait_ge(s_wlo, 2)
            sp.dma_start(prob[:].rearrange("p u n -> p (u n)").rearrange("p (i d) -> p i d", d=D),
                         w1.rearrange("(i p) d -> p i d", p=P)).then_inc(s_wload[1], 16)
            def store_k(l, g):
                scratch_store(sp, k_scr[l], key_split(l, g))

            def store_q(l, g):
                scratch_store(sp, q_scr[l], query_split(l, g))

            def load_k(l, g, halves=(0, 1)):
                stack_load(sp, ks, k_scr[l], K_PART, s_ks, key_split(l, g), 2 * g + l, halves)

            def load_q(l, g, halves=(0, 1)):
                stack_load(sp, qs, q_scr[l], Q_PART, s_qs, query_split(l, g), 2 * g + l, halves)

            def body(g, last):
                attention_sync(sp, 0, g)
                store_k(1, g)
                load_k(1, g)
                if not last:
                    sp.wait_ge(s_clo, g + 1)
                    sp.dma_start(c_raw[:], ctx_g[g + 1]).then_inc(s_ctx, 16)
                    sp.wait_ge(s_x1, GB * (g + 1))
                    sp.dma_start(xa[:], x_g[g + 1]).then_inc(s_x, 16)
                    sp.wait_ge(s_mcnt, g + 1)
                    sp.wait_ge(s_mparts, g + 1)
                    sp.dma_start(mask_raw[:], mask_g[g + 1]).then_inc(s_mask, 16)
                if g_is_later(g):
                    expert_sync(sp, g - 1, range(RING, IC))
                if not last:
                    store_k(0, g + 1)
                store_q(1, g)
                load_q(1, g)
                if not last:
                    store_q(0, g + 1)
                attention_sync(sp, 1, g)
                if not last:
                    for hf_ in range(2):
                        load_k(0, g + 1, (hf_,))
                        load_q(0, g + 1, (hf_,))

            store_k(0, 0)
            load_k(0, 0)
            sp.wait_ge(s_whi, 3)
            sp.dma_start(ew_raw[:].rearrange("p r n -> p (r n)").rearrange("p (i d) -> p i d", d=D),
                         w2T.rearrange("(i p) d -> p i d", p=P)).then_inc(s_wload[0], 16)
            store_q(0, 0)
            load_q(0, 0)
            body(0, False)
            with sp.Fori(1, NG - 1) as g:
                body(g, False)
            body(NG - 1, True)
            expert_sync(sp, NG - 1, range(IC))
            general(sp, general_sync)
            sp.wait_ge(s_macc, GB * NE)
            sp.dma_start(out_g[0], acc[:]).then_inc(s_first, 16)
            sp.wait_ge(s_first, 16)
            sp.wait_ge(s_out, 16 * NG)

        @block.gpsimd
        def _(pool):
            pool.memset(ident[:], 0.0).then_inc(s_const, 1)
            pool.memset(identb[:], 0.0).then_inc(s_const, 1)
            pool.wait_ge(s_const, 2)
            for m in (ident, identb):
                pool.affine_select(out=m[:], in_=m[:], compare_op=ALU.not_equal, fill=1.0, base=0,
                                   pattern=[[-1, P]], channel_multiplier=1).then_inc(s_const, 1)
            pool.memset(ones[:], 1.0).then_inc(s_const, 1)
            pool.memset(half[:], -0.5).then_inc(s_const, 1)
            pool.memset(eps[:], EPS).then_inc(s_const, 1)
            pool.memset(far[:], MASKED).then_inc(s_const, 1)
            pool.memset(v_sb[:, :, :, :, HD:HD + 1], 1.0).then_inc(s_const, 1)
            pool.dma_start(bk_sb[:], bk).then_inc(s_small, 16)
            pool.dma_start(bq_sb[:], bq).then_inc(s_small, 16)
            for k in range(2):
                pool.dma_start(bv_sb[:, k, :], bv[k].partition_broadcast(P)).then_inc(s_small, 16)
            pool.dma_start(b1_sb[:], b1).then_inc(s_small, 16)
            pool.dma_start(b2_sb[:], b2.partition_broadcast(P)).then_inc(s_small, 16)
            pool.dma_start(bo_sb[:], bo.partition_broadcast(P)).then_inc(s_small, 16)
            pool.dma_start(rb_sb[:], rb.partition_broadcast(P)).then_inc(s_small, 16)
            pool.dma_start(rw_raw[:], rwT.rearrange("(c p) e -> p c e", p=P)).then_inc(s_small, 16)
            pool.wait_ge(s_small, SMALL)
            pool.wait_ge(s_const, CONSTS)

            ctx_pool(pool, 0)
            ln_pool(pool, ln_index(0, 0))
            rest_pool(pool, 0)
            part2_pool(pool, 0)
            rest_pool(pool, 1)
            part2_pool(pool, 1)
            mask_pool(pool, 0)

            def store(g):
                pool.wait_ge(s_x3, 2 * (g + 1))
                pool.dma_start(out_g[g], xr[:]).then_inc(s_out, 16)

            def body(g, last):
                rest_pool(pool, key_split(1, g))
                part2_pool(pool, key_split(1, g))
                x1_pool(pool, g)
                ln_pool(pool, ln_index(1, g))
                b2_pool(pool, g, ln_index(1, g))
                if not last:
                    ctx_pool(pool, g + 1)
                if g_is_later(g):
                    expert_pool(pool, g - 1, range(EARLY, IC - 1))
                ln_pool(pool, ln_index(2, g))
                if not last:
                    rest_pool(pool, key_split(0, g + 1))
                    part2_pool(pool, key_split(0, g + 1))
                bo_pool(pool, g, ln_index(2, g))
                if not last:
                    ln_pool(pool, ln_index(0, g + 1))
                rest_pool(pool, query_split(1, g))
                part2_pool(pool, query_split(1, g))
                if not last:
                    rest_pool(pool, query_split(0, g + 1))
                    part2_pool(pool, query_split(0, g + 1))
                if g_is_later(g):
                    expert_pool(pool, g - 1, range(IC - 1, IC))
                if not last:
                    mask_pool(pool, g + 1)

            body(0, False)
            pool.wait_ge(s_x3, 2)
            pool.dma_start(acc[:], xr[:]).then_inc(s_out, 16)
            ln_pool(pool, ln_index(3, 0))
            with pool.Fori(1, NG - 1) as g:
                body(g, False)
                store(g)
            body(NG - 1, True)
            store(NG - 1)
            expert_pool(pool, NG - 1, range(IC))
            general(pool, general_pool)

        @block.scalar
        def _(act):
            act.wait_ge(s_small, SMALL)
            act.wait_ge(s_wload[0], 64)
            raw_a = ew_raw[:].rearrange("p r (c d) -> p r c d", d=D)
            raw_b = prob[:].rearrange("p u n -> p (u n)")
            act.activation(w_hi[:, 0:4], raw_a, ACT.Copy).then_inc(s_whi, 1)
            ctx_scalar(act, 0)
            act.wait_ge(s_wload[1], 48)
            act.activation(w_hi[:, 4:7].rearrange("p a c d -> p (a c d)"), raw_b[:, 0:6 * D], ACT.Copy).then_inc(s_whi, 1)
            k_scalar(act, 0, 0)
            part0_scalar(act, 0)
            ln_scalar(act, 0, xT_hi)
            q_scalar(act, 0, 0)
            act.wait_ge(s_wload[0], 80)
            act.activation(sign1[:].rearrange("p c n -> p (c n)"), ew_raw[:].rearrange("p r n -> p (r n)"),
                           ACT.Sign).then_inc(s_whi, 1)
            part0_scalar(act, 1)
            act.wait_ge(s_wload[0], 96)
            act.activation(sign2[:].rearrange("p i d -> p (i d)"), ew_raw[:].rearrange("p r n -> p (r n)"),
                           ACT.Sign).then_inc(s_whi, 1)
            act.activation(rw_hi[:], rw_raw[:], ACT.Copy).then_inc(s_whi, 1)
            act.wait_ge(s_alpha, 1)
            act.activation(raw_b, ew_raw[:].rearrange("p r n -> p (r n)"), ACT.Abs).then_inc(s_abs, 1)

            def table(function):
                act.activation(warm[:], half[:, 0:1], function)

            def body(g, last):
                attention_scalar(act, 0, g)
                table(ACT.Gelu)
                if g_is_later(g):
                    for i in range(EARLY):
                        expert_relu(act, g - 1, i)
                ln_scalar(act, ln_index(1, g), xT_hi)
                if not last:
                    ctx_scalar(act, g + 1)
                ffn_scalar(act, g)
                table(ACT.Exp)
                if not last:
                    k_scalar(act, 0, g + 1)
                    part0_scalar(act, key_split(0, g + 1))
                ln_scalar(act, ln_index(2, g), xT_hi)
                q_scalar(act, 1, g)
                part0_scalar(act, query_split(1, g))
                if not last:
                    ln_scalar(act, ln_index(0, g + 1), xT_hi)
                    q_scalar(act, 0, g + 1)
                if g_is_later(g):
                    act.wait_ge(s_f2, IC * (g + 1))
                    expert_relu(act, g - 1, 3)
                    expert_relu(act, g - 1, 4)
                if not last:
                    part0_scalar(act, query_split(0, g + 1))
                if g_is_later(g):
                    expert_relu(act, g - 1, 5)
                    expert_split_scalar(act, g - 1, IC - 1)
                    expert_relu(act, g - 1, 6)
                    expert_relu(act, g - 1, 7)
                attention_scalar(act, 1, g)
                wo_scalar(act, g)

            body(0, False)
            ln_scalar(act, ln_index(3, 0), xm_hi)
            router_scalar(act)
            with act.Fori(1, NG - 1) as g:
                body(g, False)
            body(NG - 1, True)
            for i in range(RING):
                expert_split_scalar(act, NE - 1, i)
            for i in range(IC):
                expert_relu(act, NE - 1, i)
                if 1 <= i <= RING:
                    expert_split_scalar(act, NE - 1, RING + i - 1)
            general(act, general_scalar)

        @block.vector
        def _(dve):
            dve.memset(ps[:, 6, :], 0.0).then_inc(s_zero, 1)
            dve.memset(ks[SR:SR + 2, :, :], 1.0).then_inc(s_zero, 1)
            dve.wait_ge(s_small, SMALL)
            dve.tensor_scalar(bq_sb[:], bq_sb[:], QK_SCALE, None, ALU.mult).then_inc(s_bq, 1)
            raw_a = ew_raw[:].rearrange("p r (c d) -> p r c d", d=D)
            raw_b = prob[:].rearrange("p u n -> p (u n)")
            dve.wait_ge(s_whi, 1)
            dve.tensor_tensor(w_lo[:, 0:4], raw_a, w_hi[:, 0:4].bitcast(F32), ALU.subtract).then_inc(s_wlo, 1)
            dve.wait_ge(s_whi, 2)
            dve.tensor_tensor(w_lo[:, 4:7].rearrange("p a c d -> p (a c d)"), raw_b[:, 0:6 * D],
                              w_hi[:, 4:7].rearrange("p a c d -> p (a c d)").bitcast(F32),
                              ALU.subtract).then_inc(s_wlo, 1)
            dve.wait_ge(s_x, 16)
            ln_stats(dve, xa, 0)
            part1_vector(dve, 0)
            v_vector(dve, 0, 0, range(GB))
            ln_norm(dve, xa, 0)
            ln_low(dve, 0, xT_hi, xT_lo)
            part1_vector(dve, 1)
            mask_vector(dve, 0)
            dve.wait_ge(s_wload[1], 64)
            dve.tensor_reduce(alpha1[:], raw_b.rearrange("p (i d) -> p i d", d=D), AX.X, ALU.add,
                              apply_absolute_value=True).then_inc(s_alpha, 1)
            dve.wait_ge(s_alpha, 1)
            dve.tensor_scalar(alpha1[:], alpha1[:], 1.0 / D, None, ALU.mult).then_inc(s_alpha, 1)
            dve.wait_ge(s_whi, 5)
            dve.tensor_tensor(rw_lo[:], rw_raw[:], rw_hi[:].bitcast(F32), ALU.subtract).then_inc(s_wlo, 1)
            dve.wait_ge(s_a2mm, 1)
            dve.tensor_scalar(alpha2[:], ps[:, 5, 0:D], 1.0 / NI, None, ALU.mult).then_inc(s_alpha, 1)

            mask_flag_vector(dve, 0)

            def body(g, last, column):
                attention_vector(dve, 0, g)
                ln = ln_index(1, g)
                if g_is_later(g):
                    expert_low(dve, g - 1, 0)
                dve.wait_ge(s_x1, GB * (g + 1))
                ln_stats(dve, xr, ln)
                if g_is_later(g):
                    expert_low(dve, g - 1, 1)
                    expert_low(dve, g - 1, 2)
                ln_norm(dve, xr, ln)
                ln_low(dve, ln, xT_hi, xT_lo)
                ffn_vector(dve, g)
                ln = ln_index(2, g)
                dve.wait_ge(s_x2, 2 * (g + 1))
                ln_stats(dve, xr, ln)
                if not last:
                    v_vector(dve, 0, g + 1, range(0, 2))
                ln_norm(dve, xr, ln)
                if not last:
                    part1_vector(dve, key_split(0, g + 1))
                    v_vector(dve, 0, g + 1, range(2, GB))
                ln_low(dve, ln, xT_hi, xT_lo)
                if not last:
                    ln = ln_index(0, g + 1)
                    dve.wait_ge(s_x, 16 * (g + 2))
                    ln_stats(dve, xa, ln)
                    ln_norm(dve, xa, ln)
                    mask_vector(dve, g + 1)
                part1_vector(dve, query_split(1, g))
                if not last:
                    ln_low(dve, ln, xT_hi, xT_lo)
                if g_is_later(g):
                    expert_low(dve, g - 1, 3)
                    expert_low(dve, g - 1, 4)
                if not last:
                    part1_vector(dve, query_split(0, g + 1))
                attention_vector(dve, 1, g, column)
                if not last:
                    mask_flag_vector(dve, g + 1)
                wo_vector(dve, g)

            body(0, False, None)
            dve.wait_ge(s_x3, 2)
            ln_stats(dve, xr, ln_index(3, 0))
            ln_norm(dve, xr, ln_index(3, 0))
            ln_low(dve, ln_index(3, 0), xm_hi, xm_lo)
            router_vector(dve)
            dve.wait_ge(s_route, 1)
            dve.wait_ge(s_out, 16)
            with dve.Fori(1, NG - 1) as g:
                body(g, False, lambda b: route[:, b, bass.ds(g - 1, 1)])
            body(NG - 1, True, lambda b: route[:, b, NG - 2:NG - 1])
            for i in range(IC):
                expert_low(dve, NE - 1, i)
            expert_add(dve, NG - 1, lambda b: route[:, b, NG - 1:NG])
            general(dve, general_vector)

        @block.tensor
        def _(pe):
            pe.wait_ge(s_const, CONSTS)
            pe.wait_ge(s_zero, 2)
            pe.wait_ge(s_wlo, 2)
            pe.wait_ge(s_bq, 1)
            kv_tensor(pe, 0, 0)
            ln_tensor(pe, 0)
            pe.wait_ge(s_vev, GB)
            q_tensor(pe, 0, 0, 0)
            pe.wait_ge(s_abs, 1)
            raw_b = prob[:].rearrange("p u n -> p (u n)")
            for i in range(IC):
                mm = pe.matmul(ps[:, 5, 0:D], ones[:], raw_b[:, i * D:(i + 1) * D], start=(i == 0), stop=(i == IC - 1))
            mm.then_inc(s_a2mm, 1)
            pe.wait_ge(s_alpha, 3)
            mask_count_tensor(pe, 0)
            pe.wait_ge(s_pev, 2 * KC)
            pe.wait_ge(s_xlo, KC)

            def body(g, last):
                attention_tensor(pe, 0, g)
                pe.wait_ge(s_max, 2 * NU * (2 * g + 1))
                pe.wait_ge(s_exp, NU * (2 * g + 1))
                if g_is_later(g):
                    expert_up(pe, g - 1, 0)
                transposed_out(pe, 2 * g, GB - 1)
                if g_is_later(g):
                    expert_up(pe, g - 1, 1)
                    expert_up(pe, g - 1, 2)
                    for i in range(EARLY):
                        expert_down(pe, g - 1, i)
                pe.wait_ge(s_att, GB * (2 * g + 1))
                ln_tensor(pe, ln_index(1, g))
                if g_is_later(g):
                    pe.wait_ge(s_mhlo, IC * g - IC + EARLY)
                ffn_tensor(pe, g, ln_index(1, g))
                pe.wait_ge(s_gelu, IC * (g + 1))
                if not last:
                    kv_tensor(pe, 0, g + 1)
                ln_tensor(pe, ln_index(2, g))
                if not last:
                    pe.wait_ge(s_vev, GB * (2 * g + 3))
                q_tensor(pe, 1, g, ln_index(2, g))
                if not last:
                    ln_tensor(pe, ln_index(0, g + 1))
                    pe.wait_ge(s_pev, KC * (query_split(1, g) + 1))
                    q_tensor(pe, 0, g + 1, ln_index(0, g + 1))
                attention_tensor(pe, 1, g)
                transposed_out(pe, 2 * g + 1, GB - 1)
                pe.wait_ge(s_exp, NU * (2 * g + 2))
                if not last:
                    mask_count_tensor(pe, g + 1)
                pe.wait_ge(s_att, GB * (2 * g + 2))
                wo_tensor(pe, g)

            body(0, False)
            pe.wait_ge(s_wolo, KC)
            ln_tensor(pe, ln_index(3, 0))
            pe.wait_ge(s_max, 2 * NU * 2)
            router_tensor(pe, ln_index(3, 0))
            router_count_tensor(pe)
            pe.wait_ge(s_carry, 1)
            with pe.Fori(1, NG - 1) as g:
                body(g, False)
            body(NG - 1, True)
            pe.wait_ge(s_x3, 2 * NG)
            expert_up(pe, NE - 1, 0)
            expert_up(pe, NE - 1, 1)
            for i in range(IC):
                if i + 2 < IC:
                    expert_up(pe, NE - 1, i + 2)
                expert_down(pe, NE - 1, i)
            pe.wait_ge(s_macc, GB * NE)
            general(pe, general_tensor)


SMALL = 16 * 9
CONSTS = 9


def kernel(**inputs):
    import numpy as np
    import concourse.bacc as bacc
    from concourse.bass_utils import run_bass_kernel_spmd

    a = {k: np.asarray(v) for k, v in inputs.items()}
    layers = ("L0_xattn_", "L1_xattn_")

    def by_feature(vectors):
        return np.ascontiguousarray(np.stack(vectors).reshape(len(vectors), -1, P).transpose(2, 0, 1))

    arrays = {
        "x": a["x"],
        "ctxT": np.ascontiguousarray(a["ctx_1024"].reshape(B * P, D).T),
        "mask": a["mask_BxSxS2_ff1"],
        "wT": np.stack([a[l + w].T for l in layers for w in ("Wq", "Wk", "Wv")] + [a["L1_xattn_Wo"].T]),
        "bq": by_feature([a[l + "bq"] for l in layers]),
        "bk": by_feature([a[l + "bk"] for l in layers]),
        "bv": np.stack([a[l + "bv"] for l in layers]),
        "bo": a["L1_xattn_bo"],
        "w1": a["L0_ffn_w1"],
        "w1T": np.ascontiguousarray(a["L0_ffn_w1"].T),
        "b1": by_feature([a["L0_ffn_b1"]])[:, 0],
        "w2T": np.ascontiguousarray(a["L0_ffn_w2"].T),
        "b2": a["L0_ffn_b2"],
        "rwT": np.ascontiguousarray(a["L1_ffn_router_w"].T),
        "rb": a["L1_ffn_router_b"],
        "e1": a["L1_ffn_experts_inter"],
        "e2": a["L1_ffn_experts_out"],
    }
    nc = bacc.Bacc("TRN2", target_bir_lowering=False, num_devices=1)
    args = [nc.dram_tensor(n, v.shape, mybir.dt.from_np(v.dtype), kind="ExternalInput").ap()
            for n, v in arrays.items()]
    out = nc.dram_tensor("out", (B, P, D), F32, kind="ExternalOutput").ap()
    build(nc, *args, out)
    r = run_bass_kernel_spmd(nc, [arrays], core_ids=[0])
    return r.results[0]["out"]
```

```python
from contextlib import ExitStack

import concourse.bass as bass
from concourse import mybir

F32 = mybir.dt.float32
F32R = mybir.dt.float32r
BF16 = mybir.dt.bfloat16
I32 = mybir.dt.int32
ALU = mybir.AluOpType
ACT = mybir.ActivationFunctionType
AX = mybir.AxisListType

P = 128
D = 256
KC = D // P
NH = 16
HD = D // NH
NI = 1024
IC = NI // P
NE = 8
B = 32
GB = 4
NG = B // GB
GT = GB * P
UH = 8
NU = GB * NH // UH
NT = 6
SR = NT * HD
EPS = 1e-5
MASKED = 10000.0
CAPACITY = B * P // NE
RING = 4
AHEAD = 6
EARLY = 3
QK_SCALE = float(HD) ** -0.5
Q_PART = (0, 0, 1, 1, 0, 2)
K_PART = (0, 1, 0, 1, 2, 0)
WQ, WK, WV, WO = (0, 3), (1, 4), (2, 5), 6


def build(nc, x, ctxT, mask, wT, bq, bk, bv, bo, w1, w1T, b1, w2T, b2, rwT, rb, e1, e2, out):
    assert GT == CAPACITY == 512
    x_g = x.rearrange("(g b) t d -> g t b d", b=GB)
    out_g = out.rearrange("(g b) t d -> g t b d", b=GB)
    mask_g = mask.rearrange("(g b) q k -> g q b k", b=GB)
    ctx_g = ctxT.rearrange("(c p) (g t) -> g p c t", p=P, t=GT)
    e1_c = e1.rearrange("e (c p) (i n) -> e i p c n", p=P, n=P)
    e2_c = e2.rearrange("e (i p) d -> e i p d", p=P)

    ctx = ExitStack()
    with ctx:
        def sb(name, shape, dt=F32):
            return ctx.enter_context(nc.sbuf_tensor(name, shape, dt))

        def sem(name):
            return ctx.enter_context(nc.semaphore(name))

        w_hi = sb("w_hi", [P, 7, KC, D], F32R)
        w_lo = sb("w_lo", [P, 7, KC, D], F32R)
        sign1 = sb("sign1", [P, KC, NI], F32R)
        sign2 = sb("sign2", [P, IC, D], F32R)
        alpha1 = sb("alpha1", [P, IC])
        alpha2 = sb("alpha2", [P, D])
        bq_sb = sb("bq_sb", [P, 2, KC])
        bk_sb = sb("bk_sb", [P, 2, KC])
        bv_sb = sb("bv_sb", [P, 2, D])
        bo_sb = sb("bo_sb", [P, D])
        b1_sb = sb("b1_sb", [P, IC])
        b2_sb = sb("b2_sb", [P, D])
        rw_raw = sb("rw_raw", [P, KC, NE])
        rw_hi = sb("rw_hi", [P, KC, NE], F32R)
        rw_lo = sb("rw_lo", [P, KC, NE], F32R)
        rb_sb = sb("rb_sb", [P, NE])
        ident = sb("ident", [P, P])
        identb = sb("identb", [P, P], BF16)
        ones = sb("ones", [P, P])
        half = sb("half", [P, GB])
        eps = sb("eps", [P, GB])
        far = sb("far", [P, GB])
        carrier = sb("carrier", [P, 1])
        warm = sb("warm", [P, 1])
        xa = sb("xa", [P, GB, D])
        xr = sb("xr", [P, GB, D])
        xn = sb("xn", [P, GB, D])
        stats = sb("stats", [P, GB, 6])
        mv = sb("mv", [P, GB, 2])
        vpe = sb("vpe", [P, GB])
        rstd = sb("rstd", [P, GB])
        xT_hi = sb("xT_hi", [P, KC, GT], F32R)
        xT_lo = sb("xT_lo", [P, KC, GT], F32R)
        xm_hi = sb("xm_hi", [P, KC, GT], F32R)
        xm_lo = sb("xm_lo", [P, KC, GT], F32R)
        c_raw = sb("c_raw", [P, KC, GT])
        c_hi = sb("c_hi", [P, KC, GT], F32R)
        c_lo = sb("c_lo", [P, KC, GT], F32R)
        pf = sb("pf", [P, KC, GT])
        parts = sb("parts", [P, 3, KC, GT], BF16)
        v_sb = sb("v_sb", [P, 2, GB, NH, HD + 1])
        qs = sb("qs", [SR + 2, NH, GT], BF16)
        ks = sb("ks", [SR + 2, NH, GT], BF16)
        mask_raw = sb("mask_raw", [P, GB, P])
        mbias = sb("mbias", [P, GB, P])
        mparts = sb("mparts", [P, 3, GB, P], BF16)
        mdiff = sb("mdiff", [P, GB, P], BF16)
        mcnt = sb("mcnt", [P, 1])
        mflag = sb("mflag", [1, 1], I32)
        mneg = sb("mneg", [P, 2, NH])
        mpack = sb("mpack", [P, 2, 2 * NH], BF16)
        mrow = sb("mrow", [2 * NH, 2, P], BF16)
        prob = sb("prob", [P, 2, UH * P])
        pvs = sb("pvs", [P, 2, GB * P])
        rsum = sb("rsum", [P, 2, NH])
        att = sb("att", [P, GB, D])
        hf = pf
        h_hi = sb("h_hi", [P, 3, GT], F32R)
        h_lo = sb("h_lo", [P, 3, GT], F32R)
        ew_raw = sb("ew_raw", [P, RING, 2 * D])
        ew_hi = sb("ew_hi", [P, RING, 2 * D], F32R)
        ew_lo = sb("ew_lo", [P, RING, 2 * D], F32R)
        acc = sb("acc", [P, GB, D])
        lg = sb("lg", [P, GB, NE])
        lmax = sb("lmax", [P, GB])
        lsum = sb("lsum", [P, GB])
        lrec = sb("lrec", [P, GB])
        route = sb("route", [P, GB, NE])
        taken = sb("taken", [P, GB, NE])
        carry = sb("carry", [P, NE])
        filled = sb("filled", [1, 1], I32)

        ps = ctx.enter_context(nc.psum_tensor("ps", [P, 8, 512], F32))
        ps_bf = ps[:, 7, :].bitcast(BF16)

        k_scr = [nc.dram_tensor(f"k_scr{l}", [3, D, GT], BF16).ap() for l in range(2)]
        q_scr = [nc.dram_tensor(f"q_scr{l}", [3, D, GT], BF16).ap() for l in range(2)]

        s_wload = [sem("s_wload_a"), sem("s_wload_b")]
        s_small = sem("s_small_loaded")
        s_const = sem("s_constants")
        s_ones = sem("s_rows_of_ones")
        s_w1 = sem("s_w1_loaded")
        s_whi = sem("s_weights_hi")
        s_wlo = sem("s_weights_lo")
        s_abs = sem("s_abs_w2")
        s_a2mm = sem("s_alpha2_product")
        s_alpha = sem("s_alphas")
        s_bq = sem("s_scaled_bq")
        s_x = sem("s_x_loaded")
        s_ctx = sem("s_ctx_loaded")
        s_mask = sem("s_mask_loaded")
        s_chi = sem("s_ctx_hi")
        s_clo = sem("s_ctx_lo")
        s_kvmm = sem("s_kv_products")
        s_vev = sem("s_v_evacuated")
        s_qmm = sem("s_q_products")
        s_pev = sem("s_projection_evacuated")
        s_ph = sem("s_part0")
        s_pr = sem("s_rest0")
        s_pm = sem("s_part1")
        s_pl = sem("s_part2")
        s_prq = sem("s_queries_rest0")
        s_plq = sem("s_queries_part2")
        s_scr = sem("s_parts_in_dram")
        s_ks = [sem("s_keys_stacked_a"), sem("s_keys_stacked_b")]
        s_qs = [sem("s_queries_stacked_a"), sem("s_queries_stacked_b")]
        s_mcnt = sem("s_mask_counted")
        s_mflmm = sem("s_mask_count_summed")
        s_mfl0 = sem("s_first_mask_flag")
        s_mfl = sem("s_mask_flag")
        s_mb = sem("s_mask_bias_steps")
        s_mparts = sem("s_mask_parts")
        s_smm = sem("s_scores_for_max")
        s_max = sem("s_row_max")
        s_mhi = sem("s_max_hi")
        s_mpk = sem("s_max_packed")
        s_mtmm = sem("s_max_transposed")
        s_mtc = sem("s_max_rows_copied")
        s_mrow = [sem("s_max_row_placed_a"), sem("s_max_row_placed_b")]
        s_stmm = sem("s_scores_shifted")
        s_exp = sem("s_exp")
        s_pv = sem("s_pv")
        s_pvc = sem("s_pv_copied")
        s_otmm = sem("s_att_transposed")
        s_rs = sem("s_row_sum_inverted")
        s_att = sem("s_att_normalised")
        s_x1 = sem("s_x1")
        s_st = sem("s_ln_stats")
        s_mv = sem("s_ln_moments")
        s_vpe = sem("s_ln_var_eps")
        s_rstd = sem("s_ln_rstd")
        s_xn = sem("s_ln_out")
        s_xtmm = sem("s_xT_products")
        s_xhi = sem("s_xT_hi")
        s_xlo = sem("s_xT_lo")
        s_f1 = sem("s_ffn_up")
        s_gelu = sem("s_gelu")
        s_fhi = sem("s_ffn_h_hi")
        s_flo = sem("s_ffn_h_lo")
        s_f2 = sem("s_ffn_down")
        s_fb2 = sem("s_x1_plus_b2")
        s_fy = sem("s_ffn_scaled")
        s_x2 = sem("s_x2")
        s_x2b = sem("s_x2_plus_bo")
        s_wohi = sem("s_attT_hi")
        s_wolo = sem("s_attT_lo")
        s_wotr = sem("s_attT_products")
        s_womm = sem("s_wo_products")
        s_x3 = sem("s_x3")
        s_out = sem("s_out_stored")
        s_first = sem("s_first_group_stored")
        s_rmm = sem("s_router_products")
        s_rl = sem("s_router_steps")
        s_rex = sem("s_router_exp")
        s_route = sem("s_routing_weights")
        s_ew = [sem(f"s_expert_chunk{r}_loaded") for r in range(RING)]
        s_ewhi = sem("s_expert_chunk_hi")
        s_ewlo = sem("s_expert_chunk_lo")
        s_m1 = sem("s_moe_up")
        s_mhhi = sem("s_moe_h_hi")
        s_mhlo = sem("s_moe_h_lo")
        s_m2 = sem("s_moe_down")
        s_macc = sem("s_moe_added")
        s_taken = sem("s_taken")
        s_count = sem("s_taken_counted")
        s_carry = sem("s_carry_started")
        s_filled = sem("s_filled")
        g_tri = sem("g_triangle")
        g_x = sem("g_x_loaded")
        g_st = sem("g_ln_stats")
        g_mv = sem("g_ln_moments")
        g_vpe = sem("g_ln_var_eps")
        g_rstd = sem("g_ln_rstd")
        g_xn = sem("g_ln_out")
        g_xt = sem("g_xT_products")
        g_xtc = sem("g_xT_copied")
        g_log = sem("g_router_products")
        g_r = sem("g_router_steps")
        g_exp = sem("g_router_exp")
        g_taken = sem("g_taken")
        g_cnt = sem("g_taken_counted")
        g_sel = sem("g_selection_steps")
        g_w = sem("g_expert_loaded")
        g_up = sem("g_up")
        g_relu = sem("g_relu")
        g_down = sem("g_down")
        g_acc = sem("g_added")
        g_st_out = sem("g_stored")

        def count(value):
            return max(value, 0) if isinstance(value, int) else value

        def ln_index(stage, g):
            if stage == 3:
                return 4
            late = 1 if not isinstance(g, int) or g > 1 or (g == 1 and stage > 0) else 0
            return 3 * g + stage + late

        def g_is_later(g):
            return not isinstance(g, int) or g > 0

        def g_routes(g):
            return isinstance(g, int) and g == 1

        def key_split(l, g):
            if l == 1:
                return 4 * g + 2
            return 0 if isinstance(g, int) and g == 0 else 4 * g - 1

        def pool_splits(g):
            return 3 * g + 2

        def last_query_split(g):
            last = isinstance(g, int) and g == NG - 1
            return query_split(1, g) if last else query_split(0, g + 1)

        def query_split(l, g):
            if l == 0:
                return 4 * g + 1
            return 4 * g + 3 if isinstance(g, int) and g == NG - 1 else 4 * g + 4

        def ln_stats(dve, src, t):
            for b in range(GB):
                dve.bn_stats(stats[:, b], src[:, b]).then_inc(s_st, 1)
            dve.wait_ge(s_st, GB * (t + 1))
            dve.tensor_copy(carrier[:], stats[:, GB - 1, 0:1])
            for b in range(GB):
                dve.bn_aggr(mv[:, b], stats[:, b]).then_inc(s_mv, 1)

        def ln_norm(dve, src, t):
            dve.wait_ge(s_rstd, t + 1)
            dve.wait_ge(s_xtmm, KC * t)
            for b in range(GB):
                dve.tensor_scalar(xn[:, b], src[:, b], mv[:, b, 0:1], rstd[:, b:b + 1],
                                  ALU.subtract, ALU.mult).then_inc(s_xn, 1)

        def ln_low(dve, t, hi, lo):
            for c in range(KC):
                dve.wait_ge(s_xhi, KC * t + c + 1)
                dve.tensor_tensor(lo[:, c, :], ps[:, 6 + c, :], hi[:, c, :].bitcast(F32),
                                  ALU.subtract).then_inc(s_xlo, 1)

        def ln_pool(pool, t):
            pool.wait_ge(s_mv, GB * (t + 1))
            pool.tensor_tensor(vpe[:], mv[:, :, 1], eps[:], ALU.add).then_inc(s_vpe, 1)
            pool.wait_ge(s_vpe, t + 1)
            pool.tensor_tensor(rstd[:], vpe[:], half[:], ALU.pow).then_inc(s_rstd, 1)

        def ln_tensor(pe, t):
            for c in range(KC):
                for b in range(GB):
                    if c == 0:
                        pe.wait_ge(s_xn, GB * t + b + 1)
                    mm = pe.transpose(ps[:, 6 + c, b * P:(b + 1) * P], xn[:, b, c * P:(c + 1) * P], ident[:])
                mm.then_inc(s_xtmm, 1)

        def ln_scalar(act, t, hi):
            for c in range(KC):
                act.wait_ge(s_xtmm, KC * t + c + 1)
                act.activation(hi[:, c, :], ps[:, 6 + c, :], ACT.Copy).then_inc(s_xhi, 1)

        def split_products(pe, dst, l_hi, l_lo, r_hi, r_lo, n):
            terms = [(l, r) for c in range(n) for l, r in ((l_hi, r_hi), (l_hi, r_lo), (l_lo, r_hi))
                     for l, r in ((l(c), r(c)),)]
            for k, (l, r) in enumerate(terms):
                mm = pe.matmul(dst, l, r, start=(k == 0), stop=(k == len(terms) - 1))
            return mm

        def kv_tensor(pe, l, g):
            v = 2 * g + l
            p = key_split(l, g)
            for n in range(KC):
                key_products(pe, l, g, n, n)
            for b in range(GB):
                if b < 2:
                    pe.wait_ge(s_pev, KC * p + b + 1)
                else:
                    pe.wait_ge(s_vev, GB * v + b - 1)
                value_products(pe, l, g, b, ps[:, b % 2, 0:D])

        def key_products(pe, l, g, n, bank):
            pe.wait_ge(s_clo, g + 1)
            cols = slice(n * P, (n + 1) * P)
            split_products(pe, ps[:, bank, :],
                           lambda c: w_hi[:, WK[l], c, cols], lambda c: w_lo[:, WK[l], c, cols],
                           lambda c: c_hi[:, c, :], lambda c: c_lo[:, c, :], KC).then_inc(s_kvmm, 1)

        def value_products(pe, l, g, b, dst):
            rows = slice(b * P, (b + 1) * P)
            split_products(pe, dst,
                           lambda c: c_hi[:, c, rows], lambda c: c_lo[:, c, rows],
                           lambda c: w_hi[:, WV[l], c, :], lambda c: w_lo[:, WV[l], c, :],
                           KC).then_inc(s_kvmm, 1)

        def value_place(l, b):
            return ps[:, b % 2, 0:D] if l == 0 else ps[:, 4 + b // 2, (b % 2) * D:(b % 2 + 1) * D]

        def ctx_scalar(act, g):
            act.wait_ge(s_ctx, 16 * (g + 1))
            act.wait_ge(s_kvmm, 6 * 2 * g)
            act.activation(c_hi[:], c_raw[:], ACT.Copy).then_inc(s_chi, 1)

        def ctx_pool(pool, g):
            pool.wait_ge(s_chi, g + 1)
            pool.tensor_tensor(c_lo[:], c_raw[:], c_hi[:].bitcast(F32), ALU.subtract).then_inc(s_clo, 1)

        def k_scalar(act, l, g):
            p = key_split(l, g)
            first_bank = 0 if l == 0 else 2
            if l == 0:
                act.wait_ge(s_flo, count(IC * g))
            for n in range(KC):
                act.wait_ge(s_kvmm, 6 * (2 * g + l) + n + 1)
                act.wait_ge(s_pl, count(pool_splits(g) - 2) if l == 0 else pool_splits(g))
                act.activation(pf[:, n, :], ps[:, first_bank + n, :], ACT.Identity,
                               bias=bk_sb[:, l, n:n + 1]).then_inc(s_pev, 1)

        def q_scalar(act, l, g):
            p = query_split(l, g)
            for n in range(KC):
                act.wait_ge(s_qmm, KC * (2 * g + l) + n + 1)
                if l == 1:
                    last = isinstance(g, int) and g == NG - 1
                    act.wait_ge(s_pl, pool_splits(g) + (1 if last else 2))
                elif not (isinstance(g, int) and g == 0):
                    act.wait_ge(s_plq, g)
                else:
                    act.wait_ge(s_pl, 1)
                if l == 1:
                    act.wait_ge(s_flo, IC * (g + 1))
                act.activation(pf[:, n, :], ps[:, n, :], ACT.Identity,
                               bias=bq_sb[:, l, n:n + 1], scale=QK_SCALE).then_inc(s_pev, 1)

        def q_tensor(pe, l, g, t):
            for c in range(KC):
                pe.wait_ge(s_xhi, KC * t + c + 1)
                for n in range(KC):
                    for w in (w_hi, w_lo):
                        pe.matmul(ps[:, n, :], w[:, WQ[l], c, n * P:(n + 1) * P], xT_hi[:, c, :],
                                  start=(c == 0 and w is w_hi), stop=False)
            pe.wait_ge(s_xlo, KC * t + KC)
            for n in range(KC):
                for c in range(KC):
                    mm = pe.matmul(ps[:, n, :], w_hi[:, WQ[l], c, n * P:(n + 1) * P], xT_lo[:, c, :],
                                   start=False, stop=(c == KC - 1))
                mm.then_inc(s_qmm, 1)

        def part0_scalar(act, p):
            act.wait_ge(s_pev, KC * (p + 1))
            act.wait_ge(s_scr, 48 * p)
            act.activation(parts[:, 0], pf[:], ACT.Copy).then_inc(s_ph, 1)

        def part1_vector(dve, p, n):
            dve.wait_ge(s_pr, n + 1)
            dve.tensor_copy(parts[:, 1], pf[:]).then_inc(s_pm, 1)

        def query_split_vector(dve, g):
            p = query_split(1, g)
            dve.wait_ge(s_ph, p + 1)
            dve.tensor_tensor(pf[:], pf[:], parts[:, 0], ALU.subtract).then_inc(s_prq, 1)
            dve.wait_ge(s_prq, g + 1)
            dve.tensor_copy(parts[:, 1], pf[:]).then_inc(s_pm, 1)
            dve.wait_ge(s_pm, p + 1)
            dve.tensor_tensor(parts[:, 2], pf[:], parts[:, 1], ALU.subtract).then_inc(s_plq, 1)

        def rest_pool(pool, p):
            pool.wait_ge(s_ph, p + 1)
            pool.tensor_tensor(pf[:], pf[:], parts[:, 0], ALU.subtract).then_inc(s_pr, 1)

        def part2_pool(pool, p):
            pool.wait_ge(s_pm, p + 1)
            pool.tensor_tensor(parts[:, 2], pf[:], parts[:, 1], ALU.subtract).then_inc(s_pl, 1)

        def v_vector(dve, l, g, batches):
            v = 2 * g + l
            for b in batches:
                dve.wait_ge(s_kvmm, 6 * v + KC + b + 1)
                if b == 0:
                    dve.wait_ge(s_pv, count(NU * (v - 1)))
                dve.tensor_tensor(v_sb[:, l, b, :, 0:HD],
                                  value_place(l, b).rearrange("p (h d) -> p h d", d=HD),
                                  bv_sb[:, l, :].rearrange("p (h d) -> p h d", d=HD),
                                  ALU.add).then_inc(s_vev, 1)

        def v_pair_vector(dve, g, b):
            v = 2 * g + 1
            dve.wait_ge(s_kvmm, 6 * v + KC + b + 2)
            dve.wait_ge(s_pv, count(NU * (v - 1)))
            dve.tensor_tensor(v_sb[:, 1, b:b + 2, :, 0:HD],
                              ps[:, 4 + b // 2, :].rearrange("p (b h d) -> p b h d", h=NH, d=HD),
                              bv_sb[:, 1, :].rearrange("p (h d) -> p h d", d=HD).unsqueeze(1)
                              .broadcast_to([P, 2, NH, HD]),
                              ALU.add).then_inc(s_vev, 2)

        def scratch_store(sp, scr, p, split, splits):
            for t, (ready, n) in enumerate(((s_ph, p + 1), (s_pm, p + 1), (split, splits))):
                sp.wait_ge(ready, n)
                sp.dma_start(scr[t].rearrange("(c p) n -> p c n", p=P), parts[:, t]).then_inc(s_scr, 16)

        def stack_load(sp, dst, scr, part_of, s, p, v, halves=(0, 1)):
            for hf_ in halves:
                if hf_ == 0:
                    sp.wait_ge(s_scr, 48 * (p + 1))
                cols = slice(hf_ * GT // 2, (hf_ + 1) * GT // 2)
                sp.wait_ge(s_stmm, count(NU * (v - 1) + NU // 2 * (hf_ + 1)))
                for j, part in enumerate(part_of):
                    sp.dma_start(dst[j * HD:(j + 1) * HD, :, cols],
                                 scr[part].rearrange("(h d) n -> d h n", d=HD)[:, :, cols]).then_inc(s[hf_], 16)

        def max_scores(pe, v, b, u, masked):
            j = NU * v + 2 * b + u
            if u == 0:
                pe.wait_ge(s_qs[b // 2], 16 * NT * (v + 1))
                pe.wait_ge(s_ks[b // 2], 16 * NT * (v + 1))
            rows = slice(b * P, (b + 1) * P)
            for n in range(UH):
                h = UH * u + n
                if n % 4 == 0:
                    pe.wait_ge(s_max, count(2 * j + n // 4 - 1))
                mm = pe.matmul(ps[:, n // 4, (n % 4) * P:(n % 4 + 1) * P], qs[0:SR, h, rows], ks[0:SR, h, rows],
                               start=(n % 4 == 0), stop=True, skip_group_check=True)
                if n % 4 == 3:
                    if masked:
                        mm = mask_max(pe, b, n // 4)
                    mm.then_inc(s_smm, 1)

        def mask_max(pe, b, n):
            for part in range(3):
                mm = pe.matmul(ps[:, n, :].rearrange("p (h k) -> p h k", k=P), identb[:],
                               mparts[:, part, b, :].unsqueeze(1).broadcast_to([P, 4, P]),
                               start=False, stop=True, skip_group_check=True)
            return mm

        def mask_shifted(pe, b, n):
            for part in range(3):
                mm = pe.matmul(ps[:, n, :].rearrange("p (h k) -> p h k", k=P), mparts[:, part, b, :],
                               identb[:].unsqueeze(1).broadcast_to([P, 4, P]),
                               start=False, stop=True, skip_group_check=True)
            return mm

        def attention_tensor(pe, l, g):
            v = 2 * g + l
            if l == 1:
                attention_products(pe, l, g, False)
                return
            pe.wait_ge(s_const, CONSTS)
            if isinstance(g, int) and g == 0:
                pe.wait_ge(s_mfl0, 1)
            else:
                pe.wait_ge(s_mfl, g)
            flag = pe.value_load(mflag[0:1, 0:1], min_val=0, max_val=P * GT)
            with pe.If(flag > 0):
                attention_products(pe, l, g, True)
                pe.nop()
            with pe.Else():
                attention_products(pe, l, g, False)
                pe.nop()

        def mask_count_tensor(pe, g):
            pe.wait_ge(s_mcnt, g + 1)
            pe.matmul(ps[0:1, 1, 0:1], mcnt[:], ones[:, 0:1], start=True, stop=True).then_inc(s_mflmm, 1)

        def transposed_out(pe, v, b):
            pe.wait_ge(s_pvc, GB * v + b + 1)
            pe.wait_ge(s_mtc, GB * v + min(b + 1 + AHEAD // 2, GB))
            pe.wait_ge(s_att, GB * v + b)
            for n in range(4):
                mm = pe.transpose(ps[:, 7, n * P:(n + 1) * P], pvs[:, b % 2, n * P:(n + 1) * P], ident[:])
            mm.then_inc(s_otmm, 1)

        def attention_products(pe, l, g, masked):
            v = 2 * g + l
            if masked:
                pe.wait_ge(s_mparts, g + 1)

            def scores_for_max(n):
                max_scores(pe, v, n // 2, n % 2, masked)

            def transposed_max(b):
                pe.wait_ge(s_mpk, GB * v + b + 1)
                pe.wait_ge(s_mtc, GB * v + b)
                if b == 0 and l == 0:
                    pe.wait_ge(s_wolo, KC * g)
                if b > AHEAD // 2:
                    pe.wait_ge(s_att, GB * v + b - AHEAD // 2)
                pe.transpose(ps_bf[0:2 * NH, 0:P], mpack[:, b % 2, :], identb[:]).then_inc(s_mtmm, 1)

            def shifted_scores(n):
                b, u = divmod(n, 2)
                j = NU * v + n
                pe.wait_ge(s_mrow[b % 2], 32 * (2 * v + b // 2 + 1))
                pe.wait_ge(s_exp, count(j - 1))
                if n == 0 and l == 0:
                    pe.wait_ge(s_pev, KC * (key_split(1, g) + 1))
                elif n == 1 and l == 0:
                    pe.wait_ge(s_vev, GB * (v + 2))
                elif n == 0 and g_is_later(g):
                    pe.wait_ge(s_mhlo, IC * g)
                elif n == 0:
                    pe.wait_ge(s_fy, 2)
                elif n == 1 and l == 1:
                    pe.wait_ge(s_macc, GB * g)
                rows = slice(b * P, (b + 1) * P)
                for k in range(UH):
                    h = UH * u + k
                    mm = pe.matmul(ps[:, 2 + 2 * u + k // 4, (k % 4) * P:(k % 4 + 1) * P],
                                   ks[:, h, rows], qs[:, h, rows],
                                   start=(k % 4 == 0), stop=True, skip_group_check=True)
                if masked:
                    for bank in (2 + 2 * u, 3 + 2 * u):
                        mm = mask_shifted(pe, b, bank)
                mm.then_inc(s_stmm, 1)

            def product_with_values(n):
                b, u = divmod(n, 2)
                pe.wait_ge(s_exp, NU * v + n + 1)
                if u == 0:
                    pe.wait_ge(s_pvc, GB * v + b)
                for k in range(UH):
                    h = UH * u + k
                    q = 32 * (h % 4)
                    mm = pe.matmul(ps[q:q + HD + 1, 6, (h // 4) * P:(h // 4 + 1) * P],
                                   v_sb[:, l, b, h, :], prob[:, u, k * P:(k + 1) * P], start=True, stop=True)
                mm.then_inc(s_pv, 1)

            if l == 0:
                scores_for_max(0)
                pe.wait_ge(s_x3, 2 * g)
                value_products(pe, 1, g, 0, value_place(1, 0))
                scores_for_max(1)
                value_products(pe, 1, g, 1, value_place(1, 1))
                scores_for_max(2)
                transposed_max(0)
                scores_for_max(3)
                value_products(pe, 1, g, 2, value_place(1, 2))
                scores_for_max(4)
                transposed_max(1)
                shifted_scores(0)
                scores_for_max(5)
                value_products(pe, 1, g, 3, value_place(1, 3))
                transposed_max(2)
            else:
                if g_is_later(g):
                    expert_down(pe, g - 1, 3)
                    expert_up(pe, g - 1, 6)
                    expert_down(pe, g - 1, 4)
                pe.wait_ge(s_pev, KC * (last_query_split(g) + 1))
                if g_is_later(g):
                    expert_up(pe, g - 1, 7)
                scores_for_max(0)
                scores_for_max(1)
                if g_is_later(g):
                    expert_down(pe, g - 1, 5)
                scores_for_max(2)
                transposed_max(0)
                if g_is_later(g):
                    expert_down(pe, g - 1, 6)
                scores_for_max(3)
                scores_for_max(4)
                if g_is_later(g):
                    expert_down(pe, g - 1, 7)
                transposed_max(1)
                scores_for_max(5)
                shifted_scores(0)
                transposed_max(2)
            for n in range(NU):
                if n + AHEAD < NU:
                    scores_for_max(n + AHEAD)
                if n + 1 < NU:
                    shifted_scores(n + 1)
                product_with_values(n)
                if n % 2 and n + AHEAD < NU:
                    transposed_max((n + AHEAD) // 2)
                if n % 2 == 0 and n > 0:
                    transposed_out(pe, v, n // 2 - 1)

        def attention_vector(dve, l, g, column=None):
            v = 2 * g + l

            def row_max(n):
                b, u = divmod(n, 2)
                for a in range(2):
                    dve.wait_ge(s_smm, 2 * (NU * v + n) + a + 1)
                    dve.tensor_reduce(mneg[:, b % 2, u * UH + 4 * a:u * UH + 4 * (a + 1)],
                                      ps[:, a, :].rearrange("p (h k) -> p h k", k=P),
                                      AX.X, ALU.max, negate=True).then_inc(s_max, 1)
                if u == 1:
                    dve.wait_ge(s_max, 2 * (NU * v + n + 1))
                    dve.wait_ge(s_mtmm, count(GB * v + b - 1))
                    dve.tensor_copy(mpack[:, b % 2, 0:NH], mneg[:, b % 2]).then_inc(s_mhi, 1)
                    dve.wait_ge(s_mhi, GB * v + b + 1)
                    dve.tensor_tensor(mpack[:, b % 2, NH:2 * NH], mneg[:, b % 2],
                                      mpack[:, b % 2, 0:NH], ALU.subtract).then_inc(s_mpk, 1)

            def out_copy(b):
                dve.wait_ge(s_pv, NU * v + 2 * b + 2)
                dve.wait_ge(s_otmm, count(GB * v + b - 1))
                dve.tensor_copy(pvs[:, b % 2, :], ps[:, 6, :]).then_inc(s_pvc, 1)

            def normalise(b):
                dve.wait_ge(s_otmm, GB * v + b + 1)
                o = ps[:, 7, :].rearrange("p (h d) -> p h d", d=32)
                dve.reciprocal(rsum[:, b % 2, :], o[:, :, HD]).then_inc(s_rs, 1)
                dve.wait_ge(s_rs, GB * v + b + 1)
                if b == 0:
                    if l == 0:
                        dve.wait_ge(s_wotr, KC * g)
                    else:
                        dve.wait_ge(s_x1, GB * (g + 1))
                dve.tensor_tensor(att[:, b].rearrange("p (h d) -> p h d", d=HD), o[:, :, 0:HD],
                                  rsum[:, b % 2, :].unsqueeze(2).broadcast_to([P, NH, HD]),
                                  ALU.mult).then_inc(s_att, 1)

            if l == 0:
                for n in range(AHEAD):
                    if n == AHEAD - 2:
                        v_pair_vector(dve, g, 0)
                    row_max(n)
                v_pair_vector(dve, g, 2)
                part1_vector(dve, key_split(1, g), pool_splits(g))
            else:
                later = g_is_later(g)
                if later:
                    expert_low(dve, g - 1, 6)
                for n in range(AHEAD):
                    row_max(n)
                    if n == 0 and later:
                        expert_low(dve, g - 1, 7)
                    if n == 1 and not (isinstance(g, int) and g == NG - 1):
                        part1_vector(dve, query_split(0, g + 1), pool_splits(g) + 2)
                if later:
                    expert_add(dve, g - 1, column)
            for n in range(NU):
                if n + AHEAD < NU:
                    row_max(n + AHEAD)
                if n == 1 and l == 0 and g_routes(g):
                    dve.wait_ge(s_out, 16)
                    ln_stats(dve, acc, ln_index(3, 0))
                if n == 3 and l == 0 and g_routes(g):
                    ln_norm(dve, acc, ln_index(3, 0))
                if n % 2:
                    out_copy(n // 2)
                elif n > 0:
                    normalise(n // 2 - 1)
            normalise(GB - 1)

        def attention_scalar(act, l, g):
            v = 2 * g + l

            def max_copy(b):
                act.wait_ge(s_mtmm, GB * v + b + 1)
                act.wait_ge(s_mrow[b % 2], 32 * (2 * v + b // 2))
                act.activation(mrow[:, b % 2, :], ps_bf[0:2 * NH, 0:P], ACT.Copy).then_inc(s_mtc, 1)

            def exponential(n):
                j = NU * v + n
                act.wait_ge(s_stmm, j + 1)
                act.wait_ge(s_pv, count(j - 1))
                u = n % 2
                act.activation(prob[:, u, :], ps[:, 2 + 2 * u:4 + 2 * u, :], ACT.Exp).then_inc(s_exp, 1)

            if l == 0:
                part0_scalar(act, key_split(1, g))
            max_copy(0)
            max_copy(1)
            exponential(0)
            max_copy(2)
            for n in range(NU):
                if n + 1 < NU:
                    exponential(n + 1)
                if l == 0 and g_is_later(g) and 0 <= n - 3 < EARLY:
                    expert_split_scalar(act, g - 1, n - 3)
                if l == 1 and isinstance(g, int) and g == NG - 1 and 0 <= n - 3 < RING:
                    expert_split_scalar(act, g, n - 3)
                if n % 2 and n + AHEAD < NU:
                    max_copy((n + AHEAD) // 2)

        def store_q(sp, l, g):
            if l == 1:
                scratch_store(sp, q_scr[l], query_split(l, g), s_plq, g + 1)
            else:
                scratch_store(sp, q_scr[l], query_split(l, g), s_pl, pool_splits(g))

        def attention_sync(sp, l, g):
            v = 2 * g + l
            for b in range(GB):
                sp.wait_ge(s_mtc, GB * v + b + 1)
                for k in range(2):
                    sp.dma_start(qs[SR + k:SR + k + 1, :, b * P:(b + 1) * P],
                                 mrow[k * NH:(k + 1) * NH, b % 2, :]).then_inc(s_mrow[b % 2], 16)
                if l == 0 and b == AHEAD // 2 - 1 and g_is_later(g):
                    expert_sync(sp, g - 1, range(RING))
                if l == 1 and b == AHEAD // 2 - 1 and not (isinstance(g, int) and g == NG - 1):
                    store_q(sp, 0, g + 1)
                if l == 1 and b == AHEAD // 2 - 1 and isinstance(g, int) and g == NG - 1:
                    sp.wait_ge(s_ewlo, IC * g)
                    expert_sync(sp, g, range(RING))

        def x1_pool(pool, g):
            pool.wait_ge(s_out, 16 * g)
            for b in range(GB):
                if g_is_later(g) and b < EARLY:
                    expert_pool(pool, g - 1, range(b, b + 1))
                pool.wait_ge(s_att, GB * 2 * g + b + 1)
                pool.tensor_tensor(xr[:, b], xa[:, b], att[:, b], ALU.add).then_inc(s_x1, 1)

        def mask_vector(dve, g):
            dve.wait_ge(s_mask, 16 * (g + 1))
            dve.wait_ge(s_mflmm, g)
            dve.tensor_scalar(mdiff[:], mask_raw[:], 1.0, 0.0, ALU.not_equal, ALU.add,
                              accum_out=mcnt[:]).then_inc(s_mcnt, 1)

        def mask_flag_vector(dve, g):
            dve.wait_ge(s_mflmm, g + 1)
            first = isinstance(g, int) and g == 0
            dve.tensor_copy(mflag[:], ps[0:1, 1, 0:1]).then_inc(s_mfl0 if first else s_mfl, 1)

        def mask_pool(pool, g):
            n = 5 * g
            one = ones[:].unsqueeze(1).broadcast_to([P, GB, P])
            pool.wait_ge(s_mask, 16 * (g + 1))
            pool.wait_ge(s_stmm, count(NU * 2 * g - NU))
            pool.tensor_tensor(mbias[:], mask_raw[:], one, ALU.subtract).then_inc(s_mb, 1)
            pool.wait_ge(s_mb, n + 1)
            pool.tensor_tensor(mbias[:], mbias[:], far[:].unsqueeze(2).broadcast_to([P, GB, P]),
                               ALU.mult).then_inc(s_mb, 1)
            pool.wait_ge(s_mb, n + 2)
            pool.tensor_tensor(mparts[:, 0], mbias[:], one, ALU.mult).then_inc(s_mb, 1)
            pool.wait_ge(s_mb, n + 3)
            pool.tensor_tensor(mbias[:], mbias[:], mparts[:, 0], ALU.subtract).then_inc(s_mb, 1)
            pool.wait_ge(s_mb, n + 4)
            pool.tensor_tensor(mparts[:, 1], mbias[:], one, ALU.mult).then_inc(s_mb, 1)
            pool.wait_ge(s_mb, n + 5)
            pool.tensor_tensor(mparts[:, 2], mbias[:], mparts[:, 1], ALU.subtract).then_inc(s_mparts, 1)

        def ffn_tensor(pe, g, t):
            def up_part(i, m):
                for c in range(KC):
                    mm = pe.matmul(ps[:, i % 2, :], sign1[:, c, i * P:(i + 1) * P], m[:, c, :],
                                   start=(m is xT_hi and c == 0), stop=(m is xT_lo and c == KC - 1))
                return mm

            def up(i):
                pe.wait_ge(s_gelu, IC * g + i - 1)
                up_part(i, xT_hi)
                up_part(i, xT_lo).then_inc(s_f1, 1)

            def down(i):
                for m, s in ((h_hi, s_fhi), (h_lo, s_flo)):
                    pe.wait_ge(s, IC * g + i + 1)
                    for b in range(GB):
                        mm = pe.matmul(ps[:, 2 + b // 2, (b % 2) * D:(b % 2 + 1) * D],
                                       m[:, i % 3, b * P:(b + 1) * P], sign2[:, i, :],
                                       start=(i == 0 and m is h_hi and b % 2 == 0),
                                       stop=(i == IC - 1 and m is h_lo), skip_group_check=True)
                mm.then_inc(s_f2, 1)

            pe.wait_ge(s_xhi, KC * t + KC)
            up_part(0, xT_hi)
            up_part(1, xT_hi)
            pe.wait_ge(s_xlo, KC * t + KC)
            up_part(0, xT_lo).then_inc(s_f1, 1)
            up_part(1, xT_lo).then_inc(s_f1, 1)
            for i in range(IC):
                if i + 2 < IC:
                    up(i + 2)
                down(i)

        def ffn_scalar(act, g):
            for i in range(IC):
                act.wait_ge(s_f1, IC * g + i + 1)
                act.wait_ge(s_flo, count(IC * g + i - 1))
                if i == 0:
                    act.wait_ge(s_pl, pool_splits(g) + 1)
                act.activation(hf[:, i % 2, :], ps[:, i % 2, :], ACT.Gelu,
                               bias=b1_sb[:, i:i + 1], scale=alpha1[:, i:i + 1]).then_inc(s_gelu, 1)
                if g_is_later(g) and 1 <= i <= 4:
                    expert_split_scalar(act, g - 1, EARLY + i - 1)

        def ffn_vector(dve, g):
            for i in range(IC):
                n = IC * g + i
                dve.wait_ge(s_gelu, n + 1)
                if g_is_later(g) and i < EARLY:
                    dve.wait_ge(s_m2, n - IC + 1)
                if i >= 3:
                    dve.wait_ge(s_f2, n - 2)
                dve.tensor_copy(h_hi[:, i % 3, :], hf[:, i % 2, :]).then_inc(s_fhi, 1)
                dve.wait_ge(s_fhi, n + 1)
                dve.tensor_tensor(h_lo[:, i % 3, :], hf[:, i % 2, :], h_hi[:, i % 3, :].bitcast(F32),
                                  ALU.subtract).then_inc(s_flo, 1)
            dve.wait_ge(s_f2, IC * (g + 1))
            dve.wait_ge(s_fb2, g + 1)
            y = att
            for n in range(2):
                dve.tensor_tensor(y[:, 2 * n:2 * n + 2, :], ps[:, 2 + n, :].rearrange("p (b d) -> p b d", d=D),
                                  alpha2[:].unsqueeze(1).broadcast_to([P, 2, D]), ALU.mult).then_inc(s_fy, 1)
            for n in range(2):
                dve.wait_ge(s_fy, 2 * g + n + 1)
                dve.tensor_tensor(xr[:, 2 * n:2 * n + 2, :], xr[:, 2 * n:2 * n + 2, :], y[:, 2 * n:2 * n + 2, :],
                                  ALU.add).then_inc(s_x2, 1)

        def b2_pool(pool, g, t):
            pool.wait_ge(s_xn, GB * (t + 1))
            pool.tensor_tensor(xr[:], xr[:], b2_sb[:].unsqueeze(1).broadcast_to([P, GB, D]),
                               ALU.add).then_inc(s_fb2, 1)

        def bo_pool(pool, g, t):
            pool.wait_ge(s_xn, GB * (t + 1))
            pool.tensor_tensor(xr[:], xr[:], bo_sb[:].unsqueeze(1).broadcast_to([P, GB, D]),
                               ALU.add).then_inc(s_x2b, 1)

        def wo_tensor(pe, g):
            v = 2 * g + 1
            for c in range(KC):
                for b in range(GB):
                    if c == 0:
                        pe.wait_ge(s_att, GB * v + b + 1)
                    mm = pe.transpose(ps[:, 6 + c, b * P:(b + 1) * P], att[:, b, c * P:(c + 1) * P], ident[:])
                mm.then_inc(s_wotr, 1)

            def products(b, m, w, c):
                return pe.matmul(ps[:, 4 + b // 2, (b % 2) * D:(b % 2 + 1) * D], m[:, c, b * P:(b + 1) * P],
                                 w[:, WO, c, :], start=(c == 0 and m is xT_hi and w is w_hi and b % 2 == 0),
                                 stop=(c == KC - 1 and m is xT_lo), skip_group_check=True)

            for c in range(KC):
                pe.wait_ge(s_wohi, KC * g + c + 1)
                for b in range(GB):
                    products(b, xT_hi, w_hi, c)
                    products(b, xT_hi, w_lo, c)
            pe.wait_ge(s_wolo, KC * g + KC)
            for b in range(GB):
                for c in range(KC):
                    mm = products(b, xT_lo, w_hi, c)
                mm.then_inc(s_womm, 1)

        def wo_scalar(act, g):
            for c in range(KC):
                act.wait_ge(s_wotr, KC * g + c + 1)
                act.activation(xT_hi[:, c, :], ps[:, 6 + c, :], ACT.Copy).then_inc(s_wohi, 1)

        def wo_vector(dve, g):
            for c in range(KC):
                dve.wait_ge(s_wohi, KC * g + c + 1)
                dve.tensor_tensor(xT_lo[:, c, :], ps[:, 6 + c, :], xT_hi[:, c, :].bitcast(F32),
                                  ALU.subtract).then_inc(s_wolo, 1)
            dve.wait_ge(s_x2b, g + 1)
            for n in range(2):
                dve.wait_ge(s_womm, GB * g + 2 * n + 2)
                dve.tensor_tensor(xr[:, 2 * n:2 * n + 2, :], ps[:, 4 + n, :].rearrange("p (b d) -> p b d", d=D),
                                  xr[:, 2 * n:2 * n + 2, :], ALU.add).then_inc(s_x3, 1)

        def router_tensor(pe, t):
            pe.wait_ge(s_xhi, KC * t + KC)
            pe.wait_ge(s_xlo, KC * t + KC)
            pe.wait_ge(s_wlo, 3)
            for b in range(GB):
                rows = slice(b * P, (b + 1) * P)
                mm = split_products(pe, ps[:, 7, b * NE:(b + 1) * NE],
                                    lambda c: xm_hi[:, c, rows], lambda c: xm_lo[:, c, rows],
                                    lambda c: rw_hi[:, c, :], lambda c: rw_lo[:, c, :], KC)
            mm.then_inc(s_rmm, 1)

        def router_logits_vector(dve):
            dve.wait_ge(s_rmm, 1)
            dve.tensor_tensor(lg[:], ps[:, 7, 0:GB * NE].rearrange("p (b e) -> p b e", e=NE),
                              rb_sb[:].unsqueeze(1).broadcast_to([P, GB, NE]), ALU.add).then_inc(s_rl, 1)
            dve.wait_ge(s_rl, 1)
            dve.tensor_reduce(lmax[:], lg[:], AX.X, ALU.max).then_inc(s_rl, 1)
            dve.wait_ge(s_rl, 2)
            dve.tensor_tensor(lg[:], lg[:], lmax[:].unsqueeze(2).broadcast_to([P, GB, NE]),
                              ALU.subtract).then_inc(s_rl, 1)

        def router_weights_vector(dve):
            dve.wait_ge(s_rex, 1)
            dve.tensor_reduce(lsum[:], route[:], AX.X, ALU.add).then_inc(s_rl, 1)
            dve.wait_ge(s_rl, 4)
            dve.reciprocal(lrec[:], lsum[:]).then_inc(s_rl, 1)
            dve.wait_ge(s_rl, 5)
            dve.tensor_tensor(route[:], route[:], lrec[:].unsqueeze(2).broadcast_to([P, GB, NE]),
                              ALU.mult).then_inc(s_route, 1)

            dve.wait_ge(s_route, 1)
            dve.tensor_scalar(taken[:], route[:], 0.0, None, ALU.is_gt).then_inc(s_taken, 1)

        def router_count_vector(dve):
            dve.wait_ge(s_count, 1)
            dve.tensor_copy(carry[:], ps[:, 1, P:P + NE]).then_inc(s_carry, 1)
            dve.wait_ge(s_carry, 1)
            dve.tensor_reduce(lsum[0:1, 0:1], carry[0:1, :], AX.X, ALU.add).then_inc(s_rl, 1)
            dve.wait_ge(s_rl, 6)
            dve.tensor_copy(filled[:], lsum[0:1, 0:1]).then_inc(s_filled, 1)

        def router_count_tensor(pe):
            pe.wait_ge(s_taken, 1)
            for b in range(GB):
                mm = pe.matmul(ps[:, 1, P:P + NE], ones[:], taken[:, b, :], start=(b == 0), stop=(b == GB - 1),
                               skip_group_check=True)
            mm.then_inc(s_count, 1)

        def router_scalar(act):
            act.wait_ge(s_rl, 3)
            act.activation(route[:], lg[:], ACT.Exp).then_inc(s_rex, 1)

        def expert_sync(sp, e, chunks):
            for i in chunks:
                n = IC * e + i
                r = i % RING
                if i >= RING:
                    sp.wait_ge(s_ewlo, n - RING + 1)
                sp.dma_start(ew_raw[:, r, 0:D].rearrange("p (c n) -> p c n", n=P), e1_c[e, i]).then_inc(s_ew[r], 16)
                sp.dma_start(ew_raw[:, r, D:2 * D], e2_c[e, i]).then_inc(s_ew[r], 16)

        def expert_split_scalar(act, e, i):
            n = IC * e + i
            r = i % RING
            act.wait_ge(s_ew[r], 32 * (2 * e + i // RING + 1))
            if i >= RING:
                act.wait_ge(s_m2, n - RING + 1)
            act.activation(ew_hi[:, r, :], ew_raw[:, r, :], ACT.Copy).then_inc(s_ewhi, 1)

        def expert_pool(pool, e, chunks):
            for i in chunks:
                pool.wait_ge(s_ewhi, IC * e + i + 1)
                pool.tensor_tensor(ew_lo[:, i % RING, :], ew_raw[:, i % RING, :],
                                   ew_hi[:, i % RING, :].bitcast(F32), ALU.subtract).then_inc(s_ewlo, 1)

        def hidden_bank(i):
            return i % 2 + (0 if i < EARLY else 2)

        def expert_up(pe, e, i):
            n = IC * e + i
            r = i % RING
            if i >= 2:
                pe.wait_ge(s_mhlo, n - 1)
            pe.wait_ge(s_ewhi, n + 1)
            pe.wait_ge(s_ewlo, n + 1)
            split_products(pe, ps[:, hidden_bank(i), :],
                           lambda c: ew_hi[:, r, c * P:(c + 1) * P], lambda c: ew_lo[:, r, c * P:(c + 1) * P],
                           lambda c: xm_hi[:, c, :], lambda c: xm_lo[:, c, :], KC).then_inc(s_m1, 1)

        def expert_down(pe, e, i):
            n = IC * e + i
            r = i % RING
            pe.wait_ge(s_mhhi, n + 1)
            for k, (m, w) in enumerate(((h_hi, ew_hi), (h_hi, ew_lo), (h_lo, ew_hi))):
                if k == 2:
                    pe.wait_ge(s_mhlo, n + 1)
                for b in range(GB):
                    mm = pe.matmul(ps[:, 4 + b // 2, (b % 2) * D:(b % 2 + 1) * D],
                                   m[:, i % 3, b * P:(b + 1) * P], w[:, r, D:2 * D],
                                   start=(i == 0 and k == 0 and b % 2 == 0),
                                   stop=(i == IC - 1 and k == 2), skip_group_check=True)
            mm.then_inc(s_m2, 1)

        def expert_relu(act, e, i):
            n = IC * e + i
            act.wait_ge(s_m1, n + 1)
            if i >= 3:
                act.wait_ge(s_m2, n - 2)
            act.activation(h_hi[:, i % 3, :], ps[:, hidden_bank(i), :], ACT.Relu).then_inc(s_mhhi, 1)

        def expert_low(dve, e, i):
            dve.wait_ge(s_mhhi, IC * e + i + 1)
            dve.scalar_tensor_tensor(out=h_lo[:, i % 3, :], in0=ps[:, hidden_bank(i), :], scalar=0.0,
                                     in1=h_hi[:, i % 3, :].bitcast(F32), op0=ALU.max,
                                     op1=ALU.subtract).then_inc(s_mhlo, 1)

        def expert_add(dve, e, column):
            dve.wait_ge(s_m2, IC * (e + 1))
            for b in range(GB):
                dve.scalar_tensor_tensor(out=acc[:, b], in0=ps[:, 4 + b // 2, (b % 2) * D:(b % 2 + 1) * D],
                                         scalar=column(b), in1=acc[:, b], op0=ALU.mult,
                                         op1=ALU.add).then_inc(s_macc, 1)


        GN = B - GB
        RSTEPS, SSTEPS = 6, 4
        tri = xa[:, 0, 0:P]
        gx = xa[:, 1]
        gxT = c_raw[:, :, 0:P]
        gw1 = prob[:].rearrange("p u n -> p (u n)").rearrange("p (c n) -> p c n", c=KC)
        gw2 = ew_raw[:].rearrange("p r n -> p (r n)").rearrange("p (i d) -> p i d", d=D)
        gh = pf[:].rearrange("p c n -> p (c n)")
        grank = lg[:, 1, :]
        gsel = lg[:, 2, :]

        def general(eng, program):
            eng.wait_ge(s_filled, 1)
            n = eng.value_load(filled[0:1, 0:1], min_val=0, max_val=NE * CAPACITY)
            with eng.If(n < NE * CAPACITY):
                program(eng)
                eng.nop()
            with eng.Else():
                eng.nop()

        def tiles(eng, tile):
            tile(0)
            with eng.Fori(1, GN) as k:
                tile(k)

        def experts(eng, k, expert):
            expert(k, 0)
            with eng.Fori(1, NE) as e:
                expert(k, e)

        def general_sync(sp):
            def expert(k, e):
                sp.wait_ge(g_down, NE * k + e)
                sp.dma_start(gw1, e1[e].rearrange("(c p) n -> p c n", p=P)).then_inc(g_w, 16)
                sp.dma_start(gw2, e2[e].rearrange("(i p) d -> p i d", p=P)).then_inc(g_w, 16)

            def tile(k):
                sp.wait_ge(g_st_out, 16 * k)
                sp.dma_start(gx, out[k + GB]).then_inc(g_x, 16)
                experts(sp, k, expert)
                sp.wait_ge(g_acc, NE * k + NE)
                sp.dma_start(out[k + GB], gx).then_inc(g_st_out, 16)

            sp.wait_ge(s_out, 16 * NG)
            sp.wait_ge(s_macc, GB * NE)
            tiles(sp, tile)
            sp.wait_ge(g_st_out, 16 * GN)

        def general_pool(pool):
            def tile(k):
                pool.wait_ge(g_mv, k + 1)
                pool.tensor_tensor(vpe[:, 0:1], mv[:, 0, 1:2], eps[:, 0:1], ALU.add).then_inc(g_vpe, 1)
                pool.wait_ge(g_vpe, k + 1)
                pool.tensor_tensor(rstd[:, 0:1], vpe[:, 0:1], half[:, 0:1], ALU.pow).then_inc(g_rstd, 1)

            pool.memset(tri, 1.0).then_inc(g_tri, 1)
            pool.wait_ge(g_tri, 1)
            pool.affine_select(out=tri, in_=tri, compare_op=ALU.is_gt, fill=0.0, base=0,
                               pattern=[[1, P]], channel_multiplier=-1).then_inc(g_tri, 1)
            tiles(pool, tile)

        def general_vector(dve):
            def expert(k, e):
                dve.wait_ge(g_down, NE * k + e + 1)
                dve.wait_ge(g_sel, SSTEPS * k + 4)
                dve.wait_ge(g_acc, NE * k + e)
                dve.scalar_tensor_tensor(out=gx, in0=ps[:, 2, 0:D], scalar=route[:, 0, bass.ds(e, 1)],
                                         in1=gx, op0=ALU.mult, op1=ALU.add).then_inc(g_acc, 1)

            def tile(k):
                dve.wait_ge(g_x, 16 * k + 16)
                dve.bn_stats(stats[:, 0], gx).then_inc(g_st, 1)
                dve.wait_ge(g_st, k + 1)
                dve.tensor_copy(carrier[:], stats[:, 0, 0:1])
                dve.bn_aggr(mv[:, 0], stats[:, 0]).then_inc(g_mv, 1)
                dve.wait_ge(g_rstd, k + 1)
                dve.tensor_scalar(xn[:, 0], gx, mv[:, 0, 0:1], rstd[:, 0:1],
                                  ALU.subtract, ALU.mult).then_inc(g_xn, 1)
                r, n = lg[:, 0, :], RSTEPS * k
                dve.wait_ge(g_log, k + 1)
                dve.tensor_tensor(r, ps[:, 3, 0:NE], rb_sb[:], ALU.add).then_inc(g_r, 1)
                dve.wait_ge(g_r, n + 1)
                dve.tensor_reduce(lmax[:, 0:1], r, AX.X, ALU.max).then_inc(g_r, 1)
                dve.wait_ge(g_r, n + 2)
                dve.tensor_scalar(r, r, lmax[:, 0:1], None, ALU.subtract).then_inc(g_r, 1)
                dve.wait_ge(g_exp, k + 1)
                dve.tensor_reduce(lsum[:, 0:1], route[:, 0, :], AX.X, ALU.add).then_inc(g_r, 1)
                dve.wait_ge(g_r, n + 4)
                dve.reciprocal(lrec[:, 0:1], lsum[:, 0:1]).then_inc(g_r, 1)
                dve.wait_ge(g_r, n + 5)
                dve.tensor_scalar(route[:, 0, :], route[:, 0, :], lrec[:, 0:1], None, ALU.mult).then_inc(g_r, 1)
                dve.wait_ge(g_r, n + 6)
                dve.tensor_scalar(taken[:, 0, :], route[:, 0, :], 0.0, None, ALU.is_gt).then_inc(g_taken, 1)
                m = SSTEPS * k
                dve.wait_ge(g_cnt, k + 1)
                dve.tensor_tensor(grank, ps[:, 3, NE:2 * NE], carry[:], ALU.add).then_inc(g_sel, 1)
                dve.wait_ge(g_sel, m + 1)
                dve.tensor_scalar(gsel, grank, float(CAPACITY), None, ALU.is_lt).then_inc(g_sel, 1)
                dve.wait_ge(g_sel, m + 2)
                dve.tensor_tensor(route[:, 0, :], route[:, 0, :], gsel, ALU.mult).then_inc(g_sel, 1)
                dve.tensor_tensor(carry[:], ps[:, 3, 2 * NE:3 * NE], carry[:], ALU.add).then_inc(g_sel, 1)
                experts(dve, k, expert)

            tiles(dve, tile)

        def general_scalar(act):
            def expert(k, e):
                act.wait_ge(g_up, NE * k + e + 1)
                act.activation(gh, ps[:, 0:2, :], ACT.Relu).then_inc(g_relu, 1)

            def tile(k):
                act.wait_ge(g_xt, k + 1)
                act.activation(gxT, ps[:, 6, 0:D].rearrange("p (c n) -> p c n", c=KC), ACT.Copy).then_inc(g_xtc, 1)
                act.wait_ge(g_r, RSTEPS * k + 3)
                act.activation(route[:, 0, :], lg[:, 0, :], ACT.Exp).then_inc(g_exp, 1)
                experts(act, k, expert)

            tiles(act, tile)

        def general_tensor(pe):
            def expert(k, e):
                n = NE * k + e
                pe.wait_ge(g_w, 32 * n + 32)
                pe.wait_ge(g_relu, n)
                for i in range(IC):
                    for c in range(KC):
                        mm = pe.matmul(ps[:, i // 4, (i % 4) * P:(i % 4 + 1) * P], gw1[:, c, i * P:(i + 1) * P],
                                       gxT[:, c, :], start=(c == 0), stop=(c == KC - 1))
                mm.then_inc(g_up, 1)
                pe.wait_ge(g_relu, n + 1)
                pe.wait_ge(g_acc, n)
                for i in range(IC):
                    mm = pe.matmul(ps[:, 2, 0:D], gh[:, i * P:(i + 1) * P], gw2[:, i, :],
                                   start=(i == 0), stop=(i == IC - 1))
                mm.then_inc(g_down, 1)

            def tile(k):
                pe.wait_ge(g_xn, k + 1)
                for c in range(KC):
                    mm = pe.transpose(ps[:, 6, c * P:(c + 1) * P], xn[:, 0, c * P:(c + 1) * P], ident[:])
                mm.then_inc(g_xt, 1)
                pe.wait_ge(g_xtc, k + 1)
                pe.wait_ge(g_sel, SSTEPS * k)
                for c in range(KC):
                    mm = pe.matmul(ps[:, 3, 0:NE], gxT[:, c, :], rw_raw[:, c, :], start=(c == 0), stop=(c == KC - 1))
                mm.then_inc(g_log, 1)
                pe.wait_ge(g_taken, k + 1)
                pe.matmul(ps[:, 3, NE:2 * NE], tri, taken[:, 0, :], start=True, stop=True)
                pe.matmul(ps[:, 3, 2 * NE:3 * NE], ones[:], taken[:, 0, :], start=True, stop=True).then_inc(g_cnt, 1)
                experts(pe, k, expert)

            pe.wait_ge(g_tri, 2)
            tiles(pe, tile)

        block = ctx.enter_context(nc.Block())

        @block.sync
        def _(sp):
            for n in range(4):
                sp.dma_start(ew_raw[:, n, :].rearrange("p (c d) -> p c d", d=D),
                             wT[n].rearrange("(c p) d -> p c d", p=P)).then_inc(s_wload[0], 16)
            sp.dma_start(c_raw[:], ctx_g[0]).then_inc(s_ctx, 16)
            sp.dma_start(xa[:], x_g[0]).then_inc(s_x, 16)
            sp.dma_start(bk_sb[:], bk).then_inc(s_small, 16)
            sp.dma_start(bq_sb[:], bq).then_inc(s_small, 16)
            for k in range(2):
                sp.dma_start(bv_sb[:, k, :], bv[k].partition_broadcast(P)).then_inc(s_small, 16)
            sp.dma_start(b1_sb[:], b1).then_inc(s_small, 16)
            sp.dma_start(b2_sb[:], b2.partition_broadcast(P)).then_inc(s_small, 16)
            sp.dma_start(bo_sb[:], bo.partition_broadcast(P)).then_inc(s_small, 16)
            sp.dma_start(rb_sb[:], rb.partition_broadcast(P)).then_inc(s_small, 16)
            sp.dma_start(rw_raw[:], rwT.rearrange("(c p) e -> p c e", p=P)).then_inc(s_small, 16)
            for n in range(3):
                sp.dma_start(prob[:].rearrange("p u n -> p (u n)")[:, n * 2 * D:(n + 1) * 2 * D]
                             .rearrange("p (c d) -> p c d", d=D),
                             wT[4 + n].rearrange("(c p) d -> p c d", p=P)).then_inc(s_wload[1], 16)
            sp.dma_start(mask_raw[:], mask_g[0]).then_inc(s_mask, 16)
            sp.dma_start(pvs[:].rearrange("p u n -> p (u n)").rearrange("p (i d) -> p i d", d=D),
                         w1[0:NI // 2, :].rearrange("(i p) d -> p i d", p=P)).then_inc(s_w1, 16)
            sp.dma_start(acc[:], w1[NI // 2:, :].rearrange("(i p) d -> p i d", p=P)).then_inc(s_w1, 16)
            sp.wait_ge(s_wlo, 1)
            sp.dma_start(ew_raw[:].rearrange("p r (a n) -> p (r a n)", a=1).rearrange("p (c n) -> p c n", c=KC),
                         w1T.rearrange("(c p) n -> p c n", p=P)).then_inc(s_wload[0], 16)

            def store_k(l, g):
                n = pool_splits(g) + 1 if l == 1 else 1 if isinstance(g, int) and g == 0 else pool_splits(g) - 1
                scratch_store(sp, k_scr[l], key_split(l, g), s_pl, n)

            def load_k(l, g, halves=(0, 1)):
                stack_load(sp, ks, k_scr[l], K_PART, s_ks, key_split(l, g), 2 * g + l, halves)

            def load_q(l, g, halves=(0, 1)):
                stack_load(sp, qs, q_scr[l], Q_PART, s_qs, query_split(l, g), 2 * g + l, halves)

            def body(g, last):
                attention_sync(sp, 0, g)
                store_k(1, g)
                load_k(1, g)
                if not last:
                    sp.wait_ge(s_clo, g + 1)
                    sp.dma_start(c_raw[:], ctx_g[g + 1]).then_inc(s_ctx, 16)
                    sp.wait_ge(s_x1, GB * (g + 1))
                    sp.dma_start(xa[:], x_g[g + 1]).then_inc(s_x, 16)
                    sp.wait_ge(s_mcnt, g + 1)
                    sp.wait_ge(s_mparts, g + 1)
                    sp.dma_start(mask_raw[:], mask_g[g + 1]).then_inc(s_mask, 16)
                if g_is_later(g):
                    expert_sync(sp, g - 1, range(RING, IC))
                if not last:
                    store_k(0, g + 1)
                store_q(sp, 1, g)
                load_q(1, g)
                attention_sync(sp, 1, g)
                if not last:
                    for hf_ in range(2):
                        load_k(0, g + 1, (hf_,))
                        load_q(0, g + 1, (hf_,))

            store_k(0, 0)
            load_k(0, 0)
            store_q(sp, 0, 0)
            load_q(0, 0)
            sp.wait_ge(s_whi, 3)
            sp.dma_start(ew_raw[:].rearrange("p r n -> p (r n)").rearrange("p (i d) -> p i d", d=D),
                         w2T.rearrange("(i p) d -> p i d", p=P)).then_inc(s_wload[0], 16)
            body(0, False)
            body(1, False)
            with sp.Fori(2, NG - 1) as g:
                body(g, False)
            body(NG - 1, True)
            expert_sync(sp, NG - 1, range(RING, IC))
            general(sp, general_sync)
            sp.wait_ge(s_macc, GB * NE)
            sp.dma_start(out_g[0], acc[:]).then_inc(s_first, 16)
            sp.wait_ge(s_first, 16)
            sp.wait_ge(s_out, 16 * NG)

        @block.gpsimd
        def _(pool):
            pool.memset(ident[:], 0.0).then_inc(s_const, 1)
            pool.memset(identb[:], 0.0).then_inc(s_const, 1)
            pool.wait_ge(s_const, 2)
            for m in (ident, identb):
                pool.affine_select(out=m[:], in_=m[:], compare_op=ALU.not_equal, fill=1.0, base=0,
                                   pattern=[[-1, P]], channel_multiplier=1).then_inc(s_const, 1)
            pool.memset(ones[:], 1.0).then_inc(s_const, 1)
            pool.memset(half[:], -0.5).then_inc(s_const, 1)
            pool.memset(eps[:], EPS).then_inc(s_const, 1)
            pool.memset(far[:], MASKED).then_inc(s_const, 1)
            pool.memset(v_sb[:, :, :, :, HD:HD + 1], 1.0).then_inc(s_const, 1)
            pool.wait_ge(s_const, CONSTS - 1)
            pool.memset(ks[SR:SR + 2, NH // 2:, :], 1.0).then_inc(s_const, 1)
            pool.wait_ge(s_const, CONSTS)

            ctx_pool(pool, 0)
            ln_pool(pool, ln_index(0, 0))
            rest_pool(pool, 0)
            part2_pool(pool, 0)
            rest_pool(pool, 1)
            part2_pool(pool, 1)
            mask_pool(pool, 0)

            def store(g):
                pool.wait_ge(s_x3, 2 * (g + 1))
                pool.dma_start(out_g[g], xr[:]).then_inc(s_out, 16)

            def body(g, last):
                rest_pool(pool, key_split(1, g))
                part2_pool(pool, key_split(1, g))
                if g_routes(g):
                    ln_pool(pool, ln_index(3, 0))
                x1_pool(pool, g)
                ln_pool(pool, ln_index(1, g))
                b2_pool(pool, g, ln_index(1, g))
                if not last:
                    ctx_pool(pool, g + 1)
                if g_is_later(g):
                    expert_pool(pool, g - 1, range(EARLY, IC - 1))
                ln_pool(pool, ln_index(2, g))
                if not last:
                    rest_pool(pool, key_split(0, g + 1))
                    part2_pool(pool, key_split(0, g + 1))
                if not last:
                    ln_pool(pool, ln_index(0, g + 1))
                bo_pool(pool, g, ln_index(2, g))
                if g_is_later(g):
                    expert_pool(pool, g - 1, range(IC - 1, IC))
                if not last:
                    rest_pool(pool, query_split(0, g + 1))
                    part2_pool(pool, query_split(0, g + 1))
                if not last:
                    mask_pool(pool, g + 1)

            body(0, False)
            pool.wait_ge(s_x3, 2)
            pool.dma_start(acc[:], xr[:]).then_inc(s_out, 16)
            body(1, False)
            store(1)
            with pool.Fori(2, NG - 1) as g:
                body(g, False)
                store(g)
            body(NG - 1, True)
            expert_pool(pool, NG - 1, range(RING))
            store(NG - 1)
            expert_pool(pool, NG - 1, range(RING, IC))
            general(pool, general_pool)

        @block.scalar
        def _(act):
            act.wait_ge(s_wload[0], 64)
            raw_a = ew_raw[:].rearrange("p r (c d) -> p r c d", d=D)
            raw_b = prob[:].rearrange("p u n -> p (u n)")
            act.activation(w_hi[:, 0:4], raw_a, ACT.Copy).then_inc(s_whi, 1)
            ctx_scalar(act, 0)
            act.wait_ge(s_wload[1], 48)
            act.activation(w_hi[:, 4:7].rearrange("p a c d -> p (a c d)"), raw_b[:, 0:6 * D], ACT.Copy).then_inc(s_whi, 1)
            act.wait_ge(s_small, SMALL)
            k_scalar(act, 0, 0)
            part0_scalar(act, 0)
            ln_scalar(act, 0, xT_hi)
            act.wait_ge(s_bq, 1)
            q_scalar(act, 0, 0)
            part0_scalar(act, 1)
            k_scalar(act, 1, 0)
            act.wait_ge(s_wload[0], 80)
            act.activation(sign1[:].rearrange("p c n -> p (c n)"), ew_raw[:].rearrange("p r n -> p (r n)"),
                           ACT.Sign).then_inc(s_whi, 1)
            def ffn_weights():
                act.wait_ge(s_wload[0], 96)
                act.activation(sign2[:].rearrange("p i d -> p (i d)"), ew_raw[:].rearrange("p r n -> p (r n)"),
                               ACT.Sign).then_inc(s_whi, 1)
                act.wait_ge(s_whi, 4)
                act.activation(ew_raw[:], ew_raw[:], ACT.Abs).then_inc(s_abs, 1)
                act.activation(rw_hi[:], rw_raw[:], ACT.Copy).then_inc(s_whi, 1)
                act.wait_ge(s_alpha, 2)

            def table(function):
                act.activation(warm[:], half[:, 0:1], function)

            def body(g, last):
                attention_scalar(act, 0, g)
                if not g_is_later(g):
                    ffn_weights()
                table(ACT.Gelu)
                if g_routes(g):
                    ln_scalar(act, ln_index(3, 0), xm_hi)
                if g_is_later(g):
                    for i in range(EARLY):
                        expert_relu(act, g - 1, i)
                ln_scalar(act, ln_index(1, g), xT_hi)
                if not last:
                    ctx_scalar(act, g + 1)
                ffn_scalar(act, g)
                table(ACT.Exp)
                if last:
                    expert_relu(act, g - 1, 3)
                    expert_relu(act, g - 1, 4)
                if not last:
                    k_scalar(act, 0, g + 1)
                    part0_scalar(act, key_split(0, g + 1))
                if g_routes(g):
                    router_scalar(act)
                ln_scalar(act, ln_index(2, g), xT_hi)
                if g_is_later(g) and not last:
                    act.wait_ge(s_f2, IC * (g + 1))
                    expert_relu(act, g - 1, 3)
                q_scalar(act, 1, g)
                part0_scalar(act, query_split(1, g))
                if g_is_later(g) and not last:
                    expert_relu(act, g - 1, 4)
                if not last:
                    ln_scalar(act, ln_index(0, g + 1), xT_hi)
                if g_is_later(g):
                    expert_relu(act, g - 1, 5)
                if not last:
                    q_scalar(act, 0, g + 1)
                if g_is_later(g):
                    expert_split_scalar(act, g - 1, IC - 1)
                    expert_relu(act, g - 1, 6)
                if not last:
                    part0_scalar(act, query_split(0, g + 1))
                if g_is_later(g):
                    expert_relu(act, g - 1, 7)
                attention_scalar(act, 1, g)
                if not last:
                    k_scalar(act, 1, g + 1)
                else:
                    expert_relu(act, g, 0)
                    expert_relu(act, g, 1)
                wo_scalar(act, g)

            body(0, False)
            body(1, False)
            with act.Fori(2, NG - 1) as g:
                body(g, False)
            body(NG - 1, True)
            for i in range(IC):
                if i >= 2:
                    expert_relu(act, NE - 1, i)
                if 1 <= i <= RING:
                    expert_split_scalar(act, NE - 1, RING + i - 1)
            general(act, general_scalar)

        @block.vector
        def _(dve):
            dve.memset(ks[SR:SR + 2, 0:NH // 2, :], 1.0).then_inc(s_ones, 1)
            raw_a = ew_raw[:].rearrange("p r (c d) -> p r c d", d=D)
            raw_b = prob[:].rearrange("p u n -> p (u n)")
            dve.wait_ge(s_whi, 1)
            dve.tensor_tensor(w_lo[:, 0:4], raw_a, w_hi[:, 0:4].bitcast(F32), ALU.subtract).then_inc(s_wlo, 1)
            dve.wait_ge(s_x, 16)
            ln_stats(dve, xa, 0)
            dve.wait_ge(s_whi, 2)
            dve.tensor_tensor(w_lo[:, 4:7].rearrange("p a c d -> p (a c d)"), raw_b[:, 0:6 * D],
                              w_hi[:, 4:7].rearrange("p a c d -> p (a c d)").bitcast(F32),
                              ALU.subtract).then_inc(s_wlo, 1)
            dve.wait_ge(s_small, SMALL)
            dve.tensor_scalar(bq_sb[:], bq_sb[:], QK_SCALE, None, ALU.mult).then_inc(s_bq, 1)
            ln_norm(dve, xa, 0)
            v_vector(dve, 0, 0, range(0, 2))
            part1_vector(dve, 0, 0)
            v_vector(dve, 0, 0, range(2, GB))
            ln_low(dve, 0, xT_hi, xT_lo)
            mask_vector(dve, 0)
            dve.wait_ge(s_w1, 32)
            dve.tensor_reduce(alpha1[:, 0:IC // 2],
                              pvs[:].rearrange("p u n -> p (u n)").rearrange("p (i d) -> p i d", d=D), AX.X, ALU.add, apply_absolute_value=True)
            dve.tensor_reduce(alpha1[:, IC // 2:IC], acc[:], AX.X, ALU.add,
                              apply_absolute_value=True).then_inc(s_alpha, 1)
            dve.wait_ge(s_alpha, 1)
            dve.tensor_scalar(alpha1[:], alpha1[:], 1.0 / D, None, ALU.mult).then_inc(s_alpha, 1)
            part1_vector(dve, 1, 1)
            mask_flag_vector(dve, 0)

            def body(g, last, column):
                attention_vector(dve, 0, g)
                ln = ln_index(1, g)
                if g_routes(g):
                    ln_low(dve, ln_index(3, 0), xm_hi, xm_lo)
                if g_is_later(g):
                    expert_low(dve, g - 1, 0)
                else:
                    dve.wait_ge(s_whi, 5)
                    dve.tensor_tensor(rw_lo[:], rw_raw[:], rw_hi[:].bitcast(F32), ALU.subtract).then_inc(s_wlo, 1)
                dve.wait_ge(s_x1, GB * (g + 1))
                ln_stats(dve, xr, ln)
                if g_is_later(g):
                    expert_low(dve, g - 1, 1)
                    expert_low(dve, g - 1, 2)
                ln_norm(dve, xr, ln)
                ln_low(dve, ln, xT_hi, xT_lo)
                if not g_is_later(g):
                    dve.wait_ge(s_a2mm, 1)
                    dve.tensor_scalar(alpha2[:], ps[:, 5, 0:D], 1.0 / NI, None, ALU.mult).then_inc(s_alpha, 1)
                    dve.wait_ge(s_alpha, 3)
                ffn_vector(dve, g)
                ln = ln_index(2, g)
                dve.wait_ge(s_x2, 2 * (g + 1))
                ln_stats(dve, xr, ln)
                if not last:
                    v_vector(dve, 0, g + 1, range(0, 2))
                    if g_routes(g):
                        router_logits_vector(dve)
                else:
                    expert_low(dve, g - 1, 3)
                ln_norm(dve, xr, ln)
                if not last:
                    part1_vector(dve, key_split(0, g + 1), pool_splits(g) + 1)
                    v_vector(dve, 0, g + 1, range(2, GB))
                else:
                    expert_low(dve, g - 1, 4)
                ln_low(dve, ln, xT_hi, xT_lo)
                if g_routes(g):
                    router_weights_vector(dve)
                if not last:
                    ln = ln_index(0, g + 1)
                    dve.wait_ge(s_x, 16 * (g + 2))
                    ln_stats(dve, xa, ln)
                if g_is_later(g) and not last:
                    expert_low(dve, g - 1, 3)
                if not last:
                    ln_norm(dve, xa, ln)
                if g_is_later(g) and not last:
                    expert_low(dve, g - 1, 4)
                query_split_vector(dve, g)
                if not last:
                    mask_vector(dve, g + 1)
                    ln_low(dve, ln, xT_hi, xT_lo)
                if g_is_later(g):
                    expert_low(dve, g - 1, 5)
                attention_vector(dve, 1, g, column)
                if not last:
                    mask_flag_vector(dve, g + 1)
                    if g_routes(g):
                        router_count_vector(dve)
                else:
                    expert_low(dve, g, 0)
                    expert_low(dve, g, 1)
                wo_vector(dve, g)

            body(0, False, None)
            body(1, False, lambda b: route[:, b, 0:1])
            with dve.Fori(2, NG - 1) as g:
                body(g, False, lambda b: route[:, b, bass.ds(g - 1, 1)])
            body(NG - 1, True, lambda b: route[:, b, NG - 2:NG - 1])
            for i in range(2, IC):
                expert_low(dve, NE - 1, i)
            expert_add(dve, NG - 1, lambda b: route[:, b, NG - 1:NG])
            general(dve, general_vector)

        @block.tensor
        def _(pe):
            pe.wait_ge(s_const, CONSTS)
            pe.wait_ge(s_wlo, 1)
            kv_tensor(pe, 0, 0)
            ln_tensor(pe, 0)
            pe.wait_ge(s_vev, GB)
            q_tensor(pe, 0, 0, 0)
            pe.wait_ge(s_wlo, 2)
            key_products(pe, 1, 0, 0, 2)
            key_products(pe, 1, 0, 1, 3)
            pe.wait_ge(s_pev, 2 * KC)
            mask_count_tensor(pe, 0)
            pe.wait_ge(s_xlo, KC)
            pe.wait_ge(s_ones, 1)

            def alpha2_tensor():
                pe.wait_ge(s_abs, 1)
                abs_w2 = ew_raw[:].rearrange("p r n -> p (r n)")
                for i in range(IC):
                    mm = pe.matmul(ps[:, 5, 0:D], ones[:], abs_w2[:, i * D:(i + 1) * D],
                                   start=(i == 0), stop=(i == IC - 1))
                mm.then_inc(s_a2mm, 1)
                pe.wait_ge(s_whi, 4)

            def body(g, last):
                attention_tensor(pe, 0, g)
                pe.wait_ge(s_max, 2 * NU * (2 * g + 1))
                pe.wait_ge(s_exp, NU * (2 * g + 1))
                if g_routes(g):
                    transposed_out(pe, 2 * g, GB - 1)
                    pe.wait_ge(s_att, GB * (2 * g + 1))
                    ln_tensor(pe, ln_index(3, 0))
                    pe.wait_ge(s_xhi, KC * ln_index(3, 0) + KC)
                    pe.wait_ge(s_xlo, KC * ln_index(3, 0) + KC)
                    expert_up(pe, g - 1, 0)
                else:
                    if g_is_later(g):
                        expert_up(pe, g - 1, 0)
                    transposed_out(pe, 2 * g, GB - 1)
                if not g_is_later(g):
                    alpha2_tensor()
                if g_is_later(g):
                    expert_up(pe, g - 1, 1)
                    expert_up(pe, g - 1, 2)
                    expert_down(pe, g - 1, 0)
                    expert_down(pe, g - 1, 1)
                pe.wait_ge(s_att, GB * (2 * g + 1))
                ln_tensor(pe, ln_index(1, g))
                if g_is_later(g):
                    expert_down(pe, g - 1, 2)
                    pe.wait_ge(s_mhlo, IC * g - IC + EARLY)
                ffn_tensor(pe, g, ln_index(1, g))
                if g_routes(g):
                    router_tensor(pe, ln_index(3, 0))
                pe.wait_ge(s_gelu, IC * (g + 1))
                if not last:
                    kv_tensor(pe, 0, g + 1)
                    if g_routes(g):
                        pe.wait_ge(s_rl, 1)
                else:
                    pe.wait_ge(s_fy, 2 * (g + 1))
                    expert_up(pe, g - 1, 3)
                    expert_up(pe, g - 1, 4)
                ln_tensor(pe, ln_index(2, g))
                if g_is_later(g) and not last:
                    pe.wait_ge(s_fy, 2 * (g + 1))
                    expert_up(pe, g - 1, 3)
                if not last:
                    pe.wait_ge(s_vev, GB * (2 * g + 3))
                q_tensor(pe, 1, g, ln_index(2, g))
                if g_is_later(g) and not last:
                    expert_up(pe, g - 1, 4)
                if not last:
                    ln_tensor(pe, ln_index(0, g + 1))
                if g_is_later(g):
                    expert_up(pe, g - 1, 5)
                if not last:
                    pe.wait_ge(s_pev, KC * (query_split(1, g) + 1))
                    q_tensor(pe, 0, g + 1, ln_index(0, g + 1))
                attention_tensor(pe, 1, g)
                if not last:
                    pe.wait_ge(s_exp, NU * (2 * g + 2) - 1)
                    key_products(pe, 1, g + 1, 0, 2)
                else:
                    pe.wait_ge(s_max, 2 * NU * (2 * g + 2))
                    expert_up(pe, g, 0)
                transposed_out(pe, 2 * g + 1, GB - 1)
                if not last:
                    key_products(pe, 1, g + 1, 1, 3)
                    pe.wait_ge(s_max, 2 * NU * (2 * g + 2))
                    if g_routes(g):
                        router_count_tensor(pe)
                    mask_count_tensor(pe, g + 1)
                else:
                    expert_up(pe, g, 1)
                pe.wait_ge(s_exp, NU * (2 * g + 2))
                pe.wait_ge(s_att, GB * (2 * g + 2))
                wo_tensor(pe, g)

            body(0, False)
            body(1, False)
            pe.wait_ge(s_carry, 1)
            with pe.Fori(2, NG - 1) as g:
                body(g, False)
            body(NG - 1, True)
            for i in range(IC):
                if i + 2 < IC:
                    expert_up(pe, NE - 1, i + 2)
                if i == 0:
                    pe.wait_ge(s_x3, 2 * NG)
                expert_down(pe, NE - 1, i)
            pe.wait_ge(s_macc, GB * NE)
            general(pe, general_tensor)


SMALL = 16 * 9
CONSTS = 10


def kernel(**inputs):
    import numpy as np
    import concourse.bacc as bacc
    from concourse.bass_utils import run_bass_kernel_spmd

    a = {k: np.asarray(v) for k, v in inputs.items()}
    layers = ("L0_xattn_", "L1_xattn_")

    def by_feature(vectors):
        return np.ascontiguousarray(np.stack(vectors).reshape(len(vectors), -1, P).transpose(2, 0, 1))

    arrays = {
        "x": a["x"],
        "ctxT": np.ascontiguousarray(a["ctx_1024"].reshape(B * P, D).T),
        "mask": a["mask_BxSxS2_ff1"],
        "wT": np.stack([a[l + w].T for l in layers for w in ("Wq", "Wk", "Wv")] + [a["L1_xattn_Wo"].T]),
        "bq": by_feature([a[l + "bq"] for l in layers]),
        "bk": by_feature([a[l + "bk"] for l in layers]),
        "bv": np.stack([a[l + "bv"] for l in layers]),
        "bo": a["L1_xattn_bo"],
        "w1": a["L0_ffn_w1"],
        "w1T": np.ascontiguousarray(a["L0_ffn_w1"].T),
        "b1": by_feature([a["L0_ffn_b1"]])[:, 0],
        "w2T": np.ascontiguousarray(a["L0_ffn_w2"].T),
        "b2": a["L0_ffn_b2"],
        "rwT": np.ascontiguousarray(a["L1_ffn_router_w"].T),
        "rb": a["L1_ffn_router_b"],
        "e1": a["L1_ffn_experts_inter"],
        "e2": a["L1_ffn_experts_out"],
    }
    nc = bacc.Bacc("TRN2", target_bir_lowering=False, num_devices=1)
    args = [nc.dram_tensor(n, v.shape, mybir.dt.from_np(v.dtype), kind="ExternalInput").ap()
            for n, v in arrays.items()]
    out = nc.dram_tensor("out", (B, P, D), F32, kind="ExternalOutput").ap()
    build(nc, *args, out)
    r = run_bass_kernel_spmd(nc, [arrays], core_ids=[0])
    return r.results[0]["out"]
```
